# Optimizing a Trainium2 kernel written in Bass

```python
import numpy as np
import jax
import jax.numpy as jnp

def _softmax(x, axis=-1):
    return jax.nn.softmax(x, axis=axis)

def _gelu(x):
    return jax.nn.gelu(x, approximate=True)

def _silu(x):
    return jax.nn.silu(x)

def _sigmoid(x):
    return jax.nn.sigmoid(x)

def _layernorm(x, axis=-1, eps=1e-05):
    m = jnp.mean(x, axis=axis, keepdims=True)
    v = jnp.var(x, axis=axis, keepdims=True)
    return (x - m) / jnp.sqrt(v + eps)

def _scatter_add(tgt, idx, src, axis=0):
    return tgt.at[idx].add(src)

def _segment_sum(src, seg, n):
    return jax.ops.segment_sum(src, seg, n)
kernel_name = 'mk_decoder_postln_d1_seqx_r4_d88e9d'

def setup_inputs(seed: int=0):
    np.random.seed(seed)
    _w = jnp.asarray

    def _rec_inputs():
        import jax
        import jax.numpy as jnp
        _rk = jax.random.key(seed)
        x = 7.22e-05 + 1 * jax.random.normal(jax.random.fold_in(_rk, 1), (4, 512, 256), jnp.float32)
        _lenS = 512 - jax.random.randint(jax.random.fold_in(_rk, 7), (4,), 0, max(1, 512 // 4) + 1, jnp.int32)
        _lenS2 = 64 - jax.random.randint(jax.random.fold_in(_rk, 8), (4,), 0, max(1, 64 // 4) + 1, jnp.int32)
        _ctx_1024P = jax.random.normal(jax.random.fold_in(_rk, 11), (4, 16, 256), jnp.float32)
        _ctx_1024c = jax.random.dirichlet(jax.random.fold_in(_rk, 511), 0.3 * jnp.ones((16,), jnp.float32), (4, 64))
        _ctx_1024t = jnp.einsum('bsk,bkd->bsd', _ctx_1024c, _ctx_1024P)
        _ctx_1024t = _ctx_1024t * jax.lax.rsqrt(jnp.mean(jnp.square(_ctx_1024t)) + 1e-12) * 0.953939
        ctx_1024 = 4.13588e-05 + 0.999923 * (_ctx_1024t + 0.3 * jax.random.normal(jax.random.fold_in(_rk, 611), (4, 64, 256), jnp.float32))
        return (x, ctx_1024)
    x, ctx_1024 = _rec_inputs()

    def _L0_attn_setup():
        import math
        import jax, jax.numpy as jnp
        import numpy as np
        B, T, D_MODEL = (4, 256, 256)
        N_HEADS = 16
        HEAD_DIM = D_MODEL // N_HEADS
        TOP_K = 64

        def _scatter_last(base, idx, vals):
            d = base.shape[-1]
            k = idx.shape[-1]
            fb = base.reshape(-1, d)
            fi = idx.reshape(-1, k)
            fv = vals.reshape(-1, k)
            rows = jnp.arange(fb.shape[0])[:, None]
            return fb.at[rows, fi].set(fv).reshape(base.shape)

        def _sparsify_last_dim_topk(x, keep_k):
            if keep_k >= x.shape[-1]:
                return x
            _, idx = jax.lax.top_k(jnp.abs(x), keep_k)
            vals = jnp.take_along_axis(x, idx, axis=-1)
            return _scatter_last(jnp.zeros_like(x), idx, vals)

        def _forward(x, wq, wk, wv, wo):
            Bx, Tx, C = x.shape
            k_keep = min(TOP_K, Tx)
            feature_keep = min(HEAD_DIM, max(1, math.ceil(HEAD_DIM * (k_keep / Tx))))

            def proj(w):
                y = jnp.einsum('btc,dc->btd', x, w)
                return y.reshape(Bx, Tx, N_HEADS, HEAD_DIM).transpose(0, 2, 1, 3)
            q = _sparsify_last_dim_topk(proj(wq), feature_keep)
            k = _sparsify_last_dim_topk(proj(wk), feature_keep)
            v = _sparsify_last_dim_topk(proj(wv), feature_keep)
            scores = jnp.einsum('bhqd,bhkd->bhqk', q, k) / math.sqrt(HEAD_DIM)
            causal = jnp.triu(jnp.ones((Tx, Tx), dtype=bool), k=1)
            neg_inf = jnp.float32(-jnp.inf)
            scores = jnp.where(causal[None, None], neg_inf, scores)
            topk_vals, topk_idx = jax.lax.top_k(scores, k_keep)
            sparse_scores = _scatter_last(jnp.full_like(scores, neg_inf), topk_idx, topk_vals)
            attn = jax.nn.softmax(sparse_scores, axis=-1)
            out = jnp.einsum('bhqk,bhkd->bhqd', attn, v)
            out = out.transpose(0, 2, 1, 3).reshape(Bx, Tx, C)
            return jnp.einsum('btc,dc->btd', out, wo)
        key = jax.random.key(seed)
        kx, kq, kk, kv, ko = jax.random.split(key, 5)
        scale = 0.02
        x = jax.random.normal(kx, (B, T, D_MODEL), dtype=jnp.float32)
        wq = jax.random.normal(kq, (D_MODEL, D_MODEL), dtype=jnp.float32) * scale
        wk = jax.random.normal(kk, (D_MODEL, D_MODEL), dtype=jnp.float32) * scale
        wv = jax.random.normal(kv, (D_MODEL, D_MODEL), dtype=jnp.float32) * scale
        wo = jax.random.normal(ko, (D_MODEL, D_MODEL), dtype=jnp.float32) * scale
        return {'x': x, 'wq': wq, 'wk': wk, 'wv': wv, 'wo': wo}
    _L0_attn_all = _L0_attn_setup()
    _L0_attn_in = {k: v for k, v in _L0_attn_all.items() if k in ('wq', 'wk', 'wv', 'wo')}
    del _L0_attn_all

    def _L0_xattn_setup():
        import jax, jax.numpy as jnp
        import numpy as np
        D_MODEL = 256
        NUM_HEADS = 16
        DEPTH = D_MODEL // NUM_HEADS

        def _split_heads(x, B):
            return x.reshape(B, -1, NUM_HEADS, DEPTH).transpose(0, 2, 1, 3)
        key = jax.random.key(seed)
        ks = jax.random.split(key, 10)
        B, LQ, LK = (4, 512, 512)
        bound = float(np.sqrt(6.0 / (D_MODEL + D_MODEL)))

        def w(k):
            return jax.random.uniform(k, (D_MODEL, D_MODEL), jnp.float32, -bound, bound)
        return {'query': jax.random.normal(ks[0], (B, LQ, D_MODEL), jnp.float32), 'value': jax.random.normal(ks[1], (B, LK, D_MODEL), jnp.float32), 'wq': w(ks[2]), 'bq': jnp.zeros((D_MODEL,), jnp.float32), 'wk': w(ks[3]), 'bk': jnp.zeros((D_MODEL,), jnp.float32), 'wv': w(ks[4]), 'bv': jnp.zeros((D_MODEL,), jnp.float32), 'wo': w(ks[5]), 'bo': jnp.zeros((D_MODEL,), jnp.float32)}
    _L0_xattn_all = _L0_xattn_setup()
    _L0_xattn_in = {k: v for k, v in _L0_xattn_all.items() if k in ('wq', 'bq', 'wk', 'bk', 'wv', 'bv', 'wo', 'bo')}
    del _L0_xattn_all

    def _L0_ffn_setup():
        import jax, jax.numpy as jnp
        import numpy as np
        B, S, D, E, H, K = (4, 512, 256, 8, 256, 2)
        CAPACITY_FACTOR = 1.25
        MIN_CAPACITY = 4
        key = jax.random.key(seed)
        ks = jax.random.split(key, 5)
        return {'inputs': jax.random.normal(ks[0], (B, S, D), jnp.float32), 'router_w': jax.random.normal(ks[1], (D, E), jnp.float32) / np.sqrt(D), 'router_b': jnp.zeros((E,), jnp.float32), 'w1': jax.random.normal(ks[2], (E, D, H), jnp.float32) / np.sqrt(D), 'b1': jnp.zeros((E, H), jnp.float32), 'w2': jax.random.normal(ks[3], (E, H, D), jnp.float32) / np.sqrt(H), 'b2': jnp.zeros((E, D), jnp.float32)}
    _L0_ffn_all = _L0_ffn_setup()
    _L0_ffn_in = {k: v for k, v in _L0_ffn_all.items() if k in ('router_w', 'router_b', 'w1', 'b1', 'w2', 'b2')}
    del _L0_ffn_all
    return {'x': x, 'ctx_1024': ctx_1024, 'L0_attn_wq': _L0_attn_in['wq'], 'L0_attn_wk': _L0_attn_in['wk'], 'L0_attn_wv': _L0_attn_in['wv'], 'L0_attn_wo': _L0_attn_in['wo'], 'L0_xattn_wq': _L0_xattn_in['wq'], 'L0_xattn_bq': _L0_xattn_in['bq'], 'L0_xattn_wk': _L0_xattn_in['wk'], 'L0_xattn_bk': _L0_xattn_in['bk'], 'L0_xattn_wv': _L0_xattn_in['wv'], 'L0_xattn_bv': _L0_xattn_in['bv'], 'L0_xattn_wo': _L0_xattn_in['wo'], 'L0_xattn_bo': _L0_xattn_in['bo'], 'L0_ffn_router_w': _L0_ffn_in['router_w'], 'L0_ffn_router_b': _L0_ffn_in['router_b'], 'L0_ffn_w1': _L0_ffn_in['w1'], 'L0_ffn_b1': _L0_ffn_in['b1'], 'L0_ffn_w2': _L0_ffn_in['w2'], 'L0_ffn_b2': _L0_ffn_in['b2']}

def reference(x, ctx_1024, L0_attn_wq, L0_attn_wk, L0_attn_wv, L0_attn_wo, L0_xattn_wq, L0_xattn_bq, L0_xattn_wk, L0_xattn_bk, L0_xattn_wv, L0_xattn_bv, L0_xattn_wo, L0_xattn_bo, L0_ffn_router_w, L0_ffn_router_b, L0_ffn_w1, L0_ffn_b1, L0_ffn_w2, L0_ffn_b2):
    import jax
    import jax.numpy as jnp

    def _L0_attn_ref(x, wq, wk, wv, wo):
        import math
        import jax, jax.numpy as jnp
        import numpy as np
        B, T, D_MODEL = (4, 256, 256)
        N_HEADS = 16
        HEAD_DIM = D_MODEL // N_HEADS
        TOP_K = 64

        def _scatter_last(base, idx, vals):
            d = base.shape[-1]
            k = idx.shape[-1]
            fb = base.reshape(-1, d)
            fi = idx.reshape(-1, k)
            fv = vals.reshape(-1, k)
            rows = jnp.arange(fb.shape[0])[:, None]
            return fb.at[rows, fi].set(fv).reshape(base.shape)

        def _sparsify_last_dim_topk(x, keep_k):
            if keep_k >= x.shape[-1]:
                return x
            _, idx = jax.lax.top_k(jnp.abs(x), keep_k)
            vals = jnp.take_along_axis(x, idx, axis=-1)
            return _scatter_last(jnp.zeros_like(x), idx, vals)

        def _forward(x, wq, wk, wv, wo):
            Bx, Tx, C = x.shape
            k_keep = min(TOP_K, Tx)
            feature_keep = min(HEAD_DIM, max(1, math.ceil(HEAD_DIM * (k_keep / Tx))))

            def proj(w):
                y = jnp.einsum('btc,dc->btd', x, w)
                return y.reshape(Bx, Tx, N_HEADS, HEAD_DIM).transpose(0, 2, 1, 3)
            q = _sparsify_last_dim_topk(proj(wq), feature_keep)
            k = _sparsify_last_dim_topk(proj(wk), feature_keep)
            v = _sparsify_last_dim_topk(proj(wv), feature_keep)
            scores = jnp.einsum('bhqd,bhkd->bhqk', q, k) / math.sqrt(HEAD_DIM)
            causal = jnp.triu(jnp.ones((Tx, Tx), dtype=bool), k=1)
            neg_inf = jnp.float32(-jnp.inf)
            scores = jnp.where(causal[None, None], neg_inf, scores)
            topk_vals, topk_idx = jax.lax.top_k(scores, k_keep)
            sparse_scores = _scatter_last(jnp.full_like(scores, neg_inf), topk_idx, topk_vals)
            attn = jax.nn.softmax(sparse_scores, axis=-1)
            out = jnp.einsum('bhqk,bhkd->bhqd', attn, v)
            out = out.transpose(0, 2, 1, 3).reshape(Bx, Tx, C)
            return jnp.einsum('btc,dc->btd', out, wo)
        return _forward(x, wq, wk, wv, wo)

    def _L0_xattn_ref(query, value, wq, bq, wk, bk, wv, bv, wo, bo):
        import jax, jax.numpy as jnp
        import numpy as np
        D_MODEL = 256
        NUM_HEADS = 16
        DEPTH = D_MODEL // NUM_HEADS

        def _split_heads(x, B):
            return x.reshape(B, -1, NUM_HEADS, DEPTH).transpose(0, 2, 1, 3)
        B = query.shape[0]
        q = _split_heads(query @ wq.T + bq, B)
        k = _split_heads(value @ wk.T + bk, B)
        v = _split_heads(value @ wv.T + bv, B)
        scale = jnp.sqrt(jnp.asarray(DEPTH, dtype=q.dtype))
        scores = jnp.einsum('bhqd,bhkd->bhqk', q, k) / scale
        attn = jax.nn.softmax(scores, axis=-1)
        ctx = jnp.einsum('bhqk,bhkd->bhqd', attn, v)
        ctx = ctx.transpose(0, 2, 1, 3).reshape(B, -1, D_MODEL)
        return ctx @ wo.T + bo

    def _L0_ffn_ref(inputs, router_w, router_b, w1, b1, w2, b2):
        import jax, jax.numpy as jnp
        import numpy as np
        B, S, D, E, H, K = (4, 512, 256, 8, 256, 2)
        CAPACITY_FACTOR = 1.25
        MIN_CAPACITY = 4
        b, s, d = inputs.shape
        n = b * s
        flat = inputs.reshape(n, d)
        logits = flat @ router_w + router_b
        probs = jax.nn.softmax(logits, axis=-1)
        top_p, top_i = jax.lax.top_k(probs, K)
        top_p = top_p / jnp.sum(top_p, axis=-1, keepdims=True)
        expert_capacity = max(int(n * CAPACITY_FACTOR / E), MIN_CAPACITY)
        rows = jnp.arange(n)[:, None]
        mask = jnp.zeros((n, E), inputs.dtype).at[rows, top_i].set(top_p)
        mask = mask.at[top_i, jnp.arange(K)[None, :]].add(top_p)
        mask = jnp.minimum(mask, expert_capacity)
        xin = mask[:, :, None] * flat[:, None, :]
        h = jax.nn.gelu(jnp.einsum('ned,edh->neh', xin, w1) + b1, approximate=False)
        out = jnp.einsum('neh,ehd->ned', h, w2) + b2
        final = jnp.einsum('ne,ned->nd', mask, out)
        return final.reshape(b, s, d)
    x = _layernorm(x + _L0_attn_ref(x, L0_attn_wq, L0_attn_wk, L0_attn_wv, L0_attn_wo), axis=-1)
    x = _layernorm(x + _L0_xattn_ref(x, ctx_1024, L0_xattn_wq, L0_xattn_bq, L0_xattn_wk, L0_xattn_bk, L0_xattn_wv, L0_xattn_bv, L0_xattn_wo, L0_xattn_bo), axis=-1)
    x = _layernorm(x + _L0_ffn_ref(x, L0_ffn_router_w, L0_ffn_router_b, L0_ffn_w1, L0_ffn_b1, L0_ffn_w2, L0_ffn_b2), axis=-1)
    return x

_drawn_inputs = setup_inputs


def setup_inputs(seed=0):
    import zlib

    import numpy as np

    out = dict(_drawn_inputs(seed))
    spreads = {'L0_xattn_bq': (0.0, 0.1),
     'L0_xattn_bk': (0.0, 0.8),
     'L0_xattn_bv': (0.0, 0.1),
     'L0_xattn_bo': (0.0, 0.1),
     'L0_ffn_router_b': (0.0, 0.1),
     'L0_ffn_b1': (0.0, 0.1),
     'L0_ffn_b2': (0.0, 0.1)}
    factors = {'L0_attn_wq': 5.562, 'L0_attn_wk': 5.003, 'L0_attn_wv': 3.885, 'L0_attn_wo': 3.757}
    for name, (base, spread) in spreads.items():
        noise = np.random.default_rng([zlib.crc32(name.encode()), seed]).standard_normal(out[name].shape)
        drawn = base * np.exp(spread * noise) if base else spread * noise
        out[name] = jnp.asarray(drawn.astype(out[name].dtype))
    for name, factor in factors.items():
        out[name] = (out[name] * factor).astype(out[name].dtype)
    return out
```

```python
from contextlib import ExitStack

import concourse.bass as bass
from concourse import mybir
from concourse.alu_op_type import AluOpType as ALU
import numpy as np

F32 = mybir.dt.float32
BF16 = mybir.dt.bfloat16
ACT = mybir.ActivationFunctionType
X = mybir.AxisListType.X


def ds(start, size):
    return bass.ds(val(start), size)

P = 128
B, T, D = 4, 512, 256
NH, HD = 16, 16
NC = D // P
QT = T // P
TILES = B * QT
KEEP = 64
ROUNDS = KEEP // 8
CTX = 64
NE, FH = 8, 256
CAPACITY = float(max(int(B * T * 1.25 / NE), 4))
EPS = 1e-5
NEG = -1.0e30
GONE = -3.0e38
SLOTS = NH // 2
VW = HD + 1
SPARSE = 14
ROUTE = 14
LN = 4


class Linear:
    def __init__(self, reg, times=1, plus=0):
        self.reg, self.times, self.plus = reg, times, plus

    def __add__(self, n):
        return Linear(self.reg, self.times, self.plus + n)

    def __sub__(self, n):
        return self + -n

    def __mul__(self, n):
        return Linear(self.reg, self.times * n, self.plus * n)

    __radd__, __rmul__ = __add__, __mul__


def val(n):
    if not isinstance(n, Linear):
        return n
    scaled = n.reg * n.times if n.times != 1 else n.reg
    return scaled + n.plus if n.plus else scaled


def wait(eng, sem, value):
    if isinstance(value, Linear) or value > 0:
        eng.wait_ge(sem, val(value))


def build(nc, a):
    nc.disable_value_cache = True
    with ExitStack() as ctx:
        def sb(name, shape, dt=F32):
            return ctx.enter_context(nc.sbuf_tensor(name, shape, dt))

        def sem(name):
            return ctx.enter_context(nc.semaphore(name))

        w_o = sb("w_o", [P, NC, D])
        w_q2 = sb("w_q2", [P, NC, D])
        w_k2 = sb("w_k2", [P, NC, D])
        w_v2 = sb("w_v2", [P, NC, D])
        w_o2 = sb("w_o2", [P, NC, D])
        w_r = sb("w_r", [P, NC, NE])
        w_1 = sb("w_1", [P, NE, NC, FH])
        w_2 = sb("w_2", [P, NE, NC, D])
        b_q = sb("b_q", [P, NC])
        b_q4 = sb("b_q4", [P, NC])
        b_k = sb("b_k", [P, NC])
        b_v = sb("b_v", [1, D])
        b_o = sb("b_o", [P, D])
        b_r = sb("b_r", [P, NE])
        b_1 = sb("b_1", [P, NE, NC])
        b_2 = sb("b_2", [NE, D])
        x_rows = [sb(f"x_rows{k}", [P, D]) for k in range(2)]
        ident = sb("ident", [P, P])
        ident_h = sb("ident_h", [P, P], BF16)
        causal_h = sb("causal_h", [P, P], BF16)
        head_rows = sb("head_rows", [P, 8, P])
        first_wt = sb("first_wt", [P, HD], BF16)
        earlier = sb("earlier", [P, NE, NE])
        pick_row = sb("pick_row", [NE, NE, P])
        ones = sb("ones", [P, P])
        eps = sb("eps", [P, 1])
        half = sb("half", [P, 1])

        q_t = sb("q_t", [P, NC, B * T])
        k_t = sb("k_t", [P, NC, B * T])
        v_s = sb("v_s", [P, TILES, NH, VW])

        k2_bd = sb("k2_bd", [P, B, NC, 8, CTX])
        v2_bd = sb("v2_bd", [P, B, 8, 2 * VW])

        q_h = [sb(f"q_h{k}", [P, P]) for k in range(4)]
        S_all = sb("S_all", [P, 4, T])
        S = [S_all[:, k, :] for k in range(4)]
        left = [sb(f"left{k}", [P, T]) for k in range(4)]
        eight = [sb(f"eight{k}", [P, 8]) for k in range(4)]
        eight0 = [sb(f"eight0{k}", [P, 8]) for k in range(4)]
        neg_m48 = sb("grp_f", [P, 3 * NH])
        neg_h48 = sb("grp_h", [P, 3 * NH], BF16)
        neg_m = [sb(f"neg_m{k}", [P, 1]) for k in range(4)]
        e_all = [sb(f"e_all{k}", [P, T]) for k in range(2)]
        e_left = [sb(f"e_left{k}", [P, T]) for k in range(2)]
        prob = [sb(f"prob{k}", [P, T]) for k in range(2)]
        prob_t = [sb(f"prob_t{k}", [P, QT, P]) for k in range(2)]

        den = sb("den", [P, NH])
        heads_o = sb("heads_o", [P, D])
        heads_t = sb("heads_t", [P, NC, P])
        res = sb("res", [P, D])
        stats = sb("stats", [P, 6])
        mv = sb("mv", [P, 2])
        var_e = sb("var_e", [P, 1])
        rstd = sb("rstd", [P, 1])
        x_all = sb("x_all", [P, 3, D])
        x1, x1b, x2 = (x_all[:, j, :] for j in range(3))
        x1_t = sb("x1_t", [P, NC, P])
        q2_t = sb("q2_t", [P, NC, P])
        m2 = sb("m2", [P, NH])
        p2 = sb("p2", [P, NH * CTX])
        p2_t = sb("p2_t", [P, NH * CTX])
        x2_0 = sb("x2_0", [P, D])
        x2_t = sb("x2_t", [P, NC, P])
        x2_t0 = sb("x2_t0", [P, NC, P])
        logit = sb("logit", [P, NE])
        l_max = sb("l_max", [P, 1])
        l_exp = sb("l_exp", [P, NE])
        above = sb("above", [P, NE, NE])
        tied = sb("tied", [P, NE, NE])
        rank = sb("rank", [P, NE])
        chosen = sb("chosen", [P, 2, NE])
        both = sb("both", [P, NE])
        l_sum = sb("l_sum", [P, 1])
        l_rec = sb("l_rec", [P, 1])
        gate = sb("gate", [P, NE])
        gate_0 = sb("gate_0", [P, NE])
        gates = sb("gates", [P, TILES, 2 * NE])
        gates_sum = sb("gates_sum", [P, 2, NE])
        gate_t = sb("gate_t", [NE, P])
        gate_b = sb("gate_b", [P, NE, P])
        x_in = sb("x_in", [P, 4, NC, P])
        hid_all = sb("hid_all", [P, 4, NC, P])
        hid = [hid_all[:, k, :, :] for k in range(2)]
        hid_g = [hid_all[:, 2 + k, :, :] for k in range(2)]
        fin = sb("fin", [P, D])

        w_qkv = S_all[:, :, :].rearrange("p k n -> p (k n)")[:, 0:NC * 3 * D].rearrange("p (c n) -> p c n", c=NC)
        flat_in = x_in[:, :, :, :].rearrange("p e c n -> p (e c n)")
        raw = [flat_in[:, 0:3 * D], x_all[:, :, :].rearrange("p k n -> p (k n)")]
        flat_hid = hid_all[:, :, :, :].rearrange("p e c n -> p (e c n)").rearrange("p (j c n) -> p j c n", j=2, c=NC)
        ctx_t, k2_t = flat_hid[:, 0, :, :], flat_hid[:, 1, :, :]
        mag = [p2[:, 0:3 * D], p2_t[:, 0:3 * D]]
        hit, hit_w, top1, top2 = (t[:, :].bitcast(BF16)[:, 0:3 * D] for t in (*e_all, *e_left))
        qk_s = [prob[k][:, :] for k in range(2)]
        x_t = [prob_t[k][:, 0:NC, :] for k in range(2)]
        grp_f = neg_m48
        grp_h = neg_h48
        ctx_t2 = gate_b[:, :, :].rearrange("p e n -> p (e n)").rearrange("p (c b n) -> p c b n", c=NC, b=B)

        psC = ctx.enter_context(nc.psum_tensor("psC", [P, 1024], F32))
        psS = ctx.enter_context(nc.psum_tensor("psS", [P, 1024], F32))
        psP = ctx.enter_context(nc.psum_tensor("psP", [P, 1024], F32))
        psO = ctx.enter_context(nc.psum_tensor("psO", [P, 512], F32))
        psB = ctx.enter_context(nc.psum_tensor("psB", [P, 512], F32))
        turn = psB[:, 0:D].rearrange("p (c n) -> p c n", c=NC)
        y_ps = psB[:, D:2 * D]
        qkv_ps = [psC, psS]

        ld_proj = sem("ld_proj")
        ld_const = sem("ld_const")
        ld_rest = sem("ld_rest")
        ld_exp = sem("ld_exp")
        ld_xt = [sem(f"ld_xt{k}") for k in range(2)]
        ld_xr = [sem(f"ld_xr{k}") for k in range(2)]
        a_proj = sem("a_proj")
        a_raw = sem("a_raw")
        a_dve = sem("a_dve")
        a_turn = sem("a_turn")
        a_kept = sem("a_kept")
        init = sem("init")
        carried = sem("carried")
        c_k2 = sem("c_k2")
        c_k2t = sem("c_k2t")
        c_bd = sem("c_bd")
        c_v2 = sem("c_v2")
        c_v2c = sem("c_v2c")
        qh_ready = sem("qh_ready")
        s_made = sem("s_made")
        s_ready = sem("s_ready")
        top_step = sem("top_step")
        top_done = sem("top_done")
        exp_done = sem("exp_done")
        prob_ready = sem("prob_ready")
        prob_turned = sem("prob_turned")
        probt_ready = sem("probt_ready")
        pv_done = sem("pv_done")
        g0 = sem("g0_heads")
        g1_turn, g1_t, g1_y, g1_ln = sem("g1_turn"), sem("g1_t"), sem("g1_y"), sem("g1_ln")
        rs1, x1b_ready = sem("rs1"), sem("x1b_ready")
        g2_turn, g2_t, g2_q, g2_qt, g2_s, g2_dve = (sem(n) for n in (
            "g2_turn", "g2_t", "g2_q", "g2_qt", "g2_s", "g2_dve"))
        g3_exp, g3_turn, g3_t, g3_o, g3_dve = (sem(n) for n in (
            "g3_exp", "g3_turn", "g3_t", "g3_o", "g3_dve"))
        g4_turn, g4_t, g4_y, g4_ln, rs4 = (sem(n) for n in ("g4_turn", "g4_t", "g4_y", "g4_ln", "rs4"))
        g5_turn, g5_t, g5_l, g5_dve, g5_exp = (sem(n) for n in (
            "g5_turn", "g5_t", "g5_l", "g5_dve", "g5_exp"))
        f_turn, f_t, f_b, f_bc, f_xin, f_h, f_gelu, f_hg, f_y, f_ln, rs7 = (sem(n) for n in (
            "f_turn", "f_t", "f_b", "f_bc", "f_xin", "f_h", "f_gelu", "f_hg", "f_y", "f_ln", "rs7"))
        z_sum, z_ps, z_gate = sem("z_sum"), sem("z_ps"), sem("z_gate")
        out_done = sem("out_done")

        block = ctx.enter_context(nc.Block())

        def link(eng, signal, base):
            n = [0]

            def step(ins):
                n[0] += 1
                ins.then_inc(signal, 1)
                return n[0]

            def caught_up():
                wait(eng, signal, base + n[0])
            step.caught_up = caught_up
            step.n = n
            return step

        def qtile(b, qt):
            return b * T + qt * P

        def timeline(eng, slot, segment, final):
            def tile(b, qt, prev):
                for p in range(SLOTS):
                    slot(b, qt, p, prev)

            for qt in range(QT):
                tile(0, qt, None if qt == 0 else (0, qt - 1))
            with eng.Fori(1, B) as b:
                b = Linear(b)
                for qt in range(QT):
                    tile(b, qt, (b - 1, QT - 1) if qt == 0 else (b, qt - 1))
            final()

        @block.sync
        def _(sp):
            def load_xt(t, k):
                sp.dma_start(x_t[k][:, :, :], a["x_t"].rearrange("(c p) n -> p c n", p=P)[:, :, ds(t * P, P)]
                             ).then_inc(ld_xt[k], 16)

            load_xt(0, 0)
            sp.dma_start(w_qkv[:, :, :], a["w_qkv"].rearrange("(c p) n -> p c n", p=P)).then_inc(ld_proj, 16)
            load_xt(1, 1)
            for dst, src in ((ident, "ident"), (ident_h, "ident_h"), (causal_h, "causal_h"), (first_wt, "first_wt"),
                             (half, "half"), (eps, "eps")):
                sp.dma_start(dst[:, :], a[src]).then_inc(ld_const, 16)
            for dst, src in ((head_rows, "head_rows"), (earlier, "earlier"), (pick_row, "pick_row")):
                sp.dma_start(dst[:, :, :], a[src]).then_inc(ld_const, 16)
            sp.dma_start(ones[:, :], a["ones"]).then_inc(ld_const, 16)
            with sp.Fori(0, TILES // 2 - 1) as i:
                i = Linear(i)
                for k in range(2):
                    sp.wait_ge(a_proj, val(2 * i + (k + 1)))
                    load_xt(2 * i + (k + 2), k)

            x_tiles = a["x"].rearrange("(t p) n -> p t n", p=P)
            out_tiles = a["out"].rearrange("(t p) n -> p t n", p=P)

            def load_rows(c, k):
                wait(sp, g1_ln, LN * (c - 2) + 1)
                sp.dma_start(x_rows[k][:, :].unsqueeze(1), x_tiles[:, ds(c, 1), :]).then_inc(ld_xr[k], 16)

            def store(c, f):
                sp.wait_ge(f_ln, val(LN * (f + 1)))
                sp.dma_start(out_tiles[:, ds(c, 1), :], fin[:, :].unsqueeze(1)).then_inc(out_done, 16)

            for c in range(QT):
                load_rows(c, c % 2)
                if c >= 3:
                    store(c - 2, c - 3)
            with sp.Fori(1, B) as b:
                b = Linear(b)
                for qt in range(QT):
                    load_rows(QT * b + qt, qt % 2)
                    store(QT * b + (qt - 2), QT * b + (qt - 3))
            store(TILES - 2, TILES - 3)
            store(TILES - 1, TILES - 2)
            store(0, TILES - 1)
            sp.wait_ge(out_done, val(16 * TILES))

        N_CONST, N_REST = 10, 16

        @block.gpsimd
        def _(pool):
            pool.wait_ge(ld_const, val(16 * N_CONST))
            pool.wait_ge(c_k2t, val(NC))
            for b in range(B):
                for g in range(NC):
                    nc.gpsimd.tensor_tensor(
                        k2_bd[:, b, g, :, :],
                        k2_t[:, g, b * CTX:(b + 1) * CTX].unsqueeze(1).to_broadcast([P, 8, CTX]),
                        head_rows[:, :, 0:CTX], ALU.mult).then_inc(c_bd, 1)
            pool.wait_ge(a_kept, val(2 * TILES))

            def heads_of(b, qt, p):
                s = 8 * (QT * b + qt) + p
                for k in range(2):
                    h, n = 2 * p + k, 2 * s + k
                    wait(pool, s_made, n - 3)
                    nc.gpsimd.tensor_tensor(q_h[h % 4][:, :], q_t[:, h // 8, ds(qtile(b, qt), P)],
                                            head_rows[:, h % 8, :], ALU.mult).then_inc(qh_ready, 1)

            def subtract(b, qt, p):
                W = (qt + 1) * P
                s = 8 * (QT * b + qt) + p
                for k in range(2):
                    n = 2 * s + k
                    pool.wait_ge(exp_done, val(2 * n + 2))
                    wait(pool, prob_turned, n - 1)
                    nc.gpsimd.tensor_tensor(prob[k][:, 0:W], e_all[k][:, 0:W], e_left[k][:, 0:W],
                                            ALU.subtract).then_inc(prob_ready, 1)

            def root(stat, signal, count):
                pool.wait_ge(stat, val(count))
                nc.gpsimd.tensor_tensor(var_e[:, :], mv[:, 1:2], eps[:, :], ALU.add).then_inc(signal, 1)

            def root2(signal, c):
                pool.wait_ge(signal, val(2 * c + 1))
                nc.gpsimd.tensor_tensor(rstd[:, :], var_e[:, :], half[:, :], ALU.pow).then_inc(signal, 1)

            def expert_in(f, e, xt):
                wait(pool, f_h, NE * f + e - 3)
                nc.gpsimd.tensor_tensor(x_in[:, e % 4, :, :], xt[:, :, :],
                                        gate_b[:, e, :].unsqueeze(1).to_broadcast([P, NC, P]),
                                        ALU.mult).then_inc(f_xin, 1)

            def ffn_in(f, xt):
                pool.wait_ge(f_bc, val(f + 1))
                for e in range(4):
                    expert_in(f, e, xt)

            def ffn_gate(f, xt):
                for e in range(NE):
                    if e < NE - 4:
                        expert_in(f, e + 4, xt)
                    pool.wait_ge(f_gelu, val(2 * (NE * f + e) + 2))
                    wait(pool, f_y, NE * f + e - 1)
                    nc.gpsimd.tensor_tensor(hid_g[e % 2][:, :, :], hid[e % 2][:, :, :],
                                            gate_b[:, e, :].unsqueeze(1).to_broadcast([P, NC, P]),
                                            ALU.mult).then_inc(f_hg, 1)

            def last_root(f):
                root(f_ln, rs7, LN * f + 3)
                root2(rs7, f)

            def segment(i, c, first=False):
                if i == 1:
                    root(g1_ln, rs1, LN * c + 3)
                    root2(rs1, c)
                    pool.wait_ge(g1_ln, val(LN * c + 4))
                    nc.gpsimd.tensor_tensor(x1b[:, :], x1[:, :], b_o[:, :], ALU.add).then_inc(x1b_ready, 1)
                if i == 4:
                    root(g4_ln, rs4, LN * c + 3)
                    root2(rs4, c)
                if i == 6 and not first:
                    ffn_in(c - 1, x2_t)
                if i == 7 and not first:
                    ffn_gate(c - 1, x2_t)

            def slot(b, qt, p, prev):
                heads_of(b, qt, p)
                if p == 0 and prev is not None and not (isinstance(b, int) and qt == 1):
                    c = QT * b + qt
                    if not isinstance(b, int) or c >= 3:
                        last_root(c - 3)
                if prev is not None:
                    segment(p, QT * prev[0] + prev[1], isinstance(b, int) and qt == 1)
                if p > 0:
                    subtract(b, qt, p - 1)
                elif prev is not None:
                    subtract(prev[0], prev[1], SLOTS - 1)

            def final():
                subtract(B - 1, QT - 1, SLOTS - 1)
                last_root(TILES - 3)
                for i in range(8):
                    segment(i, TILES - 1)
                last_root(TILES - 2)
                ffn_in(TILES - 1, x2_t0)
                ffn_gate(TILES - 1, x2_t0)
                last_root(TILES - 1)

            timeline(pool, slot, segment, final)

        @block.scalar
        def _(act):
            for dst, src in ((w_k2, "w_k2"), (w_v2, "w_v2"), (w_o, "w_o"), (w_q2, "w_q2"), (w_o2, "w_o2"), (w_r, "w_r"),
                             (ctx_t, "ctx_t")):
                act.dma_start(dst[:, :, :], a[src].rearrange("(c p) n -> p c n", p=P)).then_inc(ld_rest, 16)
            for b in range(B):
                act.dma_start(ctx_t2[:, :, b, :], a["ctx_t2"].rearrange("(c p) n -> p c n", p=P)[:, :, b * 2 * CTX:(b + 1) * 2 * CTX]
                              ).then_inc(ld_rest, 16)
            for dst, src in ((b_q, "b_q"), (b_k, "b_k")):
                act.dma_start(dst[:, :], a[src]).then_inc(ld_rest, 16)
            act.dma_start(b_v[:, :], a["b_v"]).then_inc(ld_rest, 16)
            act.dma_start(b_o[:, :], a["b_o"].partition_broadcast(P)).then_inc(ld_rest, 16)
            act.dma_start(b_r[:, :], a["b_r"].partition_broadcast(P)).then_inc(ld_rest, 16)
            act.dma_start(w_1[:, :, :, :], a["w_1"].rearrange("e (c p) n -> p e c n", p=P)).then_inc(ld_exp, 16)
            act.dma_start(w_2[:, :, :, :], a["w_2"].rearrange("e (c p) n -> p e c n", p=P)).then_inc(ld_exp, 16)
            act.dma_start(b_1[:, :, :], a["b_1"]).then_inc(ld_exp, 16)
            act.dma_start(b_2[:, :], a["b_2"]).then_inc(ld_exp, 16)

            act.wait_ge(ld_rest, val(16 * N_REST))
            for g in range(NC):
                act.wait_ge(c_k2, NC)
                nc.scalar.activation(k2_t[:, g, :], psO[:, g * 256:(g + 1) * 256], ACT.Identity,
                                     bias=b_k[:, g:g + 1]).then_inc(c_k2t, 1)
            nc.scalar.activation(b_q4[:, :], b_q[:, :], ACT.Copy, scale=1.0 / HD ** 0.5).then_inc(init, 1)

            def kept(t, k):
                act.wait_ge(a_turn, val(t + 1))
                ps = psP[:, k * 512:(k + 1) * 512].rearrange("p (c n) -> p c n", c=4)
                nc.scalar.activation(q_t[:, :, ds(t * P, P)], ps[:, 0:2, :], ACT.Copy,
                                     scale=1.0 / HD ** 0.5).then_inc(a_kept, 1)
                nc.scalar.activation(k_t[:, :, ds(t * P, P)], ps[:, 2:4, :], ACT.Copy).then_inc(a_kept, 1)

            def proj(t, k):
                act.wait_ge(a_proj, val(t + 1))
                wait(act, a_dve, SPARSE * (t - 1))
                nc.scalar.activation(raw[k][:, :], qkv_ps[k][:, 0:3 * D], ACT.Copy).then_inc(a_raw, 1)
                nc.scalar.activation(mag[k][:, :], qkv_ps[k][:, 0:3 * D], ACT.Abs).then_inc(a_raw, 1)

            proj(0, 0)
            proj(1, 1)
            kept(0, 0)
            with act.Fori(1, TILES // 2) as i:
                i = Linear(i)
                proj(2 * i, 0)
                kept(2 * i - 1, 1)
                proj(2 * i + 1, 1)
                kept(2 * i, 0)
            kept(TILES - 1, 1)

            def scores_out(b, qt, p):
                W = (qt + 1) * P
                s = 8 * (QT * b + qt) + p
                for k in range(2):
                    h, n = 2 * p + k, 2 * s + k
                    act.wait_ge(s_made, val(n + 1))
                    wait(act, exp_done, 2 * (n - 4) + 2)
                    nc.scalar.activation(S[h % 4][:, 0:W], psS[:, k * 512:k * 512 + W], ACT.Copy
                                         ).then_inc(s_ready, 1)

            def exps(b, qt, p):
                W = (qt + 1) * P
                s = 8 * (QT * b + qt) + p
                for k in range(2):
                    h, n = 2 * p + k, 2 * s + k
                    act.wait_ge(top_done, val(n + 1))
                    wait(act, prob_ready, n - 1)
                    nc.scalar.activation(e_all[k][:, 0:W], S[h % 4][:, 0:W], ACT.Exp,
                                         bias=neg_m[h % 4][:, :]).then_inc(exp_done, 1)
                    nc.scalar.activation(e_left[k][:, 0:W], left[h % 4][:, 0:W], ACT.Exp,
                                         bias=neg_m[h % 4][:, :]).then_inc(exp_done, 1)
                for k in range(2):
                    n = 2 * s + k
                    act.wait_ge(prob_turned, val(n + 1))
                    wait(act, pv_done, n - 1)
                    nc.scalar.activation(prob_t[k][:, 0:qt + 1, :],
                                         psP[:, k * 512:k * 512 + W].rearrange("p (c n) -> p c n", c=qt + 1),
                                         ACT.Copy).then_inc(probt_ready, 1)

            def out_of(made, count, dst, src, signal, func=ACT.Copy, **kw):
                act.wait_ge(made, val(count))
                nc.scalar.activation(dst, src, func, **kw).then_inc(signal, 1)

            def ffn_gates(f):
                out_of(f_turn, f + 1, gate_t[:, :], psB[0:NE, 0:P], f_t)
                act.wait_ge(f_b, val(f + 1))
                wait(act, f_hg, NE * f)
                nc.scalar.activation(gate_b[:, :, :], psC[:, :].rearrange("p (e n) -> p e n", e=NE), ACT.Copy
                                     ).then_inc(f_bc, 1)

            def ffn_hidden(f):
                for e in range(NE):
                    act.wait_ge(f_h, val(NE * f + e + 1))
                    wait(act, f_hg, NE * f + e - 1)
                    for g in range(NC):
                        nc.scalar.activation(hid[e % 2][:, g, :], psC[:, (e % 2) * 512 + g * P:(e % 2) * 512 + (g + 1) * P],
                                             ACT.Gelu, bias=b_1[:, e, g:g + 1]).then_inc(f_gelu, 1)

            def segment(i, c, first=False, zero=False):
                if i == 1:
                    out_of(g1_turn, c + 1, heads_t[:, :, :], turn, g1_t)
                if i == 2:
                    out_of(g2_turn, c + 1, x1_t[:, :, :], turn, g2_t)
                    for g in range(NC):
                        out_of(g2_q, NC * c + NC, q2_t[:, g, :], y_ps[:, g * P:(g + 1) * P], g2_qt,
                               ACT.Identity, bias=b_q4[:, g:g + 1], scale=1.0 / HD ** 0.5)
                if i == 3:
                    out_of(g2_dve, 2 * c + 2, p2[:, :], p2[:, :], g3_exp, ACT.Exp)
                    out_of(g3_turn, c + 1, p2_t[:, :], psC[:, :], g3_t)
                if i == 4:
                    out_of(g4_turn, c + 1, heads_t[:, :, :], turn, g4_t)
                if i == 5:
                    out_of(g5_turn, c + 1, (x2_t0 if zero else x2_t)[:, :, :], turn, g5_t)
                    out_of(g5_dve, ROUTE * c + 3, l_exp[:, :], logit[:, :], g5_exp, ACT.Exp)
                if i == 6 and not first:
                    ffn_gates(c - 1)
                if i == 7 and not first:
                    ffn_hidden(c - 1)

            def slot(b, qt, p, prev):
                scores_out(b, qt, p)
                if prev is not None:
                    zero = isinstance(b, int) and qt == 1
                    segment(p, QT * prev[0] + prev[1], zero, zero)
                if p > 0:
                    exps(b, qt, p - 1)
                elif prev is not None:
                    exps(prev[0], prev[1], SLOTS - 1)

            def final():
                exps(B - 1, QT - 1, SLOTS - 1)
                for i in range(8):
                    segment(i, TILES - 1)
                ffn_gates(TILES - 1)
                ffn_hidden(TILES - 1)

            act.wait_ge(ld_exp, val(16 * 4))
            timeline(act, slot, segment, final)

        @block.tensor
        def _(pe):
            def proj(t, k, i):
                pe.wait_ge(ld_xt[k], val(16 * (i + 1)))
                wait(pe, a_raw, 2 * (t - 1))
                for lo, hi in ((0, 2 * D), (2 * D, 3 * D)):
                    for c in range(NC):
                        mm = nc.tensor.matmul(qkv_ps[k][:, lo:hi], x_t[k][:, c, :], w_qkv[:, c, lo:hi],
                                              start=(c == 0), stop=(c == NC - 1))
                mm.then_inc(a_proj, 1)

            def turn_qk(t, k):
                pe.wait_ge(a_dve, val(SPARSE * (t + 1)))
                wait(pe, a_kept, 2 * (t - 1))
                for j in range(4):
                    mm = nc.tensor.transpose(psP[:, k * 512 + j * P:k * 512 + (j + 1) * P],
                                             qk_s[k][:, j * P:(j + 1) * P], ident[:, :])
                mm.then_inc(a_turn, 1)

            pe.wait_ge(ld_proj, 16)
            proj(0, 0, 0)
            proj(1, 1, 0)
            pe.wait_ge(ld_rest, val(16 * N_REST))
            pe.wait_ge(ld_const, val(16 * N_CONST))
            for g in range(NC):
                for c in range(NC):
                    mm = nc.tensor.matmul(psO[:, g * 256:(g + 1) * 256], w_k2[:, c, g * P:(g + 1) * P], ctx_t[:, c, :],
                                          start=(c == 0), stop=(c == NC - 1))
                mm.then_inc(c_k2, 1)
            for b in range(B):
                wait(pe, c_v2c, 2 * b)
                for c in range(NC):
                    nc.tensor.matmul(psB[:, 0:D], ctx_t2[:, c, b, :], w_v2[:, c, :], start=(c == 0), stop=False)
                nc.tensor.matmul(psB[:, 0:D], ones[0:1, :], b_v[:, :], start=False, stop=True).then_inc(c_v2, 1)
            turn_qk(0, 0)
            with pe.Fori(1, TILES // 2) as i:
                i = Linear(i)
                proj(2 * i, 0, i)
                turn_qk(2 * i - 1, 1)
                proj(2 * i + 1, 1, i)
                turn_qk(2 * i, 0)
            turn_qk(TILES - 1, 1)
            pe.wait_ge(a_kept, val(2 * TILES))
            pe.wait_ge(c_k2t, val(NC))
            pe.wait_ge(c_bd, val(B * NC))
            pe.wait_ge(c_v2c, val(2 * B))

            def scores(b, qt, p):
                W = (qt + 1) * P
                s = 8 * (QT * b + qt) + p
                for k in range(2):
                    h, n = 2 * p + k, 2 * s + k
                    pe.wait_ge(qh_ready, val(n + 1))
                    wait(pe, s_ready, n - 1)
                    out = psS[:, k * 512:k * 512 + W]
                    nc.tensor.matmul(out, q_h[h % 4][:, :], k_t[:, h // 8, ds(b * T, W)], start=True, stop=False)
                    nc.tensor.matmul(out[:, W - P:W], ident_h[:, :], causal_h[:, :], start=False, stop=True
                                     ).then_inc(s_made, 1)

            def values(b, qt, p):
                s = 8 * (QT * b + qt) + p
                for k in range(2):
                    n = 2 * s + k
                    pe.wait_ge(prob_ready, val(n + 1))
                    wait(pe, probt_ready, n - 1)
                    for j in range(qt + 1):
                        mm = nc.tensor.transpose(psP[:, k * 512 + j * P:k * 512 + (j + 1) * P],
                                                 prob[k][:, j * P:(j + 1) * P], ident[:, :])
                    mm.then_inc(prob_turned, 1)
                if p == 0:
                    wait(pe, g0, 2 * (QT * b + qt))
                for k in range(2):
                    h, n = 2 * p + k, 2 * s + k
                    pe.wait_ge(probt_ready, val(n + 1))
                    for j in range(qt + 1):
                        mm = nc.tensor.matmul(psO[:, h * VW:(h + 1) * VW], prob_t[k][:, j, :],
                                              v_s[:, ds(QT * b + j, 1), h, :].rearrange("p t v -> p (t v)"),
                                              start=(j == 0), stop=(j == qt))
                    mm.then_inc(pv_done, 1)

            def turned(ready, count, src, signal):
                pe.wait_ge(ready, val(count))
                for g in range(NC):
                    mm = nc.tensor.transpose(turn[:, g, :], src[:, g * P:(g + 1) * P], ident[:, :])
                mm.then_inc(signal, 1)

            def by_rows(ready, count, xt, w, signal, out):
                pe.wait_ge(ready, val(count))
                for c in range(NC):
                    mm = nc.tensor.matmul(out, xt[:, c, :], w[:, c, :], start=(c == 0), stop=(c == NC - 1))
                mm.then_inc(signal, 1)

            def ffn_gates(f, g):
                nc.tensor.transpose(psB[0:NE, 0:P], g[:, :], ident[:, :]).then_inc(f_turn, 1)
                pe.wait_ge(f_t, val(f + 1))
                for e in range(NE):
                    mm = nc.tensor.matmul(psC[:, e * P:(e + 1) * P], pick_row[:, e, :], gate_t[:, :],
                                          start=True, stop=True)
                mm.then_inc(f_b, 1)

            def ffn(f):
                def up(e):
                    pe.wait_ge(f_xin, val(NE * f + e + 1))
                    if e < 2:
                        pe.wait_ge(f_bc, val(f + 1))
                    else:
                        pe.wait_ge(f_gelu, val(2 * (NE * f + e - 1)))
                    for g in range(NC):
                        for c in range(NC):
                            mm = nc.tensor.matmul(psC[:, (e % 2) * 512 + g * P:(e % 2) * 512 + (g + 1) * P],
                                                  w_1[:, e, c, g * P:(g + 1) * P], x_in[:, e % 4, c, :],
                                                  start=(c == 0), stop=(c == NC - 1))
                    mm.then_inc(f_h, 1)

                def down(e):
                    pe.wait_ge(f_hg, val(NE * f + e + 1))
                    for c in range(NC):
                        mm = nc.tensor.matmul(y_ps, hid_g[e % 2][:, c, :], w_2[:, e, c, :],
                                              start=False, stop=(e == NE - 1 and c == NC - 1))
                    mm.then_inc(f_y, 1)

                nc.tensor.matmul(y_ps, gate_t[:, :], b_2[:, :], start=True, stop=False)
                up(0)
                for e in range(NE):
                    if e + 1 < NE:
                        up(e + 1)
                    down(e)

            def segment(i, c, first=False, zero=False):
                if i == 1:
                    wait(pe, f_ln, LN * (c - 2) + 1 if not isinstance(c, int) or c >= 2 else 0)
                    turned(g0, 2 * c + 2, heads_o, g1_turn)
                    by_rows(g1_t, c + 1, heads_t, w_o, g1_y, y_ps)
                if i == 2:
                    turned(g1_ln, LN * c + 4, x1, g2_turn)
                    pe.wait_ge(g2_t, val(c + 1))
                    for g in range(NC):
                        for cc in range(NC):
                            mm = nc.tensor.matmul(y_ps[:, g * P:(g + 1) * P], w_q2[:, cc, g * P:(g + 1) * P],
                                                  x1_t[:, cc, :], start=(cc == 0), stop=(cc == NC - 1))
                        mm.then_inc(g2_q, 1)
                    pe.wait_ge(g2_qt, val(NC * c + 2))
                    b = c // QT if isinstance(c, int) else None
                    for g in range(NC):
                        mm = nc.tensor.matmul(psC[:, g * 512:(g + 1) * 512], q2_t[:, g, :],
                                              k2_bd[:, ds(batch[0], 1), g, :, :].rearrange("p b h n -> p (b h n)"),
                                              start=True, stop=True)
                    mm.then_inc(g2_s, 1)
                if i == 3:
                    pe.wait_ge(g3_exp, val(c + 1))
                    for j in range(8):
                        mm = nc.tensor.transpose(psC[:, j * P:(j + 1) * P], p2[:, j * P:(j + 1) * P], ident[:, :])
                    mm.then_inc(g3_turn, 1)
                    pe.wait_ge(g3_t, val(c + 1))
                    for j in range(8):
                        mm = nc.tensor.matmul(psC[:, j * 2 * VW:(j + 1) * 2 * VW], p2_t[:, j * P:(j + 1) * P],
                                              v2_bd[:, ds(batch[0], 1), j, :].rearrange("p b n -> p (b n)"),
                                              start=True, stop=True)
                    mm.then_inc(g3_o, 1)
                if i == 4:
                    turned(g3_dve, 2 * c + 2, heads_o, g4_turn)
                    by_rows(g4_t, c + 1, heads_t, w_o2, g4_y, y_ps)
                if i == 5:
                    turned(g4_ln, LN * c + 4, x2_0 if zero else x2, g5_turn)
                    by_rows(g5_t, c + 1, x2_t0 if zero else x2_t, w_r, g5_l, y_ps[:, 0:NE])
                if i == 6 and not first:
                    pe.wait_ge(g5_dve, val(ROUTE * (c + 1)))
                    ffn_gates(c - 1, gate)
                if i == 7 and not first:
                    ffn(c - 1)

            batch = [0]

            def slot(b, qt, p, prev):
                scores(b, qt, p)
                if prev is not None:
                    batch[0] = prev[0]
                    zero = isinstance(b, int) and qt == 1
                    segment(p, QT * prev[0] + prev[1], zero, zero)
                if p > 0:
                    values(b, qt, p - 1)
                elif prev is not None:
                    values(prev[0], prev[1], SLOTS - 1)

            def final():
                values(B - 1, QT - 1, SLOTS - 1)
                batch[0] = B - 1
                for i in range(8):
                    segment(i, TILES - 1)
                pe.wait_ge(z_sum, 1)
                for k in range(2):
                    mm = nc.tensor.matmul(psO[0:NE, k:k + 1], gates_sum[:, k, :], ones[:, 0:1], start=True, stop=True)
                mm.then_inc(z_ps, 1)
                pe.wait_ge(f_ln, val(LN * (TILES - 2) + 1))
                pe.wait_ge(z_gate, 2)
                ffn_gates(TILES - 1, gate_0)
                ffn(TILES - 1)

            timeline(pe, slot, segment, final)

        @block.vector
        def _(dve):
            def settle():
                dve.sem_inc(carried, 1)

            nc.vector.memset(v2_bd[:, :, :, :], 0.0).then_inc(init, 1)
            nc.vector.memset(v_s[:, :, :, HD:VW], 1.0).then_inc(init, 1)
            dve.wait_ge(init, 3)
            nc.vector.memset(v2_bd[0:64, :, :, HD:VW], 1.0).then_inc(init, 1)
            nc.vector.memset(v2_bd[64:128, :, :, VW + HD:2 * VW], 1.0).then_inc(init, 1)
            dve.wait_ge(ld_const, val(16 * N_CONST))

            wt = first_wt[:, :].unsqueeze(1).to_broadcast([P, 3 * NH, HD])

            def grouped(t):
                return t[:, :].rearrange("p (h j) -> p h j", j=HD)

            def spread(t):
                return t[:, :].unsqueeze(2).to_broadcast([P, 3 * NH, HD])

            def sparsify(t, k):
                step = link(dve, a_dve, SPARSE * t)
                dve.wait_ge(a_raw, val(2 * (t + 1)))
                wait(dve, a_turn, t - 1)

                def first_largest(top):
                    dve_in = grouped(mag[k])
                    step(nc.vector.tensor_reduce(grp_f[:, :], dve_in, X, ALU.max))
                    step.caught_up()
                    step(nc.vector.tensor_tensor(grouped(hit), dve_in, spread(grp_f), ALU.is_equal))
                    step.caught_up()
                    step(nc.vector.tensor_tensor(grouped(hit_w), grouped(hit), wt, ALU.mult))
                    step.caught_up()
                    step(nc.vector.tensor_reduce(grp_h[:, :], grouped(hit_w), X, ALU.max))
                    step.caught_up()
                    step(nc.vector.tensor_tensor(grouped(top), grouped(hit_w), spread(grp_h), ALU.is_equal))
                    step.caught_up()

                first_largest(top1)
                step(nc.vector.scalar_tensor_tensor(out=mag[k][:, :], in0=top1[:, :], scalar=NEG, in1=mag[k][:, :],
                                                    op0=ALU.mult, op1=ALU.add))
                step.caught_up()
                first_largest(top2)
                step(nc.vector.tensor_tensor(top1[:, :], top1[:, :], top2[:, :], ALU.add))
                step.caught_up()
                step(nc.vector.tensor_tensor(qk_s[k][:, :], raw[k][:, 0:2 * D], top1[:, 0:2 * D], ALU.mult))
                step.caught_up()
                step(nc.vector.tensor_tensor(
                    v_s[:, ds(t, 1), :, 0:HD].rearrange("p t h j -> p (t h) j"),
                    raw[k][:, 2 * D:3 * D].rearrange("p (h j) -> p h j", j=HD),
                    top1[:, 2 * D:3 * D].rearrange("p (h j) -> p h j", j=HD), ALU.mult))
                step.caught_up()
                assert step.n[0] == SPARSE

            sparsify(0, 0)
            dve.wait_ge(init, 5)
            for b in range(B):
                dve.wait_ge(c_v2, val(b + 1))
                for j in range(2):
                    src = psB[64 * j:64 * j + 64, 0:D].rearrange("p (m j n) -> p m j n", j=2, n=HD)[:, :, j, :]
                    nc.vector.tensor_copy(v2_bd[64 * j:64 * j + 64, b, :, j * VW:j * VW + HD], src).then_inc(c_v2c, 1)
            sparsify(1, 1)
            with dve.Fori(1, TILES // 2) as i:
                i = Linear(i)
                sparsify(2 * i, 0)
                sparsify(2 * i + 1, 1)

            def select(b, qt, p):
                W = (qt + 1) * P
                s = 8 * (QT * b + qt) + p
                n = [0]
                heads = [(2 * p + k) % 4 for k in range(2)]
                wait(dve, top_done, 2 * s)
                settle()
                dve.sem_clear(top_step)

                def step(ins):
                    ins.then_inc(top_step, 1)
                    n[0] += 1

                def caught_up(steps=2):
                    dve.wait_ge(top_step, n[0] - steps + 1)

                for k, r in enumerate(heads):
                    dve.wait_ge(s_ready, val(2 * s + k + 1))
                    wait(dve, exp_done, 4 * (s - 1) + 2 * k - 2)
                    settle()
                    step(nc.vector.max(eight0[r][:, :], S[r][:, 0:W]))
                for r in heads:
                    caught_up()
                    step(nc.vector.match_replace(left[r][:, 0:W], eight0[r][:, :], S[r][:, 0:W], GONE))
                for r in heads:
                    step(nc.vector.tensor_scalar(neg_m[r][:, :], eight0[r][:, 0:1], -1.0, None, ALU.mult))
                for j in range(1, ROUNDS):
                    for r in heads:
                        caught_up(4 if j == 1 else 2)
                        step(nc.vector.max(eight[r][:, :], left[r][:, 0:W]))
                    for r in heads:
                        caught_up()
                        last = nc.vector.match_replace(left[r][:, 0:W], eight[r][:, :], left[r][:, 0:W], GONE)
                        if j < ROUNDS - 1:
                            step(last)
                        else:
                            last.then_inc(top_done, 1)
                            n[0] += 1

            def norm(c, signal, rs, y, ready, x_in_, out, extra=None):
                step = link(dve, signal, LN * c)
                dve.wait_ge(ready[0], val(ready[1]))
                if extra:
                    dve.wait_ge(extra[0], val(extra[1]))
                step(nc.vector.tensor_tensor(res[:, :], y, x_in_, ALU.add))
                step.caught_up()
                step(nc.vector.bn_stats(stats[:, :], res[:, :]))
                step.caught_up()
                settle()
                step(nc.vector.bn_aggr(mv[:, :], stats[:, :]))
                step.caught_up()
                dve.wait_ge(rs, val(2 * c + 2))
                step(nc.vector.tensor_scalar(out, res[:, :], mv[:, 0:1], rstd[:, 0:1], ALU.subtract, ALU.mult))
                step.caught_up()

            def normed_heads(c, signal, ready, ps):
                dve.wait_ge(ready[0], val(ready[1]))
                nc.vector.reciprocal(den[:, :], ps[:, :, HD]).then_inc(signal, 1)
                dve.wait_ge(signal, val(2 * c + 1))
                nc.vector.tensor_tensor(heads_o[:, :].rearrange("p (h j) -> p h j", j=HD), ps[:, :, 0:HD],
                                        den[:, :].unsqueeze(2).to_broadcast([P, NH, HD]), ALU.mult
                                        ).then_inc(signal, 1)
                dve.wait_ge(signal, val(2 * c + 2))

            def last_norm(c, f, x):
                if not isinstance(f, int) or f > 0:
                    dve.wait_ge(out_done, val(16 * f))
                norm(f, f_ln, rs7, y_ps, (f_y, NE * (f + 1)), x[:, :], fin[:, :])

            def route(c, gt):
                step = link(dve, g5_dve, ROUTE * c)
                v = nc.vector
                dve.wait_ge(g5_l, val(c + 1))
                step(v.tensor_tensor(logit[:, :], y_ps[:, 0:NE], b_r[:, :], ALU.add))
                step.caught_up()
                step(v.tensor_reduce(l_max[:, :], logit[:, :], X, ALU.max))
                step.caught_up()
                step(v.tensor_scalar(logit[:, :], logit[:, :], l_max[:, 0:1], None, ALU.subtract))
                dve.wait_ge(g5_exp, val(c + 1))
                e_j = l_exp[:, :].unsqueeze(1).to_broadcast([P, NE, NE])
                e_i = l_exp[:, :].unsqueeze(2).to_broadcast([P, NE, NE])
                step(v.tensor_tensor(above[:, :, :], e_j, e_i, ALU.is_gt))
                step(v.tensor_tensor(tied[:, :, :], e_j, e_i, ALU.is_equal))
                step.caught_up()
                step(v.tensor_tensor(tied[:, :, :], tied[:, :, :], earlier[:, :, :], ALU.mult))
                step.caught_up()
                step(v.tensor_tensor(above[:, :, :], above[:, :, :], tied[:, :, :], ALU.add))
                step.caught_up()
                step(v.tensor_reduce(rank[:, :], above[:, :, :], X, ALU.add))
                step.caught_up()
                for k in range(2):
                    step(v.scalar_tensor_tensor(out=chosen[:, k, :], in0=rank[:, :], scalar=float(k), in1=l_exp[:, :],
                                                op0=ALU.is_equal, op1=ALU.mult))
                step.caught_up()
                step(v.tensor_tensor(both[:, :], chosen[:, 0, :], chosen[:, 1, :], ALU.add))
                step.caught_up()
                step(v.tensor_reduce(l_sum[:, :], both[:, :], X, ALU.add))
                step.caught_up()
                step(v.reciprocal(l_rec[:, :], l_sum[:, :]))
                step.caught_up()
                v.tensor_scalar(gates[:, ds(c, 1), :].rearrange("p t e -> p (t e)"),
                                chosen[:, :, :].rearrange("p k e -> p (k e)"), l_rec[:, 0:1], None, ALU.mult)
                step(v.tensor_scalar(gt[:, :], both[:, :], l_rec[:, 0:1], CAPACITY, ALU.mult, ALU.min))
                assert step.n[0] == ROUTE
                step.caught_up()

            batch_of, qt_of = [0], [0]

            def segment(i, c, zero=False):
                v = nc.vector
                if i == 0:
                    normed_heads(c, g0, (pv_done, NH * (c + 1)),
                                 psO[:, 0:NH * VW].rearrange("p (h j) -> p h j", j=VW))
                if i == 1:
                    k = qt_of[0] % 2
                    norm(c, g1_ln, rs1, y_ps, (g1_y, c + 1), x_rows[k][:, :], x1[:, :],
                         (ld_xr[k], 16 * (QT // 2 * batch_of[0] + qt_of[0] // 2 + 1)))
                if i == 2:
                    ps = psC[:, :].rearrange("p (h n) -> p h n", n=CTX)
                    dve.wait_ge(g2_s, val(c + 1))
                    v.tensor_reduce(m2[:, :], ps, X, ALU.max).then_inc(g2_dve, 1)
                    dve.wait_ge(g2_dve, val(2 * c + 1))
                    v.tensor_tensor(p2[:, :].rearrange("p (h n) -> p h n", n=CTX), ps,
                                    m2[:, :].unsqueeze(2).to_broadcast([P, NH, CTX]), ALU.subtract
                                    ).then_inc(g2_dve, 1)
                if i == 3:
                    normed_heads(c, g3_dve, (g3_o, c + 1),
                                 psC[:, 0:NH * VW].rearrange("p (h j) -> p h j", j=VW))
                if i == 4:
                    norm(c, g4_ln, rs4, y_ps, (g4_y, c + 1), x1b[:, :], (x2_0 if zero else x2)[:, :],
                         (x1b_ready, c + 1))
                if i == 5:
                    route(c, gate_0 if zero else gate)

            def slot(b, qt, p, prev):
                select(b, qt, p)
                if prev is not None:
                    batch_of[0], qt_of[0] = prev
                    c = QT * prev[0] + prev[1]
                    zero = isinstance(b, int) and qt == 1
                    if p == 0 and not (isinstance(c, int) and c < 2):
                        last_norm(c - 1, c - 2, x2)
                    segment(p, c, zero)

            def final():
                last_norm(TILES - 2, TILES - 3, x2)
                batch_of[0], qt_of[0] = B - 1, QT - 1
                for i in range(8):
                    segment(i, TILES - 1)
                v = nc.vector
                v.tensor_reduce(gates_sum[:, :, :].rearrange("p k e -> p (k e)"),
                                gates[:, :, :].rearrange("p t e -> p e t"), X, ALU.add).then_inc(z_sum, 1)
                dve.wait_ge(z_ps, 1)
                v.tensor_tensor(gate_0[0:NE, 0:2], gate_0[0:NE, 0:2], psO[0:NE, 0:2], ALU.add).then_inc(z_gate, 1)
                dve.wait_ge(z_gate, 1)
                v.tensor_scalar(gate_0[:, :], gate_0[:, :], CAPACITY, None, ALU.min).then_inc(z_gate, 1)
                last_norm(TILES - 1, TILES - 2, x2)
                last_norm(0, TILES - 1, x2_0)

            dve.wait_ge(ld_rest, val(16 * N_REST))
            timeline(dve, slot, segment, final)


def host_constants():
    bf = mybir.dt.np(BF16)
    i = np.arange(P)
    c = {}
    c["ident"] = np.eye(P, dtype=np.float32)
    c["ident_h"] = np.eye(P, dtype=np.float32).astype(bf)
    c["causal_h"] = np.where(i[None, :] > i[:, None], NEG, 0.0).astype(np.float32).astype(bf)
    c["head_rows"] = np.repeat((i[:, None] // HD == np.arange(8)[None, :]).astype(np.float32)[:, :, None], P, axis=2)
    c["first_wt"] = np.repeat((HD - np.arange(HD, dtype=np.float32))[None, :], P, axis=0).astype(bf)
    e = np.arange(NE)
    c["earlier"] = np.repeat((e[None, None, :] < e[None, :, None]).astype(np.float32), P, axis=0)
    c["pick_row"] = np.repeat((e[:, None] == e[None, :]).astype(np.float32)[:, :, None], P, axis=2)
    c["ones"] = np.ones((P, P), np.float32)
    c["eps"] = np.full((P, 1), EPS, np.float32)
    c["half"] = np.full((P, 1), -0.5, np.float32)
    return c


def kernel(**inputs):
    import concourse.bacc as bacc
    from concourse.bass_utils import run_bass_kernel_spmd

    i = {k: np.asarray(v) for k, v in inputs.items()}
    arrays = host_constants()
    x = i["x"].reshape(B * T, D)
    arrays["x"] = x
    arrays["x_t"] = x.T
    arrays["w_qkv"] = np.concatenate([i["L0_attn_wq"].T, i["L0_attn_wk"].T, i["L0_attn_wv"].T], axis=1)
    arrays["w_o"] = i["L0_attn_wo"].T
    for n in "qkvo":
        arrays[f"w_{n}2"] = i[f"L0_xattn_w{n}"].T
    arrays["b_q"] = i["L0_xattn_bq"].reshape(NC, P).T
    arrays["b_k"] = i["L0_xattn_bk"].reshape(NC, P).T
    arrays["b_v"] = i["L0_xattn_bv"].reshape(1, D)
    arrays["b_o"] = i["L0_xattn_bo"]
    c = i["ctx_1024"].reshape(B, CTX, D)
    arrays["ctx_t"] = c.reshape(B * CTX, D).T
    arrays["ctx_t2"] = np.concatenate([c, c], axis=1).reshape(B * 2 * CTX, D).T
    arrays["w_r"] = i["L0_ffn_router_w"]
    arrays["b_r"] = i["L0_ffn_router_b"]
    arrays["w_1"] = i["L0_ffn_w1"]
    arrays["b_1"] = i["L0_ffn_b1"].reshape(NE, NC, P).transpose(2, 0, 1)
    arrays["w_2"] = i["L0_ffn_w2"]
    arrays["b_2"] = i["L0_ffn_b2"]
    arrays = {k: np.ascontiguousarray(v) for k, v in arrays.items()}

    nc = bacc.Bacc("TRN2", target_bir_lowering=False, num_devices=1)
    aps = {k: nc.dram_tensor(f"in_{k}", v.shape, mybir.dt.from_np(v.dtype), kind="ExternalInput").ap()
           for k, v in arrays.items()}
    aps["out"] = nc.dram_tensor("out_0", (B * T, D), F32, kind="ExternalOutput").ap()
    build(nc, aps)
    r = run_bass_kernel_spmd(nc, [{f"in_{k}": v for k, v in arrays.items()}], core_ids=[0])
    return r.results[0]["out_0"].reshape(B, T, D)
```

```python
from contextlib import ExitStack

import concourse.bass as bass
from concourse import mybir
from concourse.alu_op_type import AluOpType as ALU
import numpy as np

F32 = mybir.dt.float32
BF16 = mybir.dt.bfloat16
ACT = mybir.ActivationFunctionType
X = mybir.AxisListType.X


def ds(start, size):
    return bass.ds(val(start), size)

P = 128
B, T, D = 4, 512, 256
NH, HD = 16, 16
NC = D // P
QT = T // P
TILES = B * QT
KEEP = 64
ROUNDS = KEEP // 8
CTX = 64
NE, FH = 8, 256
CAPACITY = float(max(int(B * T * 1.25 / NE), 4))
EPS = 1e-5
NEG = -1.0e30
BELOW = -2.0e30
BIG = 2.0 ** 101
GONE = -3.0e38
SLOTS = NH // 2
VW = HD + 1
SPARSE = 9
SPREAD = 3
NOTES = 3
ROUTE = 14
LN = 4
SEGMENTS = 13


class Linear:
    def __init__(self, reg, times=1, plus=0):
        self.reg, self.times, self.plus = reg, times, plus

    def __add__(self, n):
        return Linear(self.reg, self.times, self.plus + n)

    def __sub__(self, n):
        return self + -n

    def __mul__(self, n):
        return Linear(self.reg, self.times * n, self.plus * n)

    __radd__, __rmul__ = __add__, __mul__


def val(n):
    if not isinstance(n, Linear):
        return n
    scaled = n.reg * n.times if n.times != 1 else n.reg
    return scaled + n.plus if n.plus else scaled


def wait(eng, sem, value):
    if isinstance(value, Linear) or value > 0:
        eng.wait_ge(sem, val(value))


def build(nc, a):
    nc.disable_value_cache = True
    with ExitStack() as ctx:
        def sb(name, shape, dt=F32):
            return ctx.enter_context(nc.sbuf_tensor(name, shape, dt))

        def sem(name):
            return ctx.enter_context(nc.semaphore(name))

        w_o = sb("w_o", [P, NC, D])
        w_q2 = sb("w_q2", [P, NC, D])
        w_k2 = sb("w_k2", [P, NC, D])
        w_v2 = sb("w_v2", [P, NC, D])
        w_o2 = sb("w_o2", [P, NC, D])
        w_r = sb("w_r", [P, NC, NE])
        w_1 = sb("w_1", [P, NE, NC, FH])
        w_2 = sb("w_2", [P, NE, NC, D])
        b_q = sb("b_q", [P, NC])
        b_q4 = sb("b_q4", [P, NC])
        b_k = sb("b_k", [P, NC])
        b_v = sb("b_v", [1, D])
        b_o = sb("b_o", [P, D])
        b_r = sb("b_r", [P, NE])
        b_1 = sb("b_1", [P, NE, NC])
        b_2 = sb("b_2", [NE, D])
        x_rows = [sb(f"x_rows{k}", [P, D]) for k in range(2)]
        ident = sb("ident", [P, P])
        ident_h = sb("ident_h", [P, P], BF16)
        causal_h = sb("causal_h", [P, P], BF16)
        head_rows = sb("head_rows", [P, 8, P])
        earlier = sb("earlier", [P, NE, NE])
        pick_row = sb("pick_row", [NE, NE, P])
        ones = sb("ones", [P, 1])
        eps = sb("eps", [P, 1])
        half = sb("half", [P, 1])

        q_t = sb("q_t", [P, NC, B * T])
        k_t = sb("k_t", [P, NC, B * T])
        v_s = sb("v_s", [P, TILES, NH, VW])

        k2_bd = sb("k2_bd", [P, B, NC, 8, CTX])
        v2_bd = sb("v2_bd", [P, B, 8, 2 * VW])

        q_h = [sb(f"q_h{k}", [P, P]) for k in range(4)]
        S_all = sb("S_all", [P, 8, T])
        S = [S_all[:, k, :] for k in range(8)]
        count = sb("count", [P, 2, T])
        y = [count[:, k, :] for k in range(2)]
        mark = [sb(f"mark{k}", [P, T], BF16) for k in range(2)]
        over = [sb(f"over{k}", [P, T], BF16) for k in range(4)]
        keep = [sb(f"keep{k}", [P, T], BF16) for k in range(2)]
        signs = [sb(f"signs{k}", [P, T], BF16) for k in range(2)]
        sided = [sb(f"sided{k}", [P, T], BF16) for k in range(4)]
        neg_m48 = sb("grp_f", [P, 3 * NH])
        late = sb("late", [P, 1])
        drop = sb("drop", [P, 1])
        iota8 = sb("iota8", [P, 8])
        neg_m = sb("neg_m", [P, 4, 2])
        balance = sb("balance", [P, 4, 2])
        filled = sb("filled", [P, 4, 2])
        turn_to = sb("turn_to", [P, 4, 2])
        ranks = sb("ranks", [P, 4, 2])
        thresh = sb("thresh", [P, 4, 2])
        balance1 = sb("balance1", [P, 4, 2])
        far = sb("far", [1, 4], mybir.dt.int32)
        far_f = sb("far_f", [P, 4])
        r_pos = sb("r_pos", [P, 2])
        r_neg = sb("r_neg", [P, 2])
        spare = sb("spare", [P, 2])
        dist = sb("dist", [P, 2, 8])
        eight = sb("eight", [P, 2, 8])
        hit8 = sb("hit8", [P, 2, 8])
        found = sb("found", [P, 2, 8])
        wanted = sb("wanted", [P, 2])
        prob = [sb(f"prob{k}", [P, T]) for k in range(2)]
        prob_t_all = sb("prob_t", [P, 2, QT, P])
        prob_t = [prob_t_all[:, k, :, :] for k in range(2)]

        den = sb("den", [P, NH])
        heads_o = sb("heads_o", [P, D])
        heads_t = sb("heads_t", [P, NC, P])
        res = sb("res", [P, D])
        stats = [sb(f"stats{k}", [P, 6]) for k in range(2)]
        mv = [sb(f"mv{k}", [P, 2]) for k in range(2)]
        var_e = [sb(f"var_e{k}", [P, 1]) for k in range(2)]
        rstd = [sb(f"rstd{k}", [P, 1]) for k in range(2)]
        x_all = sb("x_all", [P, 3, D])
        x1, x1b, x2 = (x_all[:, j, :] for j in range(3))
        x1_t = sb("x1_t", [P, NC, P])
        q2_t = sb("q2_t", [P, NC, P])
        m2 = sb("m2", [P, NH])
        p2 = sb("p2", [P, NH * CTX])
        p2_t = sb("p2_t", [P, NH * CTX])
        x2_0 = sb("x2_0", [P, D])
        x2_t = sb("x2_t", [P, NC, P])
        x2_t0 = sb("x2_t0", [P, NC, P])
        logit = sb("logit", [P, NE])
        l_max = sb("l_max", [P, 1])
        l_exp = sb("l_exp", [P, NE])
        above = sb("above", [P, NE, NE])
        tied = sb("tied", [P, NE, NE])
        rank = sb("rank", [P, NE])
        chosen = sb("chosen", [P, 2, NE])
        both = sb("both", [P, NE])
        l_sum = sb("l_sum", [P, 1])
        l_rec = sb("l_rec", [P, 1])
        gate = sb("gate", [P, NE])
        gate_0 = sb("gate_0", [P, NE])
        gates = sb("gates", [P, TILES, 2 * NE])
        gates_sum = sb("gates_sum", [P, 2, NE])
        gate_t = sb("gate_t", [NE, P])
        gate_b = sb("gate_b", [P, NE, P])
        x_in = sb("x_in", [P, 2, NC, P])
        hid_all = sb("hid_all", [P, 4, NC, P])
        hid = [hid_all[:, k, :, :] for k in range(2)]
        hid_g = [hid_all[:, 2 + k, :, :] for k in range(2)]
        fin = sb("fin", [P, D])

        w_qkv = S_all[:, :, :].rearrange("p k n -> p (k n)")[:, 0:NC * 3 * D].rearrange("p (c n) -> p c n", c=NC)
        flat_S = S_all[:, :, :].rearrange("p k n -> p (k n)")
        raw = [flat_S[:, NC * 3 * D:(NC + 1) * 3 * D], x_all[:, :, :].rearrange("p k n -> p (k n)")]
        flat_hid = hid_all[:, :, :, :].rearrange("p e c n -> p (e c n)").rearrange("p (j c n) -> p j c n", j=2, c=NC)
        ctx_t, k2_t = flat_hid[:, 0, :, :], flat_hid[:, 1, :, :]
        mag = [p2[:, 0:3 * D], p2_t[:, 0:3 * D]]
        halves = [flat_S[:, (NC + 1) * 3 * D:][:, j * 3 * D // 2:(j + 1) * 3 * D // 2] for j in range(4)]
        hit, nth, sel, same_head = (t.bitcast(BF16)[:, 0:3 * D] for t in halves)
        top1, top2 = (t.bitcast(BF16)[:, 0:3 * D] for t in y)
        qk_s = [prob[k][:, :] for k in range(2)]
        x_t = [prob_t[k][:, 0:NC, :] for k in range(2)]
        grp_f = neg_m48
        ctx_t2 = gate_b[:, :, :].rearrange("p e n -> p (e n)").rearrange("p (c b n) -> p c b n", c=NC, b=B)

        psC = ctx.enter_context(nc.psum_tensor("psC", [P, 1024], F32))
        psSF = ctx.enter_context(nc.psum_tensor("psSF", [P, 1024], F32))
        psPU = ctx.enter_context(nc.psum_tensor("psPU", [P, 1024], F32))
        psO = ctx.enter_context(nc.psum_tensor("psO", [P, 512], F32))
        psB = ctx.enter_context(nc.psum_tensor("psB", [P, 512], F32))
        psS = psSF[:, 0:512]
        psF = psSF[:, 512:512 + D]
        psP = psPU[:, 0:512]
        up_ps = [psPU[:, 512 + j * D:512 + (j + 1) * D] for j in range(2)]
        turn = psB[:, 0:D].rearrange("p (c n) -> p c n", c=NC)
        y_ps = psB[:, D:2 * D]
        qkv_ps = [psC, psSF]

        ld_proj = sem("ld_proj")
        ld_const = sem("ld_const")
        ld_rest = sem("ld_rest")
        ld_exp = sem("ld_exp")
        ld_xt = [sem(f"ld_xt{k}") for k in range(2)]
        ld_xr = [sem(f"ld_xr{k}") for k in range(2)]
        a_proj = sem("a_proj")
        a_raw = sem("a_raw")
        a_dve = sem("a_dve")
        a_sel = sem("a_sel")
        a_turn = sem("a_turn")
        a_kept = sem("a_kept")
        init = sem("init")
        carried = sem("carried")
        pool_carried = sem("pool_carried")
        c_k2 = sem("c_k2")
        c_k2t = sem("c_k2t")
        c_bd = sem("c_bd")
        c_v2 = sem("c_v2")
        c_v2c = sem("c_v2c")
        qh_ready = sem("qh_ready")
        s_made = sem("s_made")
        s_ready = sem("s_ready")
        counted = sem("counted")
        step = sem("step")
        picked = sem("picked")
        noted = sem("noted")
        flag_made = sem("flag_made")
        flag_ready = sem("flag_ready")
        sided_ready = sem("sided_ready")
        thresh_ready = sem("thresh_ready")
        over_ready = sem("over_ready")
        keep_ready = sem("keep_ready")
        exp_done = sem("exp_done")
        prob_ready = sem("prob_ready")
        prob_turned = sem("prob_turned")
        probt_ready = sem("probt_ready")
        pv_done = sem("pv_done")
        g0 = sem("g0_heads")
        g1_turn, g1_t, g1_y, g1_ln = sem("g1_turn"), sem("g1_t"), sem("g1_y"), sem("g1_ln")
        rs1, x1b_ready = sem("rs1"), sem("x1b_ready")
        g2_turn, g2_t, g2_q, g2_qt, g2_s, g2_dve = (sem(n) for n in (
            "g2_turn", "g2_t", "g2_q", "g2_qt", "g2_s", "g2_dve"))
        g3_exp, g3_turn, g3_t, g3_o, g3_dve = (sem(n) for n in (
            "g3_exp", "g3_turn", "g3_t", "g3_o", "g3_dve"))
        g4_turn, g4_t, g4_y, g4_ln, rs4 = (sem(n) for n in ("g4_turn", "g4_t", "g4_y", "g4_ln", "rs4"))
        g5_turn, g5_t, g5_l, g5_dve, g5_exp = (sem(n) for n in (
            "g5_turn", "g5_t", "g5_l", "g5_dve", "g5_exp"))
        f_turn, f_t, f_b, f_bc, f_xin, f_h, f_gelu, f_hg, f_y, f_ln, rs7 = (sem(n) for n in (
            "f_turn", "f_t", "f_b", "f_bc", "f_xin", "f_h", "f_gelu", "f_hg", "f_y", "f_ln", "rs7"))
        z_sum, z_ps, z_gate = sem("z_sum"), sem("z_ps"), sem("z_gate")
        out_done = sem("out_done")

        block = ctx.enter_context(nc.Block())

        def link(eng, signal, base):
            n = [0]

            def chain(ins):
                n[0] += 1
                ins.then_inc(signal, 1)
                return n[0]

            def caught_up():
                wait(eng, signal, base + n[0])
            chain.caught_up = caught_up
            chain.n = n
            return chain

        def qtile(b, qt):
            return b * T + qt * P

        def in_order(pieces):
            for _, piece in sorted(pieces, key=lambda x: x[0]):
                piece()

        def timeline(eng, attention, segment, last, first=lambda p: []):
            def parts(i, c, f, b, qt):
                late = isinstance(c, int) and c == 0
                both = segment(i, c, f, b, qt) if i < 7 or not late else []
                return both + (segment("gates", c, f, b, qt) if i == 6 and not late else [])

            def slot(p, now, prev, before):
                pieces = []
                for lag, kind in enumerate(("scores", "classify", "select", "keep", "out")):
                    tile, q = (now, p - lag) if p >= lag else (prev, SLOTS + p - lag)
                    if tile is not None:
                        pieces += attention(kind, tile[0], tile[1], q)
                if p >= 3 and prev is not None:
                    c = QT * prev[0] + prev[1]
                    pieces += parts(p - 3, c, c - 1, *prev)
                if before is not None:
                    c = QT * before[0] + before[1]
                    pieces += parts(p + 5, c, c - 1, *before)
                in_order([*pieces, *first(p)])

            def tile(now, prev, before):
                for p in range(SLOTS):
                    slot(p, now, prev, before)

            for qt in range(QT):
                tile((0, qt), (0, qt - 1) if qt > 0 else None, (0, qt - 2) if qt > 1 else None)
            with eng.Fori(1, B) as b:
                b = Linear(b)
                for qt in range(QT):
                    tile((b, qt), *((b, qt - j) if qt >= j else (b - 1, QT + qt - j) for j in (1, 2)))
            tile(None, (B - 1, QT - 1), (B - 1, QT - 2))
            final, zero = (TILES - 1, TILES - 2, B - 1, QT - 1), (0, TILES - 1, 0, 0)
            for i in (5, 6):
                in_order(parts(i, *final))
            last()
            for i in range(7, SEGMENTS + 5):
                in_order([*(parts(i, *final) if i < SEGMENTS else []),
                          *(segment("gates" if i == 11 else i - 5, *zero) if i >= 11 else [])])

        @block.sync
        def _(sp):
            def load_xt(t, k):
                sp.dma_start(x_t[k][:, :, :], a["x_t"].rearrange("(c p) n -> p c n", p=P)[:, :, ds(t * P, P)]
                             ).then_inc(ld_xt[k], 16)

            load_xt(0, 0)
            sp.dma_start(w_qkv[:, :, :], a["w_qkv"].rearrange("(c p) n -> p c n", p=P)).then_inc(ld_proj, 16)
            load_xt(1, 1)
            for dst, src in ((ident, "ident"), (ident_h, "ident_h"), (causal_h, "causal_h"), (same_head, "same_head"),
                             (half, "half"), (eps, "eps"), (late, "late"), (drop, "drop"), (iota8, "iota8")):
                sp.dma_start(dst[:, :], a[src]).then_inc(ld_const, 16)
            for dst, src in ((head_rows, "head_rows"), (earlier, "earlier"), (pick_row, "pick_row")):
                sp.dma_start(dst[:, :, :], a[src]).then_inc(ld_const, 16)
            sp.dma_start(ones[:, :], a["ones"]).then_inc(ld_const, 16)
            with sp.Fori(0, TILES // 2 - 1) as i:
                i = Linear(i)
                for k in range(2):
                    sp.wait_ge(a_proj, val(2 * i + (k + 1)))
                    load_xt(2 * i + (k + 2), k)

            x_tiles = a["x"].rearrange("(t p) n -> p t n", p=P)
            out_tiles = a["out"].rearrange("(t p) n -> p t n", p=P)

            def load_rows(c, k):
                wait(sp, g1_ln, LN * (c - 2) + 1)
                sp.dma_start(x_rows[k][:, :].unsqueeze(1), x_tiles[:, ds(c, 1), :]).then_inc(ld_xr[k], 16)

            def store(c, f):
                sp.wait_ge(f_ln, val(LN * (f + 1)))
                sp.dma_start(out_tiles[:, ds(c, 1), :], fin[:, :].unsqueeze(1)).then_inc(out_done, 16)

            for c in range(QT):
                load_rows(c, c % 2)
                if c >= 3:
                    store(c - 2, c - 3)
            with sp.Fori(1, B) as b:
                b = Linear(b)
                for qt in range(QT):
                    load_rows(QT * b + qt, qt % 2)
                    store(QT * b + (qt - 2), QT * b + (qt - 3))
            store(TILES - 2, TILES - 3)
            store(TILES - 1, TILES - 2)
            store(0, TILES - 1)
            sp.wait_ge(out_done, val(16 * TILES))

        N_CONST, N_REST = 13, 16

        @block.gpsimd
        def _(pool):
            pool.wait_ge(ld_const, val(16 * N_CONST))
            pool.wait_ge(c_k2t, val(NC))
            for b in range(B):
                for g in range(NC):
                    nc.gpsimd.tensor_tensor(
                        k2_bd[:, b, g, :, :],
                        k2_t[:, g, b * CTX:(b + 1) * CTX].unsqueeze(1).to_broadcast([P, 8, CTX]),
                        head_rows[:, :, 0:CTX], ALU.mult).then_inc(c_bd, 1)

            def selected(t, k):
                chain = link(pool, a_sel, SPREAD * t)
                pool.wait_ge(a_dve, val(SPARSE * (t + 1)))
                chain(nc.gpsimd.tensor_tensor(sel[:, :], top1[:, :], top2[:, :], ALU.add))
                chain.caught_up()
                wait(pool, a_turn, t - 1)
                chain(nc.gpsimd.tensor_tensor(qk_s[k][:, :], raw[k][:, 0:2 * D], sel[:, 0:2 * D], ALU.mult))
                chain(nc.gpsimd.tensor_tensor(
                    v_s[:, ds(t, 1), :, 0:HD].rearrange("p t h j -> p (t h) j"),
                    raw[k][:, 2 * D:3 * D].rearrange("p (h j) -> p h j", j=HD),
                    sel[:, 2 * D:3 * D].rearrange("p (h j) -> p h j", j=HD), ALU.mult))
                chain.caught_up()
                assert chain.n[0] == SPREAD

            selected(0, 0)
            selected(1, 1)
            with pool.Fori(1, TILES // 2) as i:
                i = Linear(i)
                selected(2 * i, 0)
                selected(2 * i + 1, 1)
            pool.wait_ge(a_kept, val(2 * TILES))

            def heads_of(b, qt, p):
                s = 8 * (QT * b + qt) + p
                for k in range(2):
                    h, n = 2 * p + k, 2 * s + k
                    wait(pool, s_made, n - 3)
                    nc.gpsimd.tensor_tensor(q_h[h % 4][:, :], q_t[:, h // 8, ds(qtile(b, qt), P)],
                                            head_rows[:, h % 8, :], ALU.mult).then_inc(qh_ready, 1)

            def mask(b, qt, p, k):
                W = (qt + 1) * P
                n = 2 * (8 * (QT * b + qt) + p) + k
                pool.wait_ge(exp_done, val(n + 1))
                pool.wait_ge(keep_ready, val(n + 1))
                wait(pool, prob_turned, n - 1)
                nc.gpsimd.tensor_tensor(prob[k][:, 0:W], S[(2 * p + k) % 8][:, 0:W], keep[k][:, 0:W],
                                        ALU.mult).then_inc(prob_ready, 1)

            def root(stat, signal, n, k):
                pool.wait_ge(stat, val(LN * n + 3))
                nc.gpsimd.tensor_tensor(var_e[k][:, :], mv[k][:, 1:2], eps[:, :], ALU.add).then_inc(signal, 1)
                pool.wait_ge(signal, val(2 * n + 1))
                nc.gpsimd.tensor_tensor(rstd[k][:, :], var_e[k][:, :], half[:, :], ALU.pow).then_inc(signal, 1)

            def flag(b, qt, p):
                s, r = 8 * (QT * b + qt) + p, p % 4
                pool.wait_ge(flag_made, val(s + 1))
                pool.sem_inc(pool_carried, 1)
                nc.gpsimd.tensor_reduce(far[0:1, r:r + 1], far_f[:, r:r + 1], mybir.AxisListType.C, ALU.max
                                        ).then_inc(flag_ready, 1)

            def add_bias(c):
                pool.wait_ge(g1_ln, val(LN * c + 4))
                nc.gpsimd.tensor_tensor(x1b[:, :], x1[:, :], b_o[:, :], ALU.add).then_inc(x1b_ready, 1)

            def experts_in(f, c, lo, hi):
                xt = x2_t0 if isinstance(c, int) and c == 0 else x2_t
                pool.wait_ge(f_bc, val(2 * f + 2))
                for e in range(lo, hi):
                    wait(pool, f_h, NE * f + e - 1)
                    nc.gpsimd.tensor_tensor(x_in[:, e % 2, :, :], xt[:, :, :],
                                            gate_b[:, e, :].unsqueeze(1).to_broadcast([P, NC, P]),
                                            ALU.mult).then_inc(f_xin, 1)

            def gated(f, lo):
                for e in range(lo, lo + 2):
                    pool.wait_ge(f_gelu, val(2 * (NE * f + e) + 2))
                    wait(pool, f_y, NE * f + e - 1)
                    nc.gpsimd.tensor_tensor(hid_g[e % 2][:, :, :], hid[e % 2][:, :, :],
                                            gate_b[:, e, :].unsqueeze(1).to_broadcast([P, NC, P]),
                                            ALU.mult).then_inc(f_hg, 1)

            def attention(kind, b, qt, p):
                if kind == "scores":
                    ahead = [(qt, 0)] if qt == 0 and p == 0 else []
                    if p < SLOTS - 1:
                        ahead.append((qt, p + 1))
                    elif qt < QT - 1:
                        ahead.append((qt + 1, 0))
                    return [(0, lambda: [heads_of(b, *q) for q in ahead])]
                if kind == "classify":
                    return [(4, lambda: flag(b, qt, p))]
                if kind == "keep":
                    return [(22, lambda: mask(b, qt, p, 0)), (22.1, lambda: mask(b, qt, p, 1))]
                return []

            def segment(i, c, f, b, qt):
                return {
                    2: [(0.5, lambda: root(g1_ln, rs1, c, 0)), (4.5, lambda: add_bias(c))],
                    5: [(0.5, lambda: root(g4_ln, rs4, c, 0))],
                    "gates": [(8.8, lambda: experts_in(f, c, 0, 2))],
                    8: [(0.7, lambda: gated(f, 0)), (0.8, lambda: experts_in(f, c, 2, 4))],
                    9: [(0.7, lambda: gated(f, 2)), (0.8, lambda: experts_in(f, c, 4, 6))],
                    10: [(0.7, lambda: gated(f, 4)), (0.8, lambda: experts_in(f, c, 6, NE))],
                    11: [(0.7, lambda: gated(f, 6))],
                    12: [(0.5, lambda: root(f_ln, rs7, f, 1))],
                }.get(i, [])

            timeline(pool, attention, segment, lambda: None)

        @block.scalar
        def _(act):
            for dst, src in ((w_k2, "w_k2"), (w_v2, "w_v2"), (w_o, "w_o"), (w_q2, "w_q2"), (w_o2, "w_o2"), (w_r, "w_r"),
                             (ctx_t, "ctx_t")):
                act.dma_start(dst[:, :, :], a[src].rearrange("(c p) n -> p c n", p=P)).then_inc(ld_rest, 16)
            for b in range(B):
                act.dma_start(ctx_t2[:, :, b, :], a["ctx_t2"].rearrange("(c p) n -> p c n", p=P)[:, :, b * 2 * CTX:(b + 1) * 2 * CTX]
                              ).then_inc(ld_rest, 16)
            for dst, src in ((b_q, "b_q"), (b_k, "b_k")):
                act.dma_start(dst[:, :], a[src]).then_inc(ld_rest, 16)
            act.dma_start(b_v[:, :], a["b_v"]).then_inc(ld_rest, 16)
            act.dma_start(b_o[:, :], a["b_o"].partition_broadcast(P)).then_inc(ld_rest, 16)
            act.dma_start(b_r[:, :], a["b_r"].partition_broadcast(P)).then_inc(ld_rest, 16)
            act.dma_start(w_1[:, :, :, :], a["w_1"].rearrange("e (c p) n -> p e c n", p=P)).then_inc(ld_exp, 16)
            act.dma_start(w_2[:, :, :, :], a["w_2"].rearrange("e (c p) n -> p e c n", p=P)).then_inc(ld_exp, 16)
            act.dma_start(b_1[:, :, :], a["b_1"]).then_inc(ld_exp, 16)
            act.dma_start(b_2[:, :], a["b_2"]).then_inc(ld_exp, 16)

            act.wait_ge(ld_rest, val(16 * N_REST))
            for g in range(NC):
                act.wait_ge(c_k2, NC)
                nc.scalar.activation(k2_t[:, g, :], psO[:, g * 256:(g + 1) * 256], ACT.Identity,
                                     bias=b_k[:, g:g + 1]).then_inc(c_k2t, 1)
            nc.scalar.activation(b_q4[:, :], b_q[:, :], ACT.Copy, scale=1.0 / HD ** 0.5).then_inc(init, 1)

            def kept(t, k):
                act.wait_ge(a_turn, val(t + 1))
                ps = psPU[:, k * 512:(k + 1) * 512].rearrange("p (c n) -> p c n", c=4)
                nc.scalar.activation(q_t[:, :, ds(t * P, P)], ps[:, 0:2, :], ACT.Copy,
                                     scale=1.0 / HD ** 0.5).then_inc(a_kept, 1)
                nc.scalar.activation(k_t[:, :, ds(t * P, P)], ps[:, 2:4, :], ACT.Copy).then_inc(a_kept, 1)

            def proj(t, k):
                act.wait_ge(a_proj, val(t + 1))
                wait(act, a_sel, SPREAD * (t - 1))
                nc.scalar.activation(raw[k][:, :], qkv_ps[k][:, 0:3 * D], ACT.Copy).then_inc(a_raw, 1)
                nc.scalar.activation(mag[k][:, :], qkv_ps[k][:, 0:3 * D], ACT.Abs).then_inc(a_raw, 1)

            proj(0, 0)
            proj(1, 1)
            kept(0, 0)
            with act.Fori(1, TILES // 2) as i:
                i = Linear(i)
                proj(2 * i, 0)
                kept(2 * i - 1, 1)
                proj(2 * i + 1, 1)
                kept(2 * i, 0)
            kept(TILES - 1, 1)

            def scores_out(b, qt, p, k):
                W = (qt + 1) * P
                h, n = 2 * p + k, 2 * (8 * (QT * b + qt) + p) + k
                two = 2 * W <= T
                act.wait_ge(s_made, val(n + 1 + two))
                wait(act, prob_ready, n - 7 + two)
                if two:
                    nc.scalar.activation(S_all[:, h % 8:h % 8 + 2, 0:W],
                                         psS.rearrange("p (k n) -> p k n", k=2)[:, :, 0:W], ACT.Copy
                                         ).then_inc(s_ready, 2)
                else:
                    nc.scalar.activation(S[h % 8][:, 0:W], psS[:, 0:W], ACT.Copy).then_inc(s_ready, 1)

            def counts(b, qt, p):
                W, s = (qt + 1) * P, 8 * (QT * b + qt) + p
                for k in range(2):
                    act.wait_ge(s_ready, val(2 * s + k + 1))
                    wait(act, counted, 4 * s - 1 + k)
                    nc.scalar.activation(signs[k][:, 0:W], S[(2 * p + k) % 8][:, 0:W], ACT.Sign,
                                         accum_out=balance[:, p % 4, k:k + 1]).then_inc(counted, 1)
                for k in range(2):
                    act.wait_ge(counted, val(4 * s + k + 1))
                    nc.scalar.activation(signs[k][:, 0:W], signs[k][:, 0:W], ACT.Abs,
                                         accum_out=filled[:, p % 4, k:k + 1]).then_inc(counted, 1)

            def compare(b, qt, p, k):
                W = (qt + 1) * P
                h, n = 2 * p + k, 2 * (8 * (QT * b + qt) + p) + k
                act.wait_ge(thresh_ready, val(8 * (QT * b + qt) + p + 1))
                wait(act, keep_ready, n - 3)
                nc.scalar.activation(over[h % 4][:, 0:W], S[h % 8][:, 0:W], ACT.Sign, scale=-1.0,
                                     bias=thresh[:, p % 4, k:k + 1], accum_out=balance1[:, p % 4, k:k + 1]
                                     ).then_inc(over_ready, 1)

            def turned_signs(b, qt, p):
                W, s = (qt + 1) * P, 8 * (QT * b + qt) + p
                for k in range(2):
                    act.wait_ge(flag_made, val(s + 1))
                    wait(act, thresh_ready, s - 1)
                    nc.scalar.activation(sided[(2 * p + k) % 4][:, 0:W], S[(2 * p + k) % 8][:, 0:W], ACT.Sign,
                                         scale=turn_to[:, p % 4, k:k + 1]).then_inc(sided_ready, 1)

            def exps(b, qt, p, k):
                W = (qt + 1) * P
                h, n = 2 * p + k, 2 * (8 * (QT * b + qt) + p) + k
                act.wait_ge(over_ready, val(n + 1))
                nc.scalar.activation(S[h % 8][:, 0:W], S[h % 8][:, 0:W], ACT.Exp,
                                     bias=neg_m[:, p % 4, k:k + 1]).then_inc(exp_done, 1)

            def turned_out(b, qt, p, k):
                W = (qt + 1) * P
                n = 2 * (8 * (QT * b + qt) + p) + k
                two = 2 * W <= T
                act.wait_ge(prob_turned, val(n + 1 + two))
                wait(act, pv_done, n - 1 + two)
                if two:
                    nc.scalar.activation(prob_t_all[:, :, 0:qt + 1, :],
                                         psP.rearrange("p (k c n) -> p k c n", k=2, n=P)[:, :, 0:qt + 1, :],
                                         ACT.Copy).then_inc(probt_ready, 2)
                else:
                    nc.scalar.activation(prob_t[k][:, 0:qt + 1, :],
                                         psP[:, 0:W].rearrange("p (c n) -> p c n", c=qt + 1),
                                         ACT.Copy).then_inc(probt_ready, 1)

            def out_of(made, count, dst, src, signal, func=ACT.Copy, **kw):
                act.wait_ge(made, val(count))
                nc.scalar.activation(dst, src, func, **kw).then_inc(signal, 1)

            def queries2(c):
                for g in range(NC):
                    out_of(g2_q, NC * c + NC, q2_t[:, g, :], y_ps[:, g * P:(g + 1) * P], g2_qt,
                           ACT.Identity, bias=b_q4[:, g:g + 1], scale=1.0 / HD ** 0.5)

            def gates_out(f):
                for j in range(2):
                    act.wait_ge(f_b, val(2 * f + 2))
                    wait(act, f_hg, NE * f)
                    nc.scalar.activation(gate_b[:, 4 * j:4 * j + 4, :],
                                         psC[:, j * 512:(j + 1) * 512].rearrange("p (e n) -> p e n", e=4), ACT.Copy
                                         ).then_inc(f_bc, 1)

            def gelus(f, lo):
                for e in range(lo, lo + 2):
                    act.wait_ge(f_h, val(NE * f + lo + 2))
                    wait(act, f_hg, NE * f + e - 1)
                    for g in range(NC):
                        nc.scalar.activation(hid[e % 2][:, g, :], up_ps[e % 2][:, g * P:(g + 1) * P],
                                             ACT.Gelu, bias=b_1[:, e, g:g + 1]).then_inc(f_gelu, 1)

            def attention(kind, b, qt, p):
                if kind == "scores":
                    return [(2, lambda: scores_out(b, qt, p, 0)), *([] if qt < 2 else [(4, lambda: scores_out(b, qt, p, 1))]),
                            (5.3, lambda: counts(b, qt, p))]
                if kind == "classify":
                    return [(5.4, lambda: turned_signs(b, qt, p))]
                if kind == "out":
                    return [(2.1, lambda: turned_out(b, qt, p, 0)),
                            *([] if qt < 2 else [(4.01, lambda: turned_out(b, qt, p, 1))])]
                if kind == "keep":
                    return [(1, lambda: compare(b, qt, p, 0)), (1.1, lambda: compare(b, qt, p, 1)),
                            (1.2, lambda: exps(b, qt, p, 0)), (1.3, lambda: exps(b, qt, p, 1))]
                return []

            def segment(i, c, f, b, qt):
                zero = isinstance(c, int) and c == 0
                return {
                    1: [(4.05, lambda: out_of(g1_turn, c + 1, heads_t[:, :, :], turn, g1_t))],
                    2: [(4.05, lambda: out_of(g2_turn, c + 1, x1_t[:, :, :], turn, g2_t)),
                        (4.7, lambda: queries2(c))],
                    3: [(4.02, lambda: out_of(g2_dve, 2 * c + 2, p2[:, :], p2[:, :], g3_exp, ACT.Exp)),
                        (6.5, lambda: out_of(g3_turn, c + 1, p2_t[:, :], psC[:, :], g3_t))],
                    4: [(4.05, lambda: out_of(g4_turn, c + 1, heads_t[:, :, :], turn, g4_t))],
                    5: [(4.05, lambda: out_of(g5_turn, c + 1, (x2_t0 if zero else x2_t)[:, :, :], turn, g5_t))],
                    6: [(1.5, lambda: out_of(g5_dve, ROUTE * c + 3, l_exp[:, :], logit[:, :], g5_exp, ACT.Exp))],
                    "gates": [(8.7, lambda: out_of(f_turn, f + 1, gate_t[:, :], psB[0:NE, 0:P], f_t)),
                              (8.9, lambda: gates_out(f))],
                    7: [(6, lambda: gelus(f, 0))],
                    8: [(6, lambda: gelus(f, 2))],
                    9: [(6, lambda: gelus(f, 4))],
                    10: [(6, lambda: gelus(f, 6))],
                }.get(i, [])

            act.wait_ge(ld_exp, val(16 * 4))
            timeline(act, attention, segment, lambda: None)

        @block.tensor
        def _(pe):
            def proj(t, k, i):
                pe.wait_ge(ld_xt[k], val(16 * (i + 1)))
                wait(pe, a_raw, 2 * (t - 1))
                for lo, hi in ((0, 2 * D), (2 * D, 3 * D)):
                    for c in range(NC):
                        mm = nc.tensor.matmul(qkv_ps[k][:, lo:hi], x_t[k][:, c, :], w_qkv[:, c, lo:hi],
                                              start=(c == 0), stop=(c == NC - 1))
                mm.then_inc(a_proj, 1)

            def turn_qk(t, k):
                pe.wait_ge(a_sel, val(SPREAD * (t + 1)))
                wait(pe, a_kept, 2 * (t - 1))
                for j in range(4):
                    mm = nc.tensor.transpose(psPU[:, k * 512 + j * P:k * 512 + (j + 1) * P],
                                             qk_s[k][:, j * P:(j + 1) * P], ident[:, :])
                mm.then_inc(a_turn, 1)

            pe.wait_ge(ld_proj, 16)
            proj(0, 0, 0)
            proj(1, 1, 0)
            pe.wait_ge(ld_rest, val(16 * N_REST))
            pe.wait_ge(ld_const, val(16 * N_CONST))
            for g in range(NC):
                for c in range(NC):
                    mm = nc.tensor.matmul(psO[:, g * 256:(g + 1) * 256], w_k2[:, c, g * P:(g + 1) * P], ctx_t[:, c, :],
                                          start=(c == 0), stop=(c == NC - 1))
                mm.then_inc(c_k2, 1)
            for b in range(B):
                wait(pe, c_v2c, 2 * b)
                for c in range(NC):
                    nc.tensor.matmul(psB[:, 0:D], ctx_t2[:, c, b, :], w_v2[:, c, :], start=(c == 0), stop=False)
                nc.tensor.matmul(psB[:, 0:D], head_rows[0:1, 0, :], b_v[:, :], start=False, stop=True).then_inc(c_v2, 1)
            turn_qk(0, 0)
            with pe.Fori(1, TILES // 2) as i:
                i = Linear(i)
                proj(2 * i, 0, i)
                turn_qk(2 * i - 1, 1)
                proj(2 * i + 1, 1, i)
                turn_qk(2 * i, 0)
            turn_qk(TILES - 1, 1)
            pe.wait_ge(a_kept, val(2 * TILES))
            pe.wait_ge(c_k2t, val(NC))
            pe.wait_ge(c_bd, val(B * NC))
            pe.wait_ge(c_v2c, val(2 * B))

            def scores(b, qt, p, k):
                W = (qt + 1) * P
                h, n = 2 * p + k, 2 * (8 * (QT * b + qt) + p) + k
                two = 2 * W <= T
                pe.wait_ge(qh_ready, val(n + 1))
                wait(pe, s_ready, n - k if two else n)
                col = k * 256 if two else 0
                out = psS[:, col:col + W]
                nc.tensor.matmul(out, q_h[h % 4][:, :], k_t[:, h // 8, ds(b * T, W)], start=True, stop=False)
                nc.tensor.matmul(out[:, W - P:W], ident_h[:, :], causal_h[:, :], start=False, stop=True
                                 ).then_inc(s_made, 1)

            def turn_probs(b, qt, p, k):
                n = 2 * (8 * (QT * b + qt) + p) + k
                two = 2 * (qt + 1) * P <= T
                pe.wait_ge(prob_ready, val(n + 1))
                wait(pe, probt_ready, n - k if two else n)
                col = k * 256 if two else 0
                for j in range(qt + 1):
                    mm = nc.tensor.transpose(psP[:, col + j * P:col + (j + 1) * P],
                                             prob[k][:, j * P:(j + 1) * P], ident[:, :])
                mm.then_inc(prob_turned, 1)

            def values(b, qt, p, k):
                h, n = 2 * p + k, 2 * (8 * (QT * b + qt) + p) + k
                if h == 0:
                    wait(pe, g0, 2 * (QT * b + qt))
                pe.wait_ge(probt_ready, val(n + 1))
                for j in range(qt + 1):
                    mm = nc.tensor.matmul(psO[:, h * VW:(h + 1) * VW], prob_t[k][:, j, :],
                                          v_s[:, ds(QT * b + j, 1), h, :].rearrange("p t v -> p (t v)"),
                                          start=(j == 0), stop=(j == qt))
                mm.then_inc(pv_done, 1)

            def turned(ready, count, src, signal):
                pe.wait_ge(ready, val(count))
                for g in range(NC):
                    mm = nc.tensor.transpose(turn[:, g, :], src[:, g * P:(g + 1) * P], ident[:, :])
                mm.then_inc(signal, 1)

            def by_rows(ready, count, xt, w, signal, out):
                pe.wait_ge(ready, val(count))
                for c in range(NC):
                    mm = nc.tensor.matmul(out, xt[:, c, :], w[:, c, :], start=(c == 0), stop=(c == NC - 1))
                mm.then_inc(signal, 1)

            def queries2(c):
                pe.wait_ge(g2_t, val(c + 1))
                for g in range(NC):
                    for cc in range(NC):
                        mm = nc.tensor.matmul(y_ps[:, g * P:(g + 1) * P], w_q2[:, cc, g * P:(g + 1) * P],
                                              x1_t[:, cc, :], start=(cc == 0), stop=(cc == NC - 1))
                    mm.then_inc(g2_q, 1)

            def scores2(c, b):
                pe.wait_ge(g2_qt, val(NC * c + 2))
                wait(pe, f_bc, 2 * (c - 1))
                for g in range(NC):
                    mm = nc.tensor.matmul(psC[:, g * 512:(g + 1) * 512], q2_t[:, g, :],
                                          k2_bd[:, ds(b, 1), g, :, :].rearrange("p b h n -> p (b h n)"),
                                          start=True, stop=True)
                mm.then_inc(g2_s, 1)

            def turn_p2(c):
                pe.wait_ge(g3_exp, val(c + 1))
                for j in range(8):
                    mm = nc.tensor.transpose(psC[:, j * P:(j + 1) * P], p2[:, j * P:(j + 1) * P], ident[:, :])
                mm.then_inc(g3_turn, 1)

            def values2(c, b):
                pe.wait_ge(g3_t, val(c + 1))
                for j in range(8):
                    mm = nc.tensor.matmul(psC[:, j * 2 * VW:(j + 1) * 2 * VW], p2_t[:, j * P:(j + 1) * P],
                                          v2_bd[:, ds(b, 1), j, :].rearrange("p b n -> p (b n)"),
                                          start=True, stop=True)
                mm.then_inc(g3_o, 1)

            def turn_gates(f, c):
                zero = isinstance(c, int) and c == 0
                if not zero:
                    pe.wait_ge(g5_dve, val(ROUTE * (c + 1)))
                nc.tensor.transpose(psB[0:NE, 0:P], (gate_0 if zero else gate)[:, :], ident[:, :]).then_inc(f_turn, 1)

            def spread_gates(f):
                pe.wait_ge(f_t, val(f + 1))
                for e in range(NE):
                    mm = nc.tensor.matmul(psC[:, e * P:(e + 1) * P], pick_row[:, e, :], gate_t[:, :],
                                          start=True, stop=True)
                    if e % 4 == 3:
                        mm.then_inc(f_b, 1)

            def up(f, lo):
                wait(pe, f_gelu, 2 * (NE * f + lo))
                for e in range(lo, lo + 2):
                    pe.wait_ge(f_xin, val(NE * f + e + 1))
                    for g in range(NC):
                        for c in range(NC):
                            mm = nc.tensor.matmul(up_ps[e % 2][:, g * P:(g + 1) * P],
                                                  w_1[:, e, c, g * P:(g + 1) * P], x_in[:, e % 2, c, :],
                                                  start=(c == 0), stop=(c == NC - 1))
                    mm.then_inc(f_h, 1)

            def down(f, lo):
                if lo == 0:
                    wait(pe, f_ln, LN * (f - 1) + 1 if not isinstance(f, int) or f > 0 else 0)
                    nc.tensor.matmul(psF, gate_t[:, :], b_2[:, :], start=True, stop=False)
                for e in range(lo, lo + 2):
                    pe.wait_ge(f_hg, val(NE * f + e + 1))
                    for c in range(NC):
                        mm = nc.tensor.matmul(psF, hid_g[e % 2][:, c, :], w_2[:, e, c, :],
                                              start=False, stop=(e == NE - 1 and c == NC - 1))
                    mm.then_inc(f_y, 1)

            def attention(kind, b, qt, p):
                if kind == "scores":
                    return [(1, lambda: scores(b, qt, p, 0)), (1.1 if qt < 2 else 3, lambda: scores(b, qt, p, 1))]
                if kind == "out":
                    return [(1.2, lambda: turn_probs(b, qt, p, 0)), (1.25 if qt < 2 else 3.1, lambda: turn_probs(b, qt, p, 1)),
                            (7, lambda: values(b, qt, p, 0)), (7.1, lambda: values(b, qt, p, 1))]
                return []

            def segment(i, c, f, b, qt):
                zero = isinstance(c, int) and c == 0
                return {
                    1: [(3.5, lambda: turned(g0, 2 * c + 2, heads_o, g1_turn)),
                        (4.5, lambda: by_rows(g1_t, c + 1, heads_t, w_o, g1_y, y_ps))],
                    2: [(3.5, lambda: turned(g1_ln, LN * c + 4, x1, g2_turn)), (4.5, lambda: queries2(c)),
                        (8.5, lambda: scores2(c, b))],
                    3: [(5.7, lambda: turn_p2(c)), (8.5, lambda: values2(c, b))],
                    4: [(3.5, lambda: turned(g3_dve, 2 * c + 2, heads_o, g4_turn)),
                        (4.5, lambda: by_rows(g4_t, c + 1, heads_t, w_o2, g4_y, y_ps))],
                    5: [(3.5, lambda: turned(g4_ln, LN * c + 4, x2_0 if zero else x2, g5_turn)),
                        (4.5, lambda: by_rows(g5_t, c + 1, x2_t0 if zero else x2_t, w_r, g5_l, y_ps[:, 0:NE]))],
                    "gates": [(8.6, lambda: turn_gates(f, c)), (8.8, lambda: spread_gates(f))],
                    7: [(5.5, lambda: up(f, 0))],
                    8: [(5.5, lambda: up(f, 2)), (5.6, lambda: down(f, 0))],
                    9: [(5.5, lambda: up(f, 4)), (5.6, lambda: down(f, 2))],
                    10: [(5.5, lambda: up(f, 6)), (5.6, lambda: down(f, 4))],
                    11: [(5.6, lambda: down(f, 6))],
                }.get(i, [])

            def last():
                pe.wait_ge(z_sum, 1)
                for k in range(2):
                    mm = nc.tensor.matmul(psO[0:NE, k:k + 1], gates_sum[:, k, :], ones[:, 0:1], start=True, stop=True)
                mm.then_inc(z_ps, 1)
                pe.wait_ge(z_gate, 2)

            timeline(pe, attention, segment, last)

        @block.vector
        def _(dve):
            def settle():
                dve.sem_inc(carried, 1)

            nc.vector.memset(v2_bd[:, :, :, :], 0.0).then_inc(init, 1)
            nc.vector.memset(v_s[:, :, :, HD:VW], 1.0).then_inc(init, 1)
            dve.wait_ge(init, 3)
            nc.vector.memset(v2_bd[0:64, :, :, HD:VW], 1.0).then_inc(init, 1)
            nc.vector.memset(v2_bd[64:128, :, :, VW + HD:2 * VW], 1.0).then_inc(init, 1)
            dve.wait_ge(ld_const, val(16 * N_CONST))

            def grouped(t):
                return t[:, :].rearrange("p (h j) -> p h j", j=HD)

            def spread(t):
                return t[:, :].unsqueeze(2).to_broadcast([P, 3 * NH, HD])

            def sparsify(t, k):
                chain = link(dve, a_dve, SPARSE * t)
                dve.wait_ge(a_raw, val(2 * (t + 1)))

                def first_largest(top):
                    dve_in = grouped(mag[k])
                    chain(nc.vector.tensor_reduce(grp_f[:, :], dve_in, X, ALU.max))
                    chain.caught_up()
                    chain(nc.vector.tensor_tensor(grouped(hit), dve_in, spread(grp_f), ALU.is_equal))
                    chain.caught_up()
                    chain(nc.vector.tensor_tensor_scan(nth[:, :], same_head[:, :], hit[:, :], 0.0, ALU.mult, ALU.add))
                    chain.caught_up()
                    wait(dve, a_sel, SPREAD * (t - 1) + 1)
                    chain(nc.vector.scalar_tensor_tensor(out=top[:, :], in0=nth[:, :], scalar=1.0, in1=hit[:, :],
                                                        op0=ALU.is_equal, op1=ALU.mult))
                    chain.caught_up()

                first_largest(top1)
                chain(nc.vector.scalar_tensor_tensor(out=mag[k][:, :], in0=top1[:, :], scalar=NEG, in1=mag[k][:, :],
                                                    op0=ALU.mult, op1=ALU.add))
                chain.caught_up()
                first_largest(top2)
                assert chain.n[0] == SPARSE

            sparsify(0, 0)
            dve.wait_ge(init, 5)
            for b in range(B):
                dve.wait_ge(c_v2, val(b + 1))
                for j in range(2):
                    src = psB[64 * j:64 * j + 64, 0:D].rearrange("p (m j n) -> p m j n", j=2, n=HD)[:, :, j, :]
                    nc.vector.tensor_copy(v2_bd[64 * j:64 * j + 64, b, :, j * VW:j * VW + HD], src).then_inc(c_v2c, 1)
            sparsify(1, 1)
            with dve.Fori(1, TILES // 2) as i:
                i = Linear(i)
                sparsify(2 * i, 0)
                sparsify(2 * i + 1, 1)

            at = [0]

            def fresh():
                if at[0]:
                    dve.wait_ge(step, at[0])
                    dve.sem_clear(step)
                at[0] = 0

            def then(ins):
                ins.then_inc(step, 1)
                at[0] += 1
                return at[0]

            def after(number):
                dve.wait_ge(step, number)

            def classify(b, qt, p):
                W, s, r, v, n = (qt + 1) * P, 8 * (QT * b + qt) + p, p % 4, nc.vector, {}

                def ranks_1():
                    dve.wait_ge(counted, val(4 * s + 4))
                    n["pos"] = then(v.tensor_tensor(r_pos[:, :], balance[:, r, :], filled[:, r, :], ALU.add))
                    n["neg"] = then(v.tensor_tensor(r_neg[:, :], filled[:, r, :], balance[:, r, :], ALU.subtract))

                def largest(k):
                    wait(dve, exp_done, 2 * (s - 4) + 2)
                    n["max"] = then(v.tensor_reduce(neg_m[:, r, k:k + 1], S[(2 * p + k) % 8][:, 0:W], X, ALU.max, negate=True))

                def side():
                    after(n["pos"])
                    n["pos"] = then(v.tensor_scalar(r_pos[:, :], r_pos[:, :], 0.5, float(1 - KEEP), ALU.mult, ALU.add))
                    after(n["neg"])
                    n["neg"] = then(v.tensor_scalar(r_neg[:, :], r_neg[:, :], 0.5, float(KEEP - W), ALU.mult, ALU.add))

                def late_rows():
                    after(n["neg"])
                    n["neg"] = then(v.tensor_scalar(r_neg[:, :], r_neg[:, :], late[:, 0:1], None, ALU.mult))

                def nearer():
                    after(n["pos"])
                    n["spare"] = then(v.tensor_scalar(spare[:, :], r_pos[:, :], 0.0, -2.0, ALU.is_gt, ALU.mult))
                    after(n["neg"])
                    n["ranks"] = then(v.tensor_tensor(ranks[:, r, :], r_pos[:, :], r_neg[:, :], ALU.max))

                def furthest():
                    after(n["spare"])
                    then(v.tensor_scalar(turn_to[:, r, :], spare[:, :], 1.0, None, ALU.add))
                    after(n["ranks"])
                    wait(dve, flag_ready, s - 3)
                    v.tensor_reduce(far_f[:, r:r + 1], ranks[:, r, :], X, ALU.max).then_inc(flag_made, 1)

                return [(2.1, ranks_1), (2.2, lambda: largest(0)), (2.3, side),
                        *([(2.35, late_rows)] if qt == 0 else []), (2.4, lambda: largest(1)), (2.5, nearer), (2.7, furthest)]

            def keep_first(b, qt, p):
                W, s, r, v, n = (qt + 1) * P, 8 * (QT * b + qt) + p, p % 4, nc.vector, {}
                o = [over[(2 * p + k) % 4] for k in range(2)]

                def ties():
                    for k in range(2):
                        dve.wait_ge(over_ready, val(2 * s + k + 1))
                        n[k] = then(v.tensor_scalar(mark[k][:, 0:W], o[k][:, 0:W], 0.0, None, ALU.is_equal))

                def running():
                    for k in range(2):
                        after(n[k])
                        n[k] = then(v.tensor_tensor_scan(count[:, k, 0:W], mark[k][:, 0:W], mark[k][:, 0:W],
                                                         0.0, ALU.add, ALU.max))

                def left():
                    after(n[1])
                    n["wanted"] = then(v.tensor_tensor(wanted[:, :], count[:, :, W - 1], balance1[:, r, :], ALU.add))

                def left_half():
                    after(n["wanted"])
                    n["wanted"] = then(v.tensor_scalar(wanted[:, :], wanted[:, :], 0.5, float(KEEP - W / 2), ALU.mult, ALU.add))

                def kept():
                    after(n["wanted"])
                    for k in range(2):
                        wait(dve, prob_ready, 2 * s + k - 1)
                        v.scalar_tensor_tensor(out=keep[k][:, 0:W], in0=count[:, k, 0:W], scalar=wanted[:, k:k + 1],
                                               in1=o[k][:, 0:W], op0=ALU.is_le, op1=ALU.is_gt).then_inc(keep_ready, 1)

                return [(5.1, ties), (5.2, running), (5.3, left), (5.4, left_half), (5.5, kept)]

            def select(b, qt, p):
                W, s, r, v, n = (qt + 1) * P, 8 * (QT * b + qt) + p, p % 4, nc.vector, {}
                two = (P, 2, 8)

                def load():
                    dve.wait_ge(flag_ready, val(s + 1))
                    settle()
                    n["furthest"] = dve.value_load(far[0:1, r:r + 1], min_val=-T, max_val=T)
                    n["found"] = then(v.memset(found[:, :, :], 0.0))
                    n["dist"] = then(v.tensor_tensor(dist[:, :, :], iota8[:, :].unsqueeze(1).to_broadcast(two),
                                                     ranks[:, r, :].unsqueeze(2).to_broadcast(two), ALU.subtract))

                def one_round(first):
                    for k in range(2):
                        v.max(eight[:, k, :], y[k][:, 0:W]).then_inc(picked, 1)
                    dve.wait_ge(picked, 1)
                    v.match_replace(y[0][:, 0:W], eight[:, 0, :], y[0][:, 0:W], GONE).then_inc(picked, 1)
                    if not first:
                        dve.wait_ge(noted, NOTES)
                        dve.sem_clear(noted)
                    dve.wait_ge(picked, 2)
                    v.scalar_tensor_tensor(out=hit8[:, :, :], in0=dist[:, :, :], scalar=0.0,
                                           in1=eight[:, :, :], op0=ALU.is_equal, op1=ALU.mult).then_inc(noted, 1)
                    v.match_replace(y[1][:, 0:W], eight[:, 1, :], y[1][:, 0:W], GONE).then_inc(picked, 1)
                    dve.wait_ge(noted, 1)
                    v.tensor_tensor(found[:, :, :], found[:, :, :], hit8[:, :, :], ALU.add).then_inc(noted, 1)
                    v.tensor_scalar(dist[:, :, :], dist[:, :, :], 8.0, None, ALU.add).then_inc(noted, 1)
                    dve.wait_ge(picked, 4)
                    dve.sem_clear(picked)

                def rounds():
                    after(at[0])
                    with dve.If(n["furthest"] > 0):
                        for k in range(2):
                            dve.wait_ge(sided_ready, val(2 * s + k + 1))
                            v.tensor_scalar(mark[k][:, 0:W], sided[(2 * p + k) % 4][:, 0:W], 0.0, -BIG, ALU.is_ge, ALU.mult
                                            ).then_inc(picked, 1)
                        wait(dve, keep_ready, 2 * (s - 1))
                        for k in range(2):
                            dve.wait_ge(picked, k + 1)
                            v.scalar_tensor_tensor(out=y[k][:, 0:W], in0=S[(2 * p + k) % 8][:, 0:W],
                                                   scalar=turn_to[:, r, k:k + 1], in1=mark[k][:, 0:W],
                                                   op0=ALU.mult, op1=ALU.add).then_inc(picked, 1)
                        dve.wait_ge(picked, 4)
                        dve.sem_clear(picked)
                        one_round(first=True)
                        with dve.Fori(8, n["furthest"], 8):
                            one_round(first=False)
                        dve.wait_ge(noted, NOTES)
                        dve.sem_clear(noted)
                    dve.end_ifs()
                    after(then(v.tensor_reduce(thresh[:, r, :], found[:, :, :], X, ALU.add)))
                    last_step = v.tensor_tensor(thresh[:, r, :], thresh[:, r, :], turn_to[:, r, :], ALU.mult)
                    if qt == 0:
                        after(then(last_step))
                        last_step = v.tensor_scalar(thresh[:, r, :], thresh[:, r, :], drop[:, 0:1], None, ALU.add)
                    last_step.then_inc(thresh_ready, 1)

                return [(0, load), (4.8, rounds)]

            def norm_1(c, signal, y, ready, x_in_, sum_, j, extra=None):
                chain = link(dve, signal, LN * c)
                dve.wait_ge(ready[0], val(ready[1]))
                if extra:
                    dve.wait_ge(extra[0], val(extra[1]))
                chain(nc.vector.tensor_tensor(sum_[:, :], y, x_in_, ALU.add))
                chain.caught_up()
                chain(nc.vector.bn_stats(stats[j][:, :], sum_[:, :]))
                chain.caught_up()
                settle()
                chain(nc.vector.bn_aggr(mv[j][:, :], stats[j][:, :]))

            def norm_2(c, signal, rs, sum_, j, out):
                dve.wait_ge(rs, val(2 * c + 2))
                nc.vector.tensor_scalar(out, sum_[:, :], mv[j][:, 0:1], rstd[j][:, 0:1], ALU.subtract, ALU.mult
                                        ).then_inc(signal, 1)

            def normed_heads(c, signal, ready, ps):
                dve.wait_ge(ready[0], val(ready[1]))
                nc.vector.reciprocal(den[:, :], ps[:, :, HD]).then_inc(signal, 1)
                dve.wait_ge(signal, val(2 * c + 1))
                nc.vector.tensor_tensor(heads_o[:, :].rearrange("p (h j) -> p h j", j=HD), ps[:, :, 0:HD],
                                        den[:, :].unsqueeze(2).to_broadcast([P, NH, HD]), ALU.mult
                                        ).then_inc(signal, 1)

            def route_1(c):
                chain = link(dve, g5_dve, ROUTE * c)
                v = nc.vector
                dve.wait_ge(g5_l, val(c + 1))
                chain(v.tensor_tensor(logit[:, :], y_ps[:, 0:NE], b_r[:, :], ALU.add))
                chain.caught_up()
                chain(v.tensor_reduce(l_max[:, :], logit[:, :], X, ALU.max))
                chain.caught_up()
                chain(v.tensor_scalar(logit[:, :], logit[:, :], l_max[:, 0:1], None, ALU.subtract))

            def route_2(c, gt):
                chain = link(dve, g5_dve, ROUTE * c + 3)
                v = nc.vector
                dve.wait_ge(g5_exp, val(c + 1))
                e_j = l_exp[:, :].unsqueeze(1).to_broadcast([P, NE, NE])
                e_i = l_exp[:, :].unsqueeze(2).to_broadcast([P, NE, NE])
                chain(v.tensor_tensor(above[:, :, :], e_j, e_i, ALU.is_gt))
                chain(v.tensor_tensor(tied[:, :, :], e_j, e_i, ALU.is_equal))
                chain.caught_up()
                chain(v.tensor_tensor(tied[:, :, :], tied[:, :, :], earlier[:, :, :], ALU.mult))
                chain.caught_up()
                chain(v.tensor_tensor(above[:, :, :], above[:, :, :], tied[:, :, :], ALU.add))
                chain.caught_up()
                chain(v.tensor_reduce(rank[:, :], above[:, :, :], X, ALU.add))
                chain.caught_up()
                for k in range(2):
                    chain(v.scalar_tensor_tensor(out=chosen[:, k, :], in0=rank[:, :], scalar=float(k), in1=l_exp[:, :],
                                                op0=ALU.is_equal, op1=ALU.mult))
                chain.caught_up()
                chain(v.tensor_tensor(both[:, :], chosen[:, 0, :], chosen[:, 1, :], ALU.add))
                chain.caught_up()
                chain(v.tensor_reduce(l_sum[:, :], both[:, :], X, ALU.add))
                chain.caught_up()
                chain(v.reciprocal(l_rec[:, :], l_sum[:, :]))
                chain.caught_up()
                v.tensor_scalar(gates[:, ds(c, 1), :].rearrange("p t e -> p (t e)"),
                                chosen[:, :, :].rearrange("p k e -> p (k e)"), l_rec[:, 0:1], None, ALU.mult)
                chain(v.tensor_scalar(gt[:, :], both[:, :], l_rec[:, 0:1], CAPACITY, ALU.mult, ALU.min))
                assert chain.n[0] + 3 == ROUTE

            def softmax2(c):
                v = nc.vector
                ps = psC[:, :].rearrange("p (h n) -> p h n", n=CTX)
                dve.wait_ge(g2_s, val(c + 1))
                v.tensor_reduce(m2[:, :], ps, X, ALU.max).then_inc(g2_dve, 1)
                dve.wait_ge(g2_dve, val(2 * c + 1))
                v.tensor_tensor(p2[:, :].rearrange("p (h n) -> p h n", n=CTX), ps,
                                m2[:, :].unsqueeze(2).to_broadcast([P, NH, CTX]), ALU.subtract
                                ).then_inc(g2_dve, 1)

            def by_heads(ps):
                return ps[:, 0:NH * VW].rearrange("p (h j) -> p h j", j=VW)

            def stored(f):
                if not isinstance(f, int) or f > 0:
                    dve.wait_ge(out_done, val(16 * f))

            def attention(kind, b, qt, p):
                work = {"classify": classify, "select": select, "keep": keep_first}
                return work[kind](b, qt, p) if kind in work else []

            def segment(i, c, f, b, qt):
                zero = isinstance(c, int) and c == 0
                k = qt % 2
                x2_c = x2_0 if zero else x2
                return {
                    1: [(2.9, lambda: normed_heads(c, g0, (pv_done, NH * (c + 1)), by_heads(psO)))],
                    2: [(2.05, lambda: norm_1(c, g1_ln, y_ps, (g1_y, c + 1), x_rows[k][:, :], res, 0,
                                              (ld_xr[k], 16 * (QT // 2 * b + qt // 2 + 1)))),
                        (2.95, lambda: norm_2(c, g1_ln, rs1, res, 0, x1[:, :]))],
                    3: [(2.9, lambda: softmax2(c))],
                    4: [(2.9, lambda: normed_heads(c, g3_dve, (g3_o, c + 1), by_heads(psC)))],
                    5: [(2.05, lambda: norm_1(c, g4_ln, y_ps, (g4_y, c + 1), x1b[:, :], res, 0, (x1b_ready, c + 1))),
                        (2.95, lambda: norm_2(c, g4_ln, rs4, res, 0, x2_c[:, :]))],
                    6: [(2.04, lambda: route_1(c)), (2.98, lambda: route_2(c, gate_0 if zero else gate))],
                    12: [(2.05, lambda: stored(f)),
                         (2.06, lambda: norm_1(f, f_ln, psF, (f_y, NE * (f + 1)), x2_c[:, :], fin, 1)),
                         (2.95, lambda: norm_2(f, f_ln, rs7, fin, 1, fin[:, :]))],
                }.get(i, [])

            def last():
                v = nc.vector
                dve.wait_ge(g5_dve, val(ROUTE * TILES))
                v.tensor_reduce(gates_sum[:, :, :].rearrange("p k e -> p (k e)"),
                                gates[:, :, :].rearrange("p t e -> p e t"), X, ALU.add).then_inc(z_sum, 1)
                dve.wait_ge(z_ps, 1)
                v.tensor_tensor(gate_0[0:NE, 0:2], gate_0[0:NE, 0:2], psO[0:NE, 0:2], ALU.add).then_inc(z_gate, 1)
                dve.wait_ge(z_gate, 1)
                v.tensor_scalar(gate_0[:, :], gate_0[:, :], CAPACITY, None, ALU.min).then_inc(z_gate, 1)

            dve.wait_ge(ld_rest, val(16 * N_REST))
            timeline(dve, attention, segment, last, lambda p: [(-1, fresh)])


def host_constants():
    bf = mybir.dt.np(BF16)
    i = np.arange(P)
    c = {}
    c["ident"] = np.eye(P, dtype=np.float32)
    c["ident_h"] = np.eye(P, dtype=np.float32).astype(bf)
    c["causal_h"] = np.where(i[None, :] > i[:, None], NEG, 0.0).astype(np.float32).astype(bf)
    c["head_rows"] = np.repeat((i[:, None] // HD == np.arange(8)[None, :]).astype(np.float32)[:, :, None], P, axis=2)
    c["same_head"] = np.repeat((np.arange(3 * D) % HD != 0).astype(np.float32)[None, :], P, axis=0).astype(bf)
    e = np.arange(NE)
    c["earlier"] = np.repeat((e[None, None, :] < e[None, :, None]).astype(np.float32), P, axis=0)
    c["pick_row"] = np.repeat((e[:, None] == e[None, :]).astype(np.float32)[:, :, None], P, axis=2)
    c["ones"] = np.ones((P, 1), np.float32)
    c["eps"] = np.full((P, 1), EPS, np.float32)
    c["late"] = (i[:, None] >= KEEP).astype(np.float32)
    c["drop"] = np.where(i[:, None] < KEEP, BELOW, 0.0).astype(np.float32)
    c["iota8"] = np.repeat(np.arange(1, 9, dtype=np.float32)[None, :], P, axis=0)
    c["half"] = np.full((P, 1), -0.5, np.float32)
    return c


def kernel(**inputs):
    import concourse.bacc as bacc
    from concourse.bass_utils import run_bass_kernel_spmd

    i = {k: np.asarray(v) for k, v in inputs.items()}
    arrays = host_constants()
    x = i["x"].reshape(B * T, D)
    arrays["x"] = x
    arrays["x_t"] = x.T
    arrays["w_qkv"] = np.concatenate([i["L0_attn_wq"].T, i["L0_attn_wk"].T, i["L0_attn_wv"].T], axis=1)
    arrays["w_o"] = i["L0_attn_wo"].T
    for n in "qkvo":
        arrays[f"w_{n}2"] = i[f"L0_xattn_w{n}"].T
    arrays["b_q"] = i["L0_xattn_bq"].reshape(NC, P).T
    arrays["b_k"] = i["L0_xattn_bk"].reshape(NC, P).T
    arrays["b_v"] = i["L0_xattn_bv"].reshape(1, D)
    arrays["b_o"] = i["L0_xattn_bo"]
    c = i["ctx_1024"].reshape(B, CTX, D)
    arrays["ctx_t"] = c.reshape(B * CTX, D).T
    arrays["ctx_t2"] = np.concatenate([c, c], axis=1).reshape(B * 2 * CTX, D).T
    arrays["w_r"] = i["L0_ffn_router_w"]
    arrays["b_r"] = i["L0_ffn_router_b"]
    arrays["w_1"] = i["L0_ffn_w1"]
    arrays["b_1"] = i["L0_ffn_b1"].reshape(NE, NC, P).transpose(2, 0, 1)
    arrays["w_2"] = i["L0_ffn_w2"]
    arrays["b_2"] = i["L0_ffn_b2"]
    arrays = {k: np.ascontiguousarray(v) for k, v in arrays.items()}

    nc = bacc.Bacc("TRN2", target_bir_lowering=False, num_devices=1)
    aps = {k: nc.dram_tensor(f"in_{k}", v.shape, mybir.dt.from_np(v.dtype), kind="ExternalInput").ap()
           for k, v in arrays.items()}
    aps["out"] = nc.dram_tensor("out_0", (B * T, D), F32, kind="ExternalOutput").ap()
    build(nc, aps)
    r = run_bass_kernel_spmd(nc, [{f"in_{k}": v for k, v in arrays.items()}], core_ids=[0])
    return r.results[0]["out_0"].reshape(B, T, D)
```

```python
from contextlib import ExitStack

import concourse.bass as bass
from concourse import mybir
from concourse.alu_op_type import AluOpType as ALU
import numpy as np

F32 = mybir.dt.float32
BF16 = mybir.dt.bfloat16
ACT = mybir.ActivationFunctionType
X = mybir.AxisListType.X


def ds(start, size):
    return bass.ds(val(start), size)

P = 128
B, T, D = 4, 512, 256
NH, HD = 16, 16
NC = D // P
QT = T // P
TILES = B * QT
KEEP = 64
ROUNDS = KEEP // 8
CTX = 64
NE, FH = 8, 256
CAPACITY = float(max(int(B * T * 1.25 / NE), 4))
EPS = 1e-5
NEG = -1.0e30
BELOW = -2.0e30
BIG = 2.0 ** 101
GONE = -3.0e38
SLOTS = NH // 2
VW = HD + 1
BY_VECTOR = (1, 2)
SPARSE = 9
SPREAD = 3
NOTES = 3
ROUTE = 14
LN = 4
FIRST = NE
TWICE = 2
SEGMENTS = 13


class Linear:
    def __init__(self, reg, times=1, plus=0):
        self.reg, self.times, self.plus = reg, times, plus

    def __add__(self, n):
        return Linear(self.reg, self.times, self.plus + n)

    def __sub__(self, n):
        return self + -n

    def __mul__(self, n):
        return Linear(self.reg, self.times * n, self.plus * n)

    __radd__, __rmul__ = __add__, __mul__


def val(n):
    if not isinstance(n, Linear):
        return n
    scaled = n.reg * n.times if n.times != 1 else n.reg
    return scaled + n.plus if n.plus else scaled


def wait(eng, sem, value):
    if isinstance(value, Linear) or value > 0:
        eng.wait_ge(sem, val(value))


def build(nc, a):
    nc.disable_value_cache = True
    with ExitStack() as ctx:
        def sb(name, shape, dt=F32):
            return ctx.enter_context(nc.sbuf_tensor(name, shape, dt))

        def sem(name):
            return ctx.enter_context(nc.semaphore(name))

        w_o = sb("w_o", [P, NC, D])
        w_q2 = sb("w_q2", [P, NC, D])
        w_k2 = sb("w_k2", [P, NC, D])
        w_v2 = sb("w_v2", [P, NC, D])
        w_o2 = sb("w_o2", [P, NC, D])
        w_r = sb("w_r", [P, NC, NE])
        w_1 = sb("w_1", [P, NE, NC, FH])
        w_2 = sb("w_2", [P, NE, NC, D])
        b_q = sb("b_q", [P, NC])
        b_q4 = sb("b_q4", [P, NC])
        b_k = sb("b_k", [P, NC])
        b_v = sb("b_v", [1, D])
        b_o = sb("b_o", [P, D])
        b_r = sb("b_r", [P, NE])
        b_1 = sb("b_1", [P, NE, NC])
        b_2 = sb("b_2", [NE, D])
        x_rows = [sb(f"x_rows{k}", [P, D]) for k in range(2)]
        ident = sb("ident", [P, P])
        ident_h = sb("ident_h", [P, P], BF16)
        causal_h = sb("causal_h", [P, P], BF16)
        head_rows = sb("head_rows", [P, 8, P])
        earlier = sb("earlier", [P, NE, NE])
        pick_row = sb("pick_row", [NE, NE, P])
        ones = sb("ones", [P, 1])
        eps = sb("eps", [P, 1])
        half = sb("half", [P, 1])

        q_t = sb("q_t", [P, NC, B * T])
        k_t = sb("k_t", [P, NC, B * T])
        v_s = sb("v_s", [P, TILES, NH, VW])

        k2_bd = sb("k2_bd", [P, B, NC, 8, CTX])
        v2_bd = sb("v2_bd", [P, B, 8, 2 * VW])

        q_h = [sb(f"q_h{k}", [P, P]) for k in range(4)]
        S_all = sb("S_all", [P, 8, T])
        S = [S_all[:, k, :] for k in range(8)]
        count = sb("count", [P, 2, T])
        y = [count[:, k, :] for k in range(2)]
        mark = [sb(f"mark{k}", [P, T], BF16) for k in range(2)]
        over = [sb(f"over{k}", [P, T], BF16) for k in range(4)]
        keep = [sb(f"keep{k}", [P, T], BF16) for k in range(2)]
        signs_all = sb("signs", [P, 2, T], BF16)
        signs = [signs_all[:, k, :] for k in range(2)]
        sided = [sb(f"sided{k}", [P, T], BF16) for k in range(4)]
        neg_m48 = sb("grp_f", [P, 3 * NH])
        late = sb("late", [P, 1])
        drop = sb("drop", [P, 1])
        iota8 = sb("iota8", [P, 8])
        neg_m = sb("neg_m", [P, 4, 2])
        balance = sb("balance", [P, 4, 2])
        filled = sb("filled", [P, 4, 2])
        turn_to = sb("turn_to", [P, 4, 2])
        ranks = sb("ranks", [P, 4, 2])
        thresh = sb("thresh", [P, 4, 2])
        balance1 = sb("balance1", [P, 4, 2])
        far = sb("far", [1, 4], mybir.dt.int32)
        far_f = sb("far_f", [P, 4])
        r_pos = sb("r_pos", [P, 2])
        r_neg = sb("r_neg", [P, 2])
        spare = sb("spare", [P, 2])
        dist = sb("dist", [P, 2, 8])
        eight = sb("eight", [P, 2, 8])
        hit8 = sb("hit8", [P, 2, 8])
        found = sb("found", [P, 2, 8])
        wanted = sb("wanted", [P, 2])
        prob = [sb(f"prob{k}", [P, T]) for k in range(2)]
        prob_t_all = sb("prob_t", [P, 2, QT, P])
        prob_t = [prob_t_all[:, k, :, :] for k in range(2)]

        den = sb("den", [P, NH])
        heads_o = sb("heads_o", [P, D])
        heads_t = sb("heads_t", [P, NC, P])
        res = sb("res", [P, D])
        stats = [sb(f"stats{k}", [P, 6]) for k in range(2)]
        mv = [sb(f"mv{k}", [P, 2]) for k in range(2)]
        var_e = [sb(f"var_e{k}", [P, 1]) for k in range(2)]
        rstd = [sb(f"rstd{k}", [P, 1]) for k in range(2)]
        x_all = sb("x_all", [P, 3, D])
        x1, x1b, x2 = (x_all[:, j, :] for j in range(3))
        x1_t = sb("x1_t", [P, NC, P])
        q2_t = sb("q2_t", [P, NC, P])
        m2 = sb("m2", [P, NH])
        p2 = sb("p2", [P, NH * CTX])
        p2_t = sb("p2_t", [P, NH * CTX])
        x2_0 = sb("x2_0", [P, D])
        x2_t = sb("x2_t", [P, NC, P])
        x2_t0 = sb("x2_t0", [P, NC, P])
        logit = sb("logit", [P, NE])
        l_max = sb("l_max", [P, 1])
        l_exp = sb("l_exp", [P, NE])
        above = sb("above", [P, NE, NE])
        tied = sb("tied", [P, NE, NE])
        rank = sb("rank", [P, NE])
        chosen = sb("chosen", [P, 2, NE])
        both = sb("both", [P, NE])
        l_sum = sb("l_sum", [P, 1])
        l_rec = sb("l_rec", [P, 1])
        gate = sb("gate", [P, NE])
        gate_0 = sb("gate_0", [P, NE])
        gates = sb("gates", [P, TILES, 2 * NE])
        gates_sum = sb("gates_sum", [P, 2, NE])
        gate_t = sb("gate_t", [NE, P])
        gate_b = sb("gate_b", [P, NE, P])
        x_in = sb("x_in", [P, 2, NC, P])
        hid_all = sb("hid_all", [P, 4, NC, P])
        hid = [hid_all[:, k, :, :] for k in range(2)]
        hid_g = [hid_all[:, 2 + k, :, :] for k in range(2)]
        fin = sb("fin", [P, D])
        gate_tz = sb("gate_tz", [NE, FIRST])
        gate_bz = sb("gate_bz", [P, TWICE, FIRST])
        x_in_z = sb("x_in_z", [P, TWICE, NC, FIRST])
        hid_z = sb("hid_z", [P, TWICE, NC, FIRST])
        hid_gz = sb("hid_gz", [P, NE, NC, FIRST])
        fin_z = sb("fin_z", [FIRST, D])
        stats_z = sb("stats_z", [FIRST, 6])
        mv_z = sb("mv_z", [FIRST, 2])
        var_z = sb("var_z", [FIRST, 1])
        rstd_z = sb("rstd_z", [FIRST, 1])

        w_qkv = S_all[:, :, :].rearrange("p k n -> p (k n)")[:, 0:NC * 3 * D].rearrange("p (c n) -> p c n", c=NC)
        flat_S = S_all[:, :, :].rearrange("p k n -> p (k n)")
        raw = [flat_S[:, NC * 3 * D:(NC + 1) * 3 * D], x_all[:, :, :].rearrange("p k n -> p (k n)")]
        flat_hid = hid_all[:, :, :, :].rearrange("p e c n -> p (e c n)").rearrange("p (j c n) -> p j c n", j=2, c=NC)
        ctx_t, k2_t = flat_hid[:, 0, :, :], flat_hid[:, 1, :, :]
        mag = [p2[:, 0:3 * D], p2_t[:, 0:3 * D]]
        halves = [flat_S[:, (NC + 1) * 3 * D:][:, j * 3 * D // 2:(j + 1) * 3 * D // 2] for j in range(4)]
        hit, nth, sel, same_head = (t.bitcast(BF16)[:, 0:3 * D] for t in halves)
        top1, top2 = (t.bitcast(BF16)[:, 0:3 * D] for t in y)
        qk_s = [prob[k][:, :] for k in range(2)]
        x_t = [prob_t[k][:, 0:NC, :] for k in range(2)]
        grp_f = neg_m48
        ctx_t2 = gate_b[:, :, :].rearrange("p e n -> p (e n)").rearrange("p (c b n) -> p c b n", c=NC, b=B)

        psC = ctx.enter_context(nc.psum_tensor("psC", [P, 1024], F32))
        psSF = ctx.enter_context(nc.psum_tensor("psSF", [P, 1024], F32))
        psPU = ctx.enter_context(nc.psum_tensor("psPU", [P, 1024], F32))
        psO = ctx.enter_context(nc.psum_tensor("psO", [P, 512], F32))
        psB = ctx.enter_context(nc.psum_tensor("psB", [P, 512], F32))
        psS = psSF[:, 0:512]
        psF = psSF[:, 512:512 + D]
        psP = psPU[:, 0:512]
        gates_z = psC[:, 0:TWICE * FIRST].rearrange("p (e n) -> p e n", e=TWICE)
        up_z = psC[:, 512:512 + TWICE * NC * FIRST].rearrange("p (e c n) -> p e c n", e=TWICE, c=NC)
        values_ps = [(psB if b < 2 else psPU[:, 512:1024])[:, b % 2 * D:(b % 2 + 1) * D] for b in range(B)]
        sum_z = psS[0:NE, 0:2]
        up_ps = [psPU[:, 512 + j * D:512 + (j + 1) * D] for j in range(2)]
        turn = psB[:, 0:D].rearrange("p (c n) -> p c n", c=NC)
        y_ps = psB[:, D:2 * D]
        qkv_ps = [psC, psSF]

        ld_proj = sem("ld_proj")
        ld_const = sem("ld_const")
        ld_ctx = sem("ld_ctx")
        ld_rest = sem("ld_rest")
        ld_exp = sem("ld_exp")
        ld_xt = [sem(f"ld_xt{k}") for k in range(2)]
        ld_xr = [sem(f"ld_xr{k}") for k in range(2)]
        a_proj = sem("a_proj")
        a_raw = sem("a_raw")
        a_dve = sem("a_dve")
        a_sel = sem("a_sel")
        a_turn = sem("a_turn")
        a_kept = sem("a_kept")
        init = sem("init")
        cleared = sem("cleared")
        carried = sem("carried")
        pool_carried = sem("pool_carried")
        c_k2 = sem("c_k2")
        c_k2t = sem("c_k2t")
        c_bd = sem("c_bd")
        c_v2 = sem("c_v2")
        c_v2c = sem("c_v2c")
        qh_ready = sem("qh_ready")
        s_made = sem("s_made")
        s_ready = sem("s_ready")
        counted = sem("counted")
        step = sem("step")
        picked = sem("picked")
        noted = sem("noted")
        flag_made = sem("flag_made")
        flag_ready = sem("flag_ready")
        sided_ready = sem("sided_ready")
        thresh_ready = sem("thresh_ready")
        over_ready = sem("over_ready")
        keep_ready = sem("keep_ready")
        exp_done = sem("exp_done")
        prob_ready = sem("prob_ready")
        prob_turned = sem("prob_turned")
        probt_ready = sem("probt_ready")
        pv_done = sem("pv_done")
        g0 = sem("g0_heads")
        g1_turn, g1_t, g1_y, g1_ln = sem("g1_turn"), sem("g1_t"), sem("g1_y"), sem("g1_ln")
        rs1, x1b_ready = sem("rs1"), sem("x1b_ready")
        g2_turn, g2_t, g2_q, g2_qt, g2_s, g2_dve = (sem(n) for n in (
            "g2_turn", "g2_t", "g2_q", "g2_qt", "g2_s", "g2_dve"))
        g3_exp, g3_turn, g3_t, g3_o, g3_dve = (sem(n) for n in (
            "g3_exp", "g3_turn", "g3_t", "g3_o", "g3_dve"))
        g4_turn, g4_t, g4_y, g4_ln, rs4 = (sem(n) for n in ("g4_turn", "g4_t", "g4_y", "g4_ln", "rs4"))
        g5_turn, g5_t, g5_l, g5_dve, g5_exp = (sem(n) for n in (
            "g5_turn", "g5_t", "g5_l", "g5_dve", "g5_exp"))
        f_turn, f_t, f_b, f_bc, f_xin, f_h, f_gelu, f_hg, f_y, f_ln, rs7 = (sem(n) for n in (
            "f_turn", "f_t", "f_b", "f_bc", "f_xin", "f_h", "f_gelu", "f_hg", "f_y", "f_ln", "rs7"))
        z_sum, z_ps, z_gate, z_turn, z_t, z_b, z_bc, z_xin, z_h, z_hb, z_gelu, z_hg, z_y, z_ln, z_root, z_kept = (sem(n) for n in (
            "z_sum", "z_ps", "z_gate", "z_turn", "z_t", "z_b", "z_bc", "z_xin", "z_h", "z_hb", "z_gelu", "z_hg", "z_y",
            "z_ln", "z_root", "z_kept"))
        out_done = sem("out_done")

        block = ctx.enter_context(nc.Block())

        def link(eng, signal, base):
            n = [0]

            def chain(ins):
                n[0] += 1
                ins.then_inc(signal, 1)
                return n[0]

            def caught_up():
                wait(eng, signal, base + n[0])
            chain.caught_up = caught_up
            chain.n = n
            return chain

        def qtile(b, qt):
            return b * T + qt * P

        def in_order(pieces):
            for _, piece in sorted(pieces, key=lambda x: x[0]):
                piece()

        def timeline(eng, attention, segment, last, again, first=lambda p: []):
            def slot(p, now, prev, before):
                pieces = []
                for lag, kind in enumerate(("scores", "classify", "select", "keep", "out")):
                    tile, q = (now, p - lag) if p >= lag else (prev, SLOTS + p - lag)
                    if tile is not None:
                        pieces += attention(kind, tile[0], tile[1], q)
                if p >= 3 and prev is not None:
                    c = QT * prev[0] + prev[1]
                    pieces += segment(p - 3, c, *prev)
                if before is not None:
                    c = QT * before[0] + before[1]
                    pieces += segment(p + 5, c, *before)
                in_order([*pieces, *first(p)])

            def tile(now, prev, before):
                for p in range(SLOTS):
                    slot(p, now, prev, before)

            for qt in range(QT):
                tile((0, qt), (0, qt - 1) if qt > 0 else None, (0, qt - 2) if qt > 1 else None)
            with eng.Fori(1, B) as b:
                b = Linear(b)
                for qt in range(QT):
                    tile((b, qt), *((b, qt - j) if qt >= j else (b - 1, QT + qt - j) for j in (1, 2)))
            tile(None, (B - 1, QT - 1), (B - 1, QT - 2))
            for i in range(5, SEGMENTS):
                in_order([*segment(i, TILES - 1, B - 1, QT - 1), *again(i)])
                if i == 6:
                    last()

        @block.sync
        def _(sp):
            def load_xt(t, k):
                sp.dma_start(x_t[k][:, :, :], a["x_t"].rearrange("(c p) n -> p c n", p=P)[:, :, ds(t * P, P)]
                             ).then_inc(ld_xt[k], 16)

            load_xt(0, 0)
            sp.dma_start(w_qkv[:, :, :], a["w_qkv"].rearrange("(c p) n -> p c n", p=P)).then_inc(ld_proj, 16)
            load_xt(1, 1)
            for dst, src in ((ident, "ident"), (ident_h, "ident_h"), (causal_h, "causal_h"), (same_head, "same_head"),
                             (half, "half"), (eps, "eps"), (late, "late"), (drop, "drop"), (iota8, "iota8")):
                sp.dma_start(dst[:, :], a[src]).then_inc(ld_const, 16)
            for dst, src in ((head_rows, "head_rows"), (earlier, "earlier"), (pick_row, "pick_row")):
                sp.dma_start(dst[:, :, :], a[src]).then_inc(ld_const, 16)
            sp.dma_start(ones[:, :], a["ones"]).then_inc(ld_const, 16)
            with sp.Fori(0, TILES // 2 - 1) as i:
                i = Linear(i)
                for k in range(2):
                    sp.wait_ge(a_proj, val(2 * i + (k + 1)))
                    load_xt(2 * i + (k + 2), k)

            x_tiles = a["x"].rearrange("(t p) n -> p t n", p=P)
            out_tiles = a["out"].rearrange("(t p) n -> p t n", p=P)

            def load_rows(c, k):
                wait(sp, g1_ln, LN * (c - 2) + 1)
                sp.dma_start(x_rows[k][:, :].unsqueeze(1), x_tiles[:, ds(c, 1), :]).then_inc(ld_xr[k], 16)

            def store(c):
                sp.wait_ge(f_ln, val(LN * (c + 1)))
                sp.dma_start(out_tiles[:, ds(c, 1), :], fin[:, :].unsqueeze(1)).then_inc(out_done, 16)

            for c in range(QT):
                load_rows(c, c % 2)
                if c >= 2:
                    store(c - 2)
            with sp.Fori(1, B) as b:
                b = Linear(b)
                for qt in range(QT):
                    load_rows(QT * b + qt, qt % 2)
                    store(QT * b + (qt - 2))
            store(TILES - 2)
            store(TILES - 1)
            sp.wait_ge(out_done, val(16 * TILES))
            sp.wait_ge(z_ln, LN)
            sp.dma_start(a["out"][0:FIRST, :], fin_z[:, :]).then_inc(out_done, 16)
            sp.wait_ge(out_done, 16 * (TILES + 1))

        N_CONST, N_CTX, N_REST = 13, 9, 7

        @block.gpsimd
        def _(pool):
            pool.wait_ge(ld_const, val(16 * N_CONST))
            pool.wait_ge(c_k2t, val(NC))
            for b in range(B):
                for g in range(NC):
                    nc.gpsimd.tensor_tensor(
                        k2_bd[:, b, g, :, :],
                        k2_t[:, g, b * CTX:(b + 1) * CTX].unsqueeze(1).to_broadcast([P, 8, CTX]),
                        head_rows[:, :, 0:CTX], ALU.mult).then_inc(c_bd, 1)

            def selected(t, k):
                chain = link(pool, a_sel, SPREAD * t)
                pool.wait_ge(a_dve, val(SPARSE * (t + 1)))
                chain(nc.gpsimd.tensor_tensor(sel[:, :], top1[:, :], top2[:, :], ALU.add))
                chain.caught_up()
                wait(pool, a_turn, t - 1)
                chain(nc.gpsimd.tensor_tensor(qk_s[k][:, :], raw[k][:, 0:2 * D], sel[:, 0:2 * D], ALU.mult))
                chain(nc.gpsimd.tensor_tensor(
                    v_s[:, ds(t, 1), :, 0:HD].rearrange("p t h j -> p (t h) j"),
                    raw[k][:, 2 * D:3 * D].rearrange("p (h j) -> p h j", j=HD),
                    sel[:, 2 * D:3 * D].rearrange("p (h j) -> p h j", j=HD), ALU.mult))
                chain.caught_up()
                assert chain.n[0] == SPREAD

            selected(0, 0)
            selected(1, 1)
            with pool.Fori(1, TILES // 2) as i:
                i = Linear(i)
                selected(2 * i, 0)
                selected(2 * i + 1, 1)
            pool.wait_ge(a_kept, val(2 * TILES))

            def heads_of(b, qt, p):
                s = 8 * (QT * b + qt) + p
                for k in range(2):
                    h, n = 2 * p + k, 2 * s + k
                    wait(pool, s_made, n - 3)
                    nc.gpsimd.tensor_tensor(q_h[h % 4][:, :], q_t[:, h // 8, ds(qtile(b, qt), P)],
                                            head_rows[:, h % 8, :], ALU.mult).then_inc(qh_ready, 1)

            def mask(b, qt, p, k):
                W = (qt + 1) * P
                n = 2 * (8 * (QT * b + qt) + p) + k
                pool.wait_ge(exp_done, val(n + 1))
                pool.wait_ge(keep_ready, val(n + 1))
                wait(pool, prob_turned, n - 1)
                nc.gpsimd.tensor_tensor(prob[k][:, 0:W], S[(2 * p + k) % 8][:, 0:W], keep[k][:, 0:W],
                                        ALU.mult).then_inc(prob_ready, 1)

            def root(stat, signal, n, k):
                pool.wait_ge(stat, val(LN * n + 3))
                nc.gpsimd.tensor_tensor(var_e[k][:, :], mv[k][:, 1:2], eps[:, :], ALU.add).then_inc(signal, 1)
                pool.wait_ge(signal, val(2 * n + 1))
                nc.gpsimd.tensor_tensor(rstd[k][:, :], var_e[k][:, :], half[:, :], ALU.pow).then_inc(signal, 1)

            def flag(b, qt, p):
                s, r = 8 * (QT * b + qt) + p, p % 4
                pool.wait_ge(flag_made, val(s + 1))
                pool.sem_inc(pool_carried, 1)
                nc.gpsimd.tensor_reduce(far[0:1, r:r + 1], far_f[:, r:r + 1], mybir.AxisListType.C, ALU.max
                                        ).then_inc(flag_ready, 1)

            def add_bias(c):
                pool.wait_ge(g1_ln, val(LN * c + 4))
                nc.gpsimd.tensor_tensor(x1b[:, :], x1[:, :], b_o[:, :], ALU.add).then_inc(x1b_ready, 1)

            def experts_in(f, c, lo, hi):
                xt = x2_t0 if isinstance(c, int) and c == 0 else x2_t
                pool.wait_ge(f_bc, val(2 * f + 2))
                for e in range(lo, hi):
                    wait(pool, f_h, NE * f + e - 1)
                    nc.gpsimd.tensor_tensor(x_in[:, e % 2, :, :], xt[:, :, :],
                                            gate_b[:, e, :].unsqueeze(1).to_broadcast([P, NC, P]),
                                            ALU.mult).then_inc(f_xin, 1)

            def gated(f, lo):
                for e in range(lo, lo + 2):
                    pool.wait_ge(f_gelu, val(2 * (NE * f + e) + 2))
                    wait(pool, f_y, NE * f + e - 1)
                    nc.gpsimd.tensor_tensor(hid_g[e % 2][:, :, :], hid[e % 2][:, :, :],
                                            gate_b[:, e, :].unsqueeze(1).to_broadcast([P, NC, P]),
                                            ALU.mult).then_inc(f_hg, 1)
                    if isinstance(f, int) and f == 0 and e >= TWICE:
                        nc.gpsimd.tensor_tensor(hid_gz[:, e, :, :], hid[e % 2][:, :, 0:FIRST],
                                                gate_b[:, e, 0:FIRST].unsqueeze(1).to_broadcast([P, NC, FIRST]),
                                                ALU.mult).then_inc(z_kept, 1)

            def attention(kind, b, qt, p):
                if kind == "scores":
                    ahead = [(qt, 0)] if qt == 0 and p == 0 else []
                    if p < SLOTS - 1:
                        ahead.append((qt, p + 1))
                    elif qt < QT - 1:
                        ahead.append((qt + 1, 0))
                    return [(0, lambda: [heads_of(b, *q) for q in ahead])]
                if kind == "classify":
                    return [(4, lambda: flag(b, qt, p))]
                if kind == "keep":
                    return [(22, lambda: mask(b, qt, p, 0)), (22.1, lambda: mask(b, qt, p, 1))]
                return []

            def segment(i, c, b, qt):
                f = c
                return {
                    2: [(0.5, lambda: root(g1_ln, rs1, c, 0)), (4.5, lambda: add_bias(c))],
                    5: [(0.5, lambda: root(g4_ln, rs4, c, 0))],
                    6: [(8.8, lambda: experts_in(f, c, 0, 2))],
                    8: [(0.7, lambda: gated(f, 0)), (0.8, lambda: experts_in(f, c, 2, 4))],
                    9: [(0.7, lambda: gated(f, 2)), (0.8, lambda: experts_in(f, c, 4, 6))],
                    10: [(0.7, lambda: gated(f, 4)), (0.8, lambda: experts_in(f, c, 6, NE))],
                    11: [(0.7, lambda: gated(f, 6))],
                    12: [(0.5, lambda: root(f_ln, rs7, f, 1))],
                }.get(i, [])

            def root_z():
                pool.wait_ge(z_ln, 3)
                nc.gpsimd.tensor_tensor(var_z[:, :], mv_z[:, 1:2], eps[0:FIRST, :], ALU.add).then_inc(z_root, 1)
                pool.wait_ge(z_root, 1)
                nc.gpsimd.tensor_tensor(rstd_z[:, :], var_z[:, :], half[0:FIRST, :], ALU.pow).then_inc(z_root, 1)

            timeline(pool, attention, segment, lambda: None, lambda i: [(30, root_z)] if i == 12 else [])

        @block.scalar
        def _(act):
            def load_rows_of(dst, src, signal):
                act.dma_start(dst[:, :, :], a[src].rearrange("(c p) n -> p c n", p=P)).then_inc(signal, 16)

            for dst, src in ((w_k2, "w_k2"), (w_v2, "w_v2"), (ctx_t, "ctx_t")):
                load_rows_of(dst, src, ld_ctx)
            for b in range(B):
                act.dma_start(ctx_t2[:, :, b, :], a["ctx_t2"].rearrange("(c p) n -> p c n", p=P)[:, :, b * 2 * CTX:(b + 1) * 2 * CTX]
                              ).then_inc(ld_ctx, 16)
            act.dma_start(b_k[:, :], a["b_k"]).then_inc(ld_ctx, 16)
            act.dma_start(b_v[:, :], a["b_v"]).then_inc(ld_ctx, 16)

            def kept(t, k):
                act.wait_ge(a_turn, val(t + 1))
                ps = psPU[:, k * 512:(k + 1) * 512].rearrange("p (c n) -> p c n", c=4)
                nc.scalar.activation(q_t[:, :, ds(t * P, P)], ps[:, 0:2, :], ACT.Copy,
                                     scale=1.0 / HD ** 0.5).then_inc(a_kept, 1)
                nc.scalar.activation(k_t[:, :, ds(t * P, P)], ps[:, 2:4, :], ACT.Copy).then_inc(a_kept, 1)

            def proj(t, k):
                act.wait_ge(a_proj, val(t + 1))
                wait(act, a_sel, SPREAD * (t - 1))
                nc.scalar.activation(raw[k][:, :], qkv_ps[k][:, 0:3 * D], ACT.Copy).then_inc(a_raw, 1)
                nc.scalar.activation(mag[k][:, :], qkv_ps[k][:, 0:3 * D], ACT.Abs).then_inc(a_raw, 1)

            proj(0, 0)
            proj(1, 1)
            for dst, src in ((w_o, "w_o"), (w_q2, "w_q2"), (w_o2, "w_o2"), (w_r, "w_r")):
                load_rows_of(dst, src, ld_rest)
            act.dma_start(b_q[:, :], a["b_q"]).then_inc(ld_rest, 16)
            act.dma_start(b_o[:, :], a["b_o"].partition_broadcast(P)).then_inc(ld_rest, 16)
            act.dma_start(b_r[:, :], a["b_r"].partition_broadcast(P)).then_inc(ld_rest, 16)
            act.dma_start(w_1[:, :, :, :], a["w_1"].rearrange("e (c p) n -> p e c n", p=P)).then_inc(ld_exp, 16)
            act.dma_start(w_2[:, :, :, :], a["w_2"].rearrange("e (c p) n -> p e c n", p=P)).then_inc(ld_exp, 16)
            act.dma_start(b_1[:, :, :], a["b_1"]).then_inc(ld_exp, 16)
            act.dma_start(b_2[:, :], a["b_2"]).then_inc(ld_exp, 16)
            act.wait_ge(ld_ctx, val(16 * N_CTX))
            for g in range(NC):
                act.wait_ge(c_k2, NC)
                nc.scalar.activation(k2_t[:, g, :], psO[:, g * 256:(g + 1) * 256], ACT.Identity,
                                     bias=b_k[:, g:g + 1]).then_inc(c_k2t, 1)
            act.wait_ge(ld_rest, val(16 * N_REST))
            nc.scalar.activation(b_q4[:, :], b_q[:, :], ACT.Copy, scale=1.0 / HD ** 0.5).then_inc(init, 1)
            kept(0, 0)
            with act.Fori(1, TILES // 2) as i:
                i = Linear(i)
                proj(2 * i, 0)
                kept(2 * i - 1, 1)
                proj(2 * i + 1, 1)
                kept(2 * i, 0)
            kept(TILES - 1, 1)

            def scores_out(b, qt, p, k):
                W = (qt + 1) * P
                h, n = 2 * p + k, 2 * (8 * (QT * b + qt) + p) + k
                two = 2 * W <= T
                act.wait_ge(s_made, val(n + 1 + two))
                wait(act, prob_ready, n - 7 + two)
                if two:
                    nc.scalar.activation(S_all[:, h % 8:h % 8 + 2, 0:W],
                                         psS.rearrange("p (k n) -> p k n", k=2)[:, :, 0:W], ACT.Copy
                                         ).then_inc(s_ready, 2)
                else:
                    nc.scalar.activation(S[h % 8][:, 0:W], psS[:, 0:W], ACT.Copy).then_inc(s_ready, 1)

            def counts(b, qt, p):
                W, s = (qt + 1) * P, 8 * (QT * b + qt) + p
                act.wait_ge(s_ready, val(2 * s + 2))
                wait(act, counted, 4 * s)
                wait(act, flag_made, s)
                if qt in BY_VECTOR:
                    nc.scalar.activation(signs_all[:, :, 0:W], S_all[:, 2 * p % 8:2 * p % 8 + 2, 0:W], ACT.Sign
                                         ).then_inc(counted, 4)
                    return
                for k in range(2):
                    nc.scalar.activation(signs[k][:, 0:W], S[(2 * p + k) % 8][:, 0:W], ACT.Sign,
                                         accum_out=balance[:, p % 4, k:k + 1]).then_inc(counted, 1)
                for k in range(2):
                    act.wait_ge(counted, val(4 * s + k + 1))
                    nc.scalar.activation(signs[k][:, 0:W], signs[k][:, 0:W], ACT.Abs,
                                         accum_out=filled[:, p % 4, k:k + 1]).then_inc(counted, 1)

            def compare(b, qt, p, k):
                W = (qt + 1) * P
                h, n = 2 * p + k, 2 * (8 * (QT * b + qt) + p) + k
                act.wait_ge(thresh_ready, val(8 * (QT * b + qt) + p + 1))
                wait(act, keep_ready, n - 3)
                nc.scalar.activation(over[h % 4][:, 0:W], S[h % 8][:, 0:W], ACT.Sign, scale=-1.0,
                                     bias=thresh[:, p % 4, k:k + 1], accum_out=balance1[:, p % 4, k:k + 1]
                                     ).then_inc(over_ready, 1)

            def turned_signs(b, qt, p):
                W, s = (qt + 1) * P, 8 * (QT * b + qt) + p
                for k in range(2):
                    act.wait_ge(flag_made, val(s + 1))
                    wait(act, thresh_ready, s - 1)
                    nc.scalar.activation(sided[(2 * p + k) % 4][:, 0:W], S[(2 * p + k) % 8][:, 0:W], ACT.Sign,
                                         scale=turn_to[:, p % 4, k:k + 1]).then_inc(sided_ready, 1)

            def exps(b, qt, p, k):
                W = (qt + 1) * P
                h, n = 2 * p + k, 2 * (8 * (QT * b + qt) + p) + k
                act.wait_ge(over_ready, val(n + 1))
                nc.scalar.activation(S[h % 8][:, 0:W], S[h % 8][:, 0:W], ACT.Exp,
                                     bias=neg_m[:, p % 4, k:k + 1]).then_inc(exp_done, 1)

            def turned_out(b, qt, p, k):
                W = (qt + 1) * P
                n = 2 * (8 * (QT * b + qt) + p) + k
                two = 2 * W <= T
                act.wait_ge(prob_turned, val(n + 1 + two))
                wait(act, pv_done, n - 1 + two)
                if two:
                    nc.scalar.activation(prob_t_all[:, :, 0:qt + 1, :],
                                         psP.rearrange("p (k c n) -> p k c n", k=2, n=P)[:, :, 0:qt + 1, :],
                                         ACT.Copy).then_inc(probt_ready, 2)
                else:
                    nc.scalar.activation(prob_t[k][:, 0:qt + 1, :],
                                         psP[:, 0:W].rearrange("p (c n) -> p c n", c=qt + 1),
                                         ACT.Copy).then_inc(probt_ready, 1)

            def out_of(made, count, dst, src, signal, func=ACT.Copy, **kw):
                act.wait_ge(made, val(count))
                nc.scalar.activation(dst, src, func, **kw).then_inc(signal, 1)

            def queries2(c):
                for g in range(NC):
                    out_of(g2_q, NC * c + NC, q2_t[:, g, :], y_ps[:, g * P:(g + 1) * P], g2_qt,
                           ACT.Identity, bias=b_q4[:, g:g + 1], scale=1.0 / HD ** 0.5)

            def gates_out(f):
                for j in range(2):
                    act.wait_ge(f_b, val(2 * f + 2))
                    wait(act, f_hg, NE * f)
                    nc.scalar.activation(gate_b[:, 4 * j:4 * j + 4, :],
                                         psC[:, j * 512:(j + 1) * 512].rearrange("p (e n) -> p e n", e=4), ACT.Copy
                                         ).then_inc(f_bc, 1)

            def gelus(f, lo):
                for e in range(lo, lo + 2):
                    act.wait_ge(f_h, val(NE * f + lo + 2))
                    wait(act, f_hg, NE * f + e - 1)
                    for g in range(NC):
                        nc.scalar.activation(hid[e % 2][:, g, :], up_ps[e % 2][:, g * P:(g + 1) * P],
                                             ACT.Gelu, bias=b_1[:, e, g:g + 1]).then_inc(f_gelu, 1)

            def attention(kind, b, qt, p):
                if kind == "scores":
                    return [(2, lambda: scores_out(b, qt, p, 0)), *([] if qt < 2 else [(4, lambda: scores_out(b, qt, p, 1))]),
                            (5.3, lambda: counts(b, qt, p))]
                if kind == "classify":
                    return [(5.4, lambda: turned_signs(b, qt, p))]
                if kind == "out":
                    return [(2.1, lambda: turned_out(b, qt, p, 0)),
                            *([] if qt < 2 else [(4.01, lambda: turned_out(b, qt, p, 1))])]
                if kind == "keep":
                    return [(1, lambda: compare(b, qt, p, 0)), (1.1, lambda: compare(b, qt, p, 1)),
                            (1.2, lambda: exps(b, qt, p, 0)), (1.3, lambda: exps(b, qt, p, 1))]
                return []

            def segment(i, c, b, qt):
                f = c
                zero = isinstance(c, int) and c == 0
                return {
                    1: [(4.05, lambda: out_of(g1_turn, c + 1, heads_t[:, :, :], turn, g1_t))],
                    2: [(4.05, lambda: out_of(g2_turn, c + 1, x1_t[:, :, :], turn, g2_t)),
                        (4.7, lambda: queries2(c))],
                    3: [(4.02, lambda: out_of(g2_dve, 2 * c + 2, p2[:, :], p2[:, :], g3_exp, ACT.Exp)),
                        (6.5, lambda: out_of(g3_turn, c + 1, p2_t[:, :], psC[:, :], g3_t))],
                    4: [(4.05, lambda: out_of(g4_turn, c + 1, heads_t[:, :, :], turn, g4_t))],
                    5: [(4.05, lambda: out_of(g5_turn, c + 1, (x2_t0 if zero else x2_t)[:, :, :], turn, g5_t))],
                    6: [(1.5, lambda: out_of(g5_dve, ROUTE * c + 3, l_exp[:, :], logit[:, :], g5_exp, ACT.Exp)),
                        (8.7, lambda: out_of(f_turn, f + 1, gate_t[:, :], psB[0:NE, 0:P], f_t)),
                        (8.9, lambda: gates_out(f))],
                    7: [(6, lambda: gelus(f, 0))],
                    8: [(6, lambda: gelus(f, 2))],
                    9: [(6, lambda: gelus(f, 4))],
                    10: [(6, lambda: gelus(f, 6))],
                }.get(i, [])

            act.wait_ge(ld_exp, val(16 * 4))
            def again(i):
                return {7: [(30, lambda: out_of(z_turn, 1, gate_tz[:, :], psB[0:NE, 0:FIRST], z_t))],
                        8: [(30, lambda: out_of(z_b, 1, gate_bz[:, :, :], gates_z, z_bc))],
                        10: [(30, lambda: out_of(z_hb, 1, hid_z[:, :, :, :], hid_z[:, :, :, :], z_gelu, ACT.Gelu))],
                        }.get(i, [])

            timeline(act, attention, segment, lambda: None, again)

        @block.tensor
        def _(pe):
            def proj(t, k, i):
                pe.wait_ge(ld_xt[k], val(16 * (i + 1)))
                wait(pe, a_raw, 2 * (t - 1))
                for lo, hi in ((0, 2 * D), (2 * D, 3 * D)):
                    for c in range(NC):
                        mm = nc.tensor.matmul(qkv_ps[k][:, lo:hi], x_t[k][:, c, :], w_qkv[:, c, lo:hi],
                                              start=(c == 0), stop=(c == NC - 1))
                mm.then_inc(a_proj, 1)

            def turn_qk(t, k):
                pe.wait_ge(a_sel, val(SPREAD * (t + 1)))
                wait(pe, a_kept, 2 * (t - 1))
                if isinstance(t, Linear):
                    pe.wait_ge(c_v2c, 2 * B)
                for j in range(4):
                    mm = nc.tensor.transpose(psPU[:, k * 512 + j * P:k * 512 + (j + 1) * P],
                                             qk_s[k][:, j * P:(j + 1) * P], ident[:, :])
                mm.then_inc(a_turn, 1)

            pe.wait_ge(ld_proj, 16)
            proj(0, 0, 0)
            proj(1, 1, 0)
            pe.wait_ge(ld_ctx, val(16 * N_CTX))
            pe.wait_ge(ld_const, val(16 * N_CONST))
            for g in range(NC):
                for c in range(NC):
                    mm = nc.tensor.matmul(psO[:, g * 256:(g + 1) * 256], w_k2[:, c, g * P:(g + 1) * P], ctx_t[:, c, :],
                                          start=(c == 0), stop=(c == NC - 1))
                mm.then_inc(c_k2, 1)
            for b in range(B):
                for c in range(NC):
                    nc.tensor.matmul(values_ps[b], ctx_t2[:, c, b, :], w_v2[:, c, :], start=(c == 0), stop=False)
                nc.tensor.matmul(values_ps[b], head_rows[0:1, 0, :], b_v[:, :], start=False, stop=True).then_inc(c_v2, 1)
            turn_qk(0, 0)
            with pe.Fori(1, TILES // 2) as i:
                i = Linear(i)
                proj(2 * i, 0, i)
                turn_qk(2 * i - 1, 1)
                proj(2 * i + 1, 1, i)
                turn_qk(2 * i, 0)
            turn_qk(TILES - 1, 1)
            pe.wait_ge(a_kept, val(2 * TILES))
            pe.wait_ge(c_k2t, val(NC))
            pe.wait_ge(c_bd, val(B * NC))
            pe.wait_ge(c_v2c, val(2 * B))
            pe.wait_ge(ld_rest, val(16 * N_REST))

            def scores(b, qt, p, k):
                W = (qt + 1) * P
                h, n = 2 * p + k, 2 * (8 * (QT * b + qt) + p) + k
                two = 2 * W <= T
                pe.wait_ge(qh_ready, val(n + 1))
                wait(pe, s_ready, n - k if two else n)
                col = k * 256 if two else 0
                out = psS[:, col:col + W]
                nc.tensor.matmul(out, q_h[h % 4][:, :], k_t[:, h // 8, ds(b * T, W)], start=True, stop=False)
                nc.tensor.matmul(out[:, W - P:W], ident_h[:, :], causal_h[:, :], start=False, stop=True
                                 ).then_inc(s_made, 1)

            def turn_probs(b, qt, p, k):
                n = 2 * (8 * (QT * b + qt) + p) + k
                two = 2 * (qt + 1) * P <= T
                pe.wait_ge(prob_ready, val(n + 1))
                wait(pe, probt_ready, n - k if two else n)
                col = k * 256 if two else 0
                for j in range(qt + 1):
                    mm = nc.tensor.transpose(psP[:, col + j * P:col + (j + 1) * P],
                                             prob[k][:, j * P:(j + 1) * P], ident[:, :])
                mm.then_inc(prob_turned, 1)

            def values(b, qt, p, k):
                h, n = 2 * p + k, 2 * (8 * (QT * b + qt) + p) + k
                if h == 0:
                    wait(pe, g0, 2 * (QT * b + qt))
                pe.wait_ge(probt_ready, val(n + 1))
                for j in range(qt + 1):
                    mm = nc.tensor.matmul(psO[:, h * VW:(h + 1) * VW], prob_t[k][:, j, :],
                                          v_s[:, ds(QT * b + j, 1), h, :].rearrange("p t v -> p (t v)"),
                                          start=(j == 0), stop=(j == qt))
                mm.then_inc(pv_done, 1)

            def turned(ready, count, src, signal):
                pe.wait_ge(ready, val(count))
                for g in range(NC):
                    mm = nc.tensor.transpose(turn[:, g, :], src[:, g * P:(g + 1) * P], ident[:, :])
                mm.then_inc(signal, 1)

            def by_rows(ready, count, xt, w, signal, out):
                pe.wait_ge(ready, val(count))
                for c in range(NC):
                    mm = nc.tensor.matmul(out, xt[:, c, :], w[:, c, :], start=(c == 0), stop=(c == NC - 1))
                mm.then_inc(signal, 1)

            def queries2(c):
                pe.wait_ge(g2_t, val(c + 1))
                for g in range(NC):
                    for cc in range(NC):
                        mm = nc.tensor.matmul(y_ps[:, g * P:(g + 1) * P], w_q2[:, cc, g * P:(g + 1) * P],
                                              x1_t[:, cc, :], start=(cc == 0), stop=(cc == NC - 1))
                    mm.then_inc(g2_q, 1)

            def scores2(c, b):
                pe.wait_ge(g2_qt, val(NC * c + 2))
                wait(pe, f_bc, 2 * c)
                for g in range(NC):
                    mm = nc.tensor.matmul(psC[:, g * 512:(g + 1) * 512], q2_t[:, g, :],
                                          k2_bd[:, ds(b, 1), g, :, :].rearrange("p b h n -> p (b h n)"),
                                          start=True, stop=True)
                mm.then_inc(g2_s, 1)

            def turn_p2(c):
                pe.wait_ge(g3_exp, val(c + 1))
                for j in range(8):
                    mm = nc.tensor.transpose(psC[:, j * P:(j + 1) * P], p2[:, j * P:(j + 1) * P], ident[:, :])
                mm.then_inc(g3_turn, 1)

            def values2(c, b):
                pe.wait_ge(g3_t, val(c + 1))
                for j in range(8):
                    mm = nc.tensor.matmul(psC[:, j * 2 * VW:(j + 1) * 2 * VW], p2_t[:, j * P:(j + 1) * P],
                                          v2_bd[:, ds(b, 1), j, :].rearrange("p b n -> p (b n)"),
                                          start=True, stop=True)
                mm.then_inc(g3_o, 1)

            def turn_gates(f, c):
                zero = isinstance(c, int) and c == 0
                pe.wait_ge(g5_dve, val(ROUTE * (c + 1)))
                nc.tensor.transpose(psB[0:NE, 0:P], (gate_0 if zero else gate)[:, :], ident[:, :]).then_inc(f_turn, 1)

            def spread_gates(f):
                pe.wait_ge(f_t, val(f + 1))
                for e in range(NE):
                    mm = nc.tensor.matmul(psC[:, e * P:(e + 1) * P], pick_row[:, e, :], gate_t[:, :],
                                          start=True, stop=True)
                    if e % 4 == 3:
                        mm.then_inc(f_b, 1)

            def up(f, lo):
                wait(pe, f_gelu, 2 * (NE * f + lo))
                for e in range(lo, lo + 2):
                    pe.wait_ge(f_xin, val(NE * f + e + 1))
                    for g in range(NC):
                        for c in range(NC):
                            mm = nc.tensor.matmul(up_ps[e % 2][:, g * P:(g + 1) * P],
                                                  w_1[:, e, c, g * P:(g + 1) * P], x_in[:, e % 2, c, :],
                                                  start=(c == 0), stop=(c == NC - 1))
                    mm.then_inc(f_h, 1)

            def down(f, lo):
                if lo == 0:
                    wait(pe, f_ln, LN * (f - 1) + 1 if not isinstance(f, int) or f > 0 else 0)
                    nc.tensor.matmul(psF, gate_t[:, :], b_2[:, :], start=True, stop=False)
                for e in range(lo, lo + 2):
                    pe.wait_ge(f_hg, val(NE * f + e + 1))
                    for c in range(NC):
                        mm = nc.tensor.matmul(psF, hid_g[e % 2][:, c, :], w_2[:, e, c, :],
                                              start=False, stop=(e == NE - 1 and c == NC - 1))
                    mm.then_inc(f_y, 1)

            def attention(kind, b, qt, p):
                if kind == "scores":
                    return [(1, lambda: scores(b, qt, p, 0)), (1.1 if qt < 2 else 3, lambda: scores(b, qt, p, 1))]
                if kind == "out":
                    return [(1.2, lambda: turn_probs(b, qt, p, 0)), (1.25 if qt < 2 else 3.1, lambda: turn_probs(b, qt, p, 1)),
                            (7, lambda: values(b, qt, p, 0)), (7.1, lambda: values(b, qt, p, 1))]
                return []

            def segment(i, c, b, qt):
                f = c
                zero = isinstance(c, int) and c == 0
                return {
                    1: [(3.5, lambda: turned(g0, 2 * c + 2, heads_o, g1_turn)),
                        (4.5, lambda: by_rows(g1_t, c + 1, heads_t, w_o, g1_y, y_ps))],
                    2: [(3.5, lambda: turned(g1_ln, LN * c + 4, x1, g2_turn)), (4.5, lambda: queries2(c)),
                        (8.5, lambda: scores2(c, b))],
                    3: [(5.7, lambda: turn_p2(c)), (8.5, lambda: values2(c, b))],
                    4: [(3.5, lambda: turned(g3_dve, 2 * c + 2, heads_o, g4_turn)),
                        (4.5, lambda: by_rows(g4_t, c + 1, heads_t, w_o2, g4_y, y_ps))],
                    5: [(3.5, lambda: turned(g4_ln, LN * c + 4, x2_0 if zero else x2, g5_turn)),
                        (4.5, lambda: by_rows(g5_t, c + 1, x2_t0 if zero else x2_t, w_r, g5_l, y_ps[:, 0:NE]))],
                    6: [(8.6, lambda: turn_gates(f, c)), (8.8, lambda: spread_gates(f))],
                    7: [(5.5, lambda: up(f, 0))],
                    8: [(5.5, lambda: up(f, 2)), (5.6, lambda: down(f, 0))],
                    9: [(5.5, lambda: up(f, 4)), (5.6, lambda: down(f, 2))],
                    10: [(5.5, lambda: up(f, 6)), (5.6, lambda: down(f, 4))],
                    11: [(5.6, lambda: down(f, 6))],
                }.get(i, [])

            def last():
                pe.wait_ge(z_sum, 1)
                for k in range(2):
                    mm = nc.tensor.matmul(sum_z[:, k:k + 1], gates_sum[:, k, :], ones[:, 0:1], start=True, stop=True)
                mm.then_inc(z_ps, 1)
                pe.wait_ge(z_gate, 2)

            def turn_z():
                pe.wait_ge(f_t, TILES)
                nc.tensor.transpose(psB[0:NE, 0:FIRST], gate_0[0:FIRST, :], ident[0:FIRST, 0:FIRST]).then_inc(z_turn, 1)

            def spread_z():
                pe.wait_ge(z_t, 1)
                pe.wait_ge(f_bc, 2 * TILES)
                for e in range(TWICE):
                    mm = nc.tensor.matmul(gates_z[:, e, :], pick_row[:, e, :], gate_tz[:, :], start=True, stop=True)
                mm.then_inc(z_b, 1)

            def up_first():
                pe.wait_ge(z_xin, 1)
                for e in range(TWICE):
                    for g in range(NC):
                        for c in range(NC):
                            mm = nc.tensor.matmul(up_z[:, e, g, :], w_1[:, e, c, g * P:(g + 1) * P], x_in_z[:, e, c, :],
                                                  start=(c == 0), stop=(c == NC - 1))
                mm.then_inc(z_h, 1)

            def down_others():
                pe.wait_ge(z_kept, NE - TWICE)
                for e in range(TWICE, NE):
                    for c in range(NC):
                        nc.tensor.matmul(psO[0:FIRST, 0:D], hid_gz[:, e, c, :], w_2[:, e, c, :],
                                         start=(e == TWICE and c == 0), stop=False)

            def down_first():
                nc.tensor.matmul(psO[0:FIRST, 0:D], gate_tz[:, :], b_2[:, :], start=False, stop=False)
                pe.wait_ge(z_hg, 1)
                for e in range(TWICE):
                    for c in range(NC):
                        mm = nc.tensor.matmul(psO[0:FIRST, 0:D], hid_gz[:, e, c, :], w_2[:, e, c, :],
                                              start=False, stop=(e == TWICE - 1 and c == NC - 1))
                mm.then_inc(z_y, 1)

            def again(i):
                return {5: [(3, down_others)], 7: [(30, turn_z)], 8: [(30, spread_z)], 9: [(30, up_first)], 11: [(30, down_first)]}.get(i, [])

            timeline(pe, attention, segment, last, again)

        @block.vector
        def _(dve):
            def settle():
                dve.sem_inc(carried, 1)

            nc.vector.memset(v2_bd[:, :, :, :], 0.0).then_inc(cleared, 1)
            nc.vector.memset(v_s[:, :, :, HD:VW], 1.0).then_inc(cleared, 1)
            dve.wait_ge(cleared, 2)
            nc.vector.memset(v2_bd[0:64, :, :, HD:VW], 1.0).then_inc(cleared, 1)
            nc.vector.memset(v2_bd[64:128, :, :, VW + HD:2 * VW], 1.0).then_inc(cleared, 1)
            dve.wait_ge(ld_const, val(16 * N_CONST))

            def grouped(t):
                return t[:, :].rearrange("p (h j) -> p h j", j=HD)

            def spread(t):
                return t[:, :].unsqueeze(2).to_broadcast([P, 3 * NH, HD])

            def sparsify(t, k):
                chain = link(dve, a_dve, SPARSE * t)
                dve.wait_ge(a_raw, val(2 * (t + 1)))

                def first_largest(top):
                    dve_in = grouped(mag[k])
                    chain(nc.vector.tensor_reduce(grp_f[:, :], dve_in, X, ALU.max))
                    chain.caught_up()
                    chain(nc.vector.tensor_tensor(grouped(hit), dve_in, spread(grp_f), ALU.is_equal))
                    chain.caught_up()
                    chain(nc.vector.tensor_tensor_scan(nth[:, :], same_head[:, :], hit[:, :], 0.0, ALU.mult, ALU.add))
                    chain.caught_up()
                    wait(dve, a_sel, SPREAD * (t - 1) + 1)
                    chain(nc.vector.scalar_tensor_tensor(out=top[:, :], in0=nth[:, :], scalar=1.0, in1=hit[:, :],
                                                        op0=ALU.is_equal, op1=ALU.mult))
                    chain.caught_up()

                first_largest(top1)
                chain(nc.vector.scalar_tensor_tensor(out=mag[k][:, :], in0=top1[:, :], scalar=NEG, in1=mag[k][:, :],
                                                    op0=ALU.mult, op1=ALU.add))
                chain.caught_up()
                first_largest(top2)
                assert chain.n[0] == SPARSE

            sparsify(0, 0)
            dve.wait_ge(init, 1)
            dve.wait_ge(cleared, 4)
            for b in range(B):
                dve.wait_ge(c_v2, val(b // 2 * 2 + 2))
                for j in range(2):
                    src = values_ps[b][64 * j:64 * j + 64, :].rearrange("p (m j n) -> p m j n", j=2, n=HD)[:, :, j, :]
                    nc.vector.tensor_copy(v2_bd[64 * j:64 * j + 64, b, :, j * VW:j * VW + HD], src).then_inc(c_v2c, 1)
            sparsify(1, 1)
            with dve.Fori(1, TILES // 2) as i:
                i = Linear(i)
                sparsify(2 * i, 0)
                sparsify(2 * i + 1, 1)

            at = [0]

            def fresh():
                if at[0]:
                    dve.wait_ge(step, at[0])
                    dve.sem_clear(step)
                at[0] = 0

            def then(ins):
                ins.then_inc(step, 1)
                at[0] += 1
                return at[0]

            def after(number):
                dve.wait_ge(step, number)

            def classify(b, qt, p):
                W, s, r, v, n = (qt + 1) * P, 8 * (QT * b + qt) + p, p % 4, nc.vector, {}

                def ranks_1():
                    dve.wait_ge(counted, val(4 * s + 4))
                    if qt in BY_VECTOR:
                        then(v.tensor_reduce(balance[:, r, :], signs_all[:, :, 0:W], X, ALU.add))
                        after(then(v.tensor_reduce(filled[:, r, :], signs_all[:, :, 0:W], X, ALU.add,
                                                   apply_absolute_value=True)))
                    n["pos"] = then(v.tensor_tensor(r_pos[:, :], balance[:, r, :], filled[:, r, :], ALU.add))
                    n["neg"] = then(v.tensor_tensor(r_neg[:, :], filled[:, r, :], balance[:, r, :], ALU.subtract))

                def largest(k):
                    wait(dve, exp_done, 2 * (s - 4) + 2)
                    n["max"] = then(v.tensor_reduce(neg_m[:, r, k:k + 1], S[(2 * p + k) % 8][:, 0:W], X, ALU.max, negate=True))

                def side():
                    after(n["pos"])
                    n["pos"] = then(v.tensor_scalar(r_pos[:, :], r_pos[:, :], 0.5, float(1 - KEEP), ALU.mult, ALU.add))
                    after(n["neg"])
                    n["neg"] = then(v.tensor_scalar(r_neg[:, :], r_neg[:, :], 0.5, float(KEEP - W), ALU.mult, ALU.add))

                def late_rows():
                    after(n["neg"])
                    n["neg"] = then(v.tensor_scalar(r_neg[:, :], r_neg[:, :], late[:, 0:1], None, ALU.mult))

                def nearer():
                    after(n["pos"])
                    n["spare"] = then(v.tensor_scalar(spare[:, :], r_pos[:, :], 0.0, -2.0, ALU.is_gt, ALU.mult))
                    after(n["neg"])
                    n["ranks"] = then(v.tensor_tensor(ranks[:, r, :], r_pos[:, :], r_neg[:, :], ALU.max))

                def furthest():
                    after(n["spare"])
                    then(v.tensor_scalar(turn_to[:, r, :], spare[:, :], 1.0, None, ALU.add))
                    after(n["ranks"])
                    wait(dve, flag_ready, s - 3)
                    v.tensor_reduce(far_f[:, r:r + 1], ranks[:, r, :], X, ALU.max).then_inc(flag_made, 1)

                return [(2.1, ranks_1), (2.2, lambda: largest(0)), (2.3, side),
                        *([(2.35, late_rows)] if qt == 0 else []), (2.5, nearer), (2.6, lambda: largest(1)), (2.7, furthest)]

            def keep_first(b, qt, p):
                W, s, r, v, n = (qt + 1) * P, 8 * (QT * b + qt) + p, p % 4, nc.vector, {}
                o = [over[(2 * p + k) % 4] for k in range(2)]

                def ties():
                    for k in range(2):
                        dve.wait_ge(over_ready, val(2 * s + k + 1))
                        n[k] = then(v.tensor_scalar(mark[k][:, 0:W], o[k][:, 0:W], 0.0, 2.0, ALU.is_equal, ALU.mult))

                def running():
                    for k in range(2):
                        after(n[k])
                        n[k] = then(v.tensor_tensor_scan(count[:, k, 0:W], mark[k][:, 0:W], mark[k][:, 0:W],
                                                         2.0 * W - 4.0 * KEEP, ALU.add, ALU.max))

                def left():
                    after(n[1])
                    n["wanted"] = then(v.scalar_tensor_tensor(out=wanted[:, :], in0=count[:, :, W - 1], scalar=0.5,
                                                              in1=balance1[:, r, :], op0=ALU.mult, op1=ALU.add))

                def kept():
                    after(n["wanted"])
                    for k in range(2):
                        wait(dve, prob_ready, 2 * s + k - 1)
                        v.scalar_tensor_tensor(out=keep[k][:, 0:W], in0=count[:, k, 0:W], scalar=wanted[:, k:k + 1],
                                               in1=o[k][:, 0:W], op0=ALU.is_le, op1=ALU.is_gt).then_inc(keep_ready, 1)

                return [(5.1, ties), (5.2, running), (5.3, left), (5.5, kept)]

            def select(b, qt, p):
                W, s, r, v, n = (qt + 1) * P, 8 * (QT * b + qt) + p, p % 4, nc.vector, {}
                two = (P, 2, 8)

                def load():
                    dve.wait_ge(flag_ready, val(s + 1))
                    settle()
                    n["furthest"] = dve.value_load(far[0:1, r:r + 1], min_val=-T, max_val=T)
                    n["found"] = then(v.memset(found[:, :, :], 0.0))
                    n["dist"] = then(v.tensor_tensor(dist[:, :, :], iota8[:, :].unsqueeze(1).to_broadcast(two),
                                                     ranks[:, r, :].unsqueeze(2).to_broadcast(two), ALU.subtract))

                def one_round(first):
                    for k in range(2):
                        v.max(eight[:, k, :], y[k][:, 0:W]).then_inc(picked, 1)
                    dve.wait_ge(picked, 1)
                    v.match_replace(y[0][:, 0:W], eight[:, 0, :], y[0][:, 0:W], GONE).then_inc(picked, 1)
                    if not first:
                        dve.wait_ge(noted, NOTES)
                        dve.sem_clear(noted)
                    dve.wait_ge(picked, 2)
                    v.scalar_tensor_tensor(out=hit8[:, :, :], in0=dist[:, :, :], scalar=0.0,
                                           in1=eight[:, :, :], op0=ALU.is_equal, op1=ALU.mult).then_inc(noted, 1)
                    v.match_replace(y[1][:, 0:W], eight[:, 1, :], y[1][:, 0:W], GONE).then_inc(picked, 1)
                    dve.wait_ge(noted, 1)
                    v.tensor_tensor(found[:, :, :], found[:, :, :], hit8[:, :, :], ALU.add).then_inc(noted, 1)
                    v.tensor_scalar(dist[:, :, :], dist[:, :, :], 8.0, None, ALU.add).then_inc(noted, 1)
                    dve.wait_ge(picked, 4)
                    dve.sem_clear(picked)

                def rounds():
                    after(at[0])
                    with dve.If(n["furthest"] > 0):
                        for k in range(2):
                            dve.wait_ge(sided_ready, val(2 * s + k + 1))
                            v.tensor_scalar(mark[k][:, 0:W], sided[(2 * p + k) % 4][:, 0:W], 0.0, -BIG, ALU.is_ge, ALU.mult
                                            ).then_inc(picked, 1)
                        wait(dve, keep_ready, 2 * (s - 1))
                        for k in range(2):
                            dve.wait_ge(picked, k + 1)
                            v.scalar_tensor_tensor(out=y[k][:, 0:W], in0=S[(2 * p + k) % 8][:, 0:W],
                                                   scalar=turn_to[:, r, k:k + 1], in1=mark[k][:, 0:W],
                                                   op0=ALU.mult, op1=ALU.add).then_inc(picked, 1)
                        dve.wait_ge(picked, 4)
                        dve.sem_clear(picked)
                        one_round(first=True)
                        with dve.Fori(8, n["furthest"], 8):
                            one_round(first=False)
                        dve.wait_ge(noted, NOTES)
                        dve.sem_clear(noted)
                    dve.end_ifs()
                    n["thresh"] = then(v.tensor_reduce(thresh[:, r, :], found[:, :, :], X, ALU.add))

                def turned_back():
                    after(n["thresh"])
                    last_step = v.tensor_tensor(thresh[:, r, :], thresh[:, r, :], turn_to[:, r, :], ALU.mult)
                    if qt == 0:
                        after(then(last_step))
                        last_step = v.tensor_scalar(thresh[:, r, :], thresh[:, r, :], drop[:, 0:1], None, ALU.add)
                    last_step.then_inc(thresh_ready, 1)

                return [(0, load), (4.8, rounds), (5.15, turned_back)]

            def norm_1(c, signal, y, ready, x_in_, sum_, j, extra=None):
                chain = link(dve, signal, LN * c)
                dve.wait_ge(ready[0], val(ready[1]))
                if extra:
                    dve.wait_ge(extra[0], val(extra[1]))
                chain(nc.vector.tensor_tensor(sum_[:, :], y, x_in_, ALU.add))
                chain.caught_up()
                chain(nc.vector.bn_stats(stats[j][:, :], sum_[:, :]))
                chain.caught_up()
                settle()
                chain(nc.vector.bn_aggr(mv[j][:, :], stats[j][:, :]))

            def norm_2(c, signal, rs, sum_, j, out):
                dve.wait_ge(rs, val(2 * c + 2))
                nc.vector.tensor_scalar(out, sum_[:, :], mv[j][:, 0:1], rstd[j][:, 0:1], ALU.subtract, ALU.mult
                                        ).then_inc(signal, 1)

            def normed_heads(c, signal, ready, ps):
                dve.wait_ge(ready[0], val(ready[1]))
                nc.vector.reciprocal(den[:, :], ps[:, :, HD]).then_inc(signal, 1)
                dve.wait_ge(signal, val(2 * c + 1))
                nc.vector.tensor_tensor(heads_o[:, :].rearrange("p (h j) -> p h j", j=HD), ps[:, :, 0:HD],
                                        den[:, :].unsqueeze(2).to_broadcast([P, NH, HD]), ALU.mult
                                        ).then_inc(signal, 1)

            def route_1(c):
                chain = link(dve, g5_dve, ROUTE * c)
                v = nc.vector
                dve.wait_ge(g5_l, val(c + 1))
                chain(v.tensor_tensor(logit[:, :], y_ps[:, 0:NE], b_r[:, :], ALU.add))
                chain.caught_up()
                chain(v.tensor_reduce(l_max[:, :], logit[:, :], X, ALU.max))
                chain.caught_up()
                chain(v.tensor_scalar(logit[:, :], logit[:, :], l_max[:, 0:1], None, ALU.subtract))

            def route_2(c, gt):
                chain = link(dve, g5_dve, ROUTE * c + 3)
                v = nc.vector
                dve.wait_ge(g5_exp, val(c + 1))
                e_j = l_exp[:, :].unsqueeze(1).to_broadcast([P, NE, NE])
                e_i = l_exp[:, :].unsqueeze(2).to_broadcast([P, NE, NE])
                chain(v.tensor_tensor(above[:, :, :], e_j, e_i, ALU.is_gt))
                chain(v.tensor_tensor(tied[:, :, :], e_j, e_i, ALU.is_equal))
                chain.caught_up()
                chain(v.tensor_tensor(tied[:, :, :], tied[:, :, :], earlier[:, :, :], ALU.mult))
                chain.caught_up()
                chain(v.tensor_tensor(above[:, :, :], above[:, :, :], tied[:, :, :], ALU.add))
                chain.caught_up()
                chain(v.tensor_reduce(rank[:, :], above[:, :, :], X, ALU.add))
                chain.caught_up()
                for k in range(2):
                    chain(v.scalar_tensor_tensor(out=chosen[:, k, :], in0=rank[:, :], scalar=float(k), in1=l_exp[:, :],
                                                op0=ALU.is_equal, op1=ALU.mult))
                chain.caught_up()
                chain(v.tensor_tensor(both[:, :], chosen[:, 0, :], chosen[:, 1, :], ALU.add))
                chain.caught_up()
                chain(v.tensor_reduce(l_sum[:, :], both[:, :], X, ALU.add))
                chain.caught_up()
                chain(v.reciprocal(l_rec[:, :], l_sum[:, :]))
                chain.caught_up()
                v.tensor_scalar(gates[:, ds(c, 1), :].rearrange("p t e -> p (t e)"),
                                chosen[:, :, :].rearrange("p k e -> p (k e)"), l_rec[:, 0:1], None, ALU.mult)
                chain(v.tensor_scalar(gt[:, :], both[:, :], l_rec[:, 0:1], CAPACITY, ALU.mult, ALU.min))
                assert chain.n[0] + 3 == ROUTE

            def softmax2(c):
                v = nc.vector
                ps = psC[:, :].rearrange("p (h n) -> p h n", n=CTX)
                dve.wait_ge(g2_s, val(c + 1))
                v.tensor_reduce(m2[:, :], ps, X, ALU.max).then_inc(g2_dve, 1)
                dve.wait_ge(g2_dve, val(2 * c + 1))
                v.tensor_tensor(p2[:, :].rearrange("p (h n) -> p h n", n=CTX), ps,
                                m2[:, :].unsqueeze(2).to_broadcast([P, NH, CTX]), ALU.subtract
                                ).then_inc(g2_dve, 1)

            def by_heads(ps):
                return ps[:, 0:NH * VW].rearrange("p (h j) -> p h j", j=VW)

            def stored(f):
                if not isinstance(f, int) or f > 0:
                    dve.wait_ge(out_done, val(16 * f))

            def attention(kind, b, qt, p):
                work = {"classify": classify, "select": select, "keep": keep_first}
                return work[kind](b, qt, p) if kind in work else []

            def segment(i, c, b, qt):
                f = c
                zero = isinstance(c, int) and c == 0
                k = qt % 2
                x2_c = x2_0 if zero else x2
                return {
                    1: [(2.9, lambda: normed_heads(c, g0, (pv_done, NH * (c + 1)), by_heads(psO)))],
                    2: [(2.05, lambda: norm_1(c, g1_ln, y_ps, (g1_y, c + 1), x_rows[k][:, :], res, 0,
                                              (ld_xr[k], 16 * (QT // 2 * b + qt // 2 + 1)))),
                        (2.95, lambda: norm_2(c, g1_ln, rs1, res, 0, x1[:, :]))],
                    3: [(2.9, lambda: softmax2(c))],
                    4: [(2.9, lambda: normed_heads(c, g3_dve, (g3_o, c + 1), by_heads(psC)))],
                    5: [(2.05, lambda: norm_1(c, g4_ln, y_ps, (g4_y, c + 1), x1b[:, :], res, 0, (x1b_ready, c + 1))),
                        (2.95, lambda: norm_2(c, g4_ln, rs4, res, 0, x2_c[:, :]))],
                    6: [(2.04, lambda: route_1(c)), (2.98, lambda: route_2(c, gate_0 if zero else gate))],
                    12: [(2.05, lambda: stored(f)),
                         (2.06, lambda: norm_1(f, f_ln, psF, (f_y, NE * (f + 1)), x2_c[:, :], fin, 1)),
                         (2.95, lambda: norm_2(f, f_ln, rs7, fin, 1, fin[:, :]))],
                }.get(i, [])

            def last():
                v = nc.vector
                dve.wait_ge(g5_dve, val(ROUTE * TILES))
                v.tensor_reduce(gates_sum[:, :, :].rearrange("p k e -> p (k e)"),
                                gates[:, :, :].rearrange("p t e -> p e t"), X, ALU.add).then_inc(z_sum, 1)
                dve.wait_ge(z_ps, 1)
                v.tensor_tensor(gate_0[0:NE, 0:2], gate_0[0:NE, 0:2], sum_z, ALU.add).then_inc(z_gate, 1)
                dve.wait_ge(z_gate, 1)
                v.tensor_scalar(gate_0[:, :], gate_0[:, :], CAPACITY, None, ALU.min).then_inc(z_gate, 1)

            dve.wait_ge(ld_rest, val(16 * N_REST))
            def x_in_first():
                dve.wait_ge(z_bc, 1)
                nc.vector.tensor_tensor(x_in_z[:, :, :, :], x2_t0[:, :, 0:FIRST].unsqueeze(1).to_broadcast([P, TWICE, NC, FIRST]),
                                        gate_bz[:, :, :].unsqueeze(2).to_broadcast([P, TWICE, NC, FIRST]), ALU.mult
                                        ).then_inc(z_xin, 1)

            def hidden_first():
                dve.wait_ge(z_h, 1)
                nc.vector.tensor_tensor(hid_z[:, :, :, :], up_z,
                                        b_1[:, 0:TWICE, :].unsqueeze(3).to_broadcast([P, TWICE, NC, FIRST]), ALU.add).then_inc(z_hb, 1)

            def gated_first():
                dve.wait_ge(z_gelu, 1)
                nc.vector.tensor_tensor(hid_gz[:, 0:TWICE, :, :], hid_z[:, :, :, :],
                                        gate_bz[:, :, :].unsqueeze(2).to_broadcast([P, TWICE, NC, FIRST]), ALU.mult
                                        ).then_inc(z_hg, 1)

            def norm_first():
                chain = link(dve, z_ln, 0)
                dve.wait_ge(z_y, 1)
                chain(nc.vector.tensor_tensor(fin_z[:, :], psO[0:FIRST, 0:D], x2_0[0:FIRST, :], ALU.add))
                chain.caught_up()
                chain(nc.vector.bn_stats(stats_z[:, :], fin_z[:, :]))
                chain.caught_up()
                chain(nc.vector.bn_aggr(mv_z[:, :], stats_z[:, :]))
                dve.wait_ge(z_root, 2)
                chain(nc.vector.tensor_scalar(fin_z[:, :], fin_z[:, :], mv_z[:, 0:1], rstd_z[:, 0:1], ALU.subtract, ALU.mult))

            def again(i):
                return {9: [(30, x_in_first)], 10: [(30, hidden_first), (31, gated_first)], 12: [(30, norm_first)]}.get(i, [])

            timeline(dve, attention, segment, last, again, lambda p: [(-1, fresh)])


def host_constants():
    bf = mybir.dt.np(BF16)
    i = np.arange(P)
    c = {}
    c["ident"] = np.eye(P, dtype=np.float32)
    c["ident_h"] = np.eye(P, dtype=np.float32).astype(bf)
    c["causal_h"] = np.where(i[None, :] > i[:, None], NEG, 0.0).astype(np.float32).astype(bf)
    c["head_rows"] = np.repeat((i[:, None] // HD == np.arange(8)[None, :]).astype(np.float32)[:, :, None], P, axis=2)
    c["same_head"] = np.repeat((np.arange(3 * D) % HD != 0).astype(np.float32)[None, :], P, axis=0).astype(bf)
    e = np.arange(NE)
    c["earlier"] = np.repeat((e[None, None, :] < e[None, :, None]).astype(np.float32), P, axis=0)
    c["pick_row"] = np.repeat((e[:, None] == e[None, :]).astype(np.float32)[:, :, None], P, axis=2)
    c["ones"] = np.ones((P, 1), np.float32)
    c["eps"] = np.full((P, 1), EPS, np.float32)
    c["late"] = (i[:, None] >= KEEP).astype(np.float32)
    c["drop"] = np.where(i[:, None] < KEEP, BELOW, 0.0).astype(np.float32)
    c["iota8"] = np.repeat(np.arange(1, 9, dtype=np.float32)[None, :], P, axis=0)
    c["half"] = np.full((P, 1), -0.5, np.float32)
    return c


def kernel(**inputs):
    import concourse.bacc as bacc
    from concourse.bass_utils import run_bass_kernel_spmd

    i = {k: np.asarray(v) for k, v in inputs.items()}
    arrays = host_constants()
    x = i["x"].reshape(B * T, D)
    arrays["x"] = x
    arrays["x_t"] = x.T
    arrays["w_qkv"] = np.concatenate([i["L0_attn_wq"].T, i["L0_attn_wk"].T, i["L0_attn_wv"].T], axis=1)
    arrays["w_o"] = i["L0_attn_wo"].T
    for n in "qkvo":
        arrays[f"w_{n}2"] = i[f"L0_xattn_w{n}"].T
    arrays["b_q"] = i["L0_xattn_bq"].reshape(NC, P).T
    arrays["b_k"] = i["L0_xattn_bk"].reshape(NC, P).T
    arrays["b_v"] = i["L0_xattn_bv"].reshape(1, D)
    arrays["b_o"] = i["L0_xattn_bo"]
    c = i["ctx_1024"].reshape(B, CTX, D)
    arrays["ctx_t"] = c.reshape(B * CTX, D).T
    arrays["ctx_t2"] = np.concatenate([c, c], axis=1).reshape(B * 2 * CTX, D).T
    arrays["w_r"] = i["L0_ffn_router_w"]
    arrays["b_r"] = i["L0_ffn_router_b"]
    arrays["w_1"] = i["L0_ffn_w1"]
    arrays["b_1"] = i["L0_ffn_b1"].reshape(NE, NC, P).transpose(2, 0, 1)
    arrays["w_2"] = i["L0_ffn_w2"]
    arrays["b_2"] = i["L0_ffn_b2"]
    arrays = {k: np.ascontiguousarray(v) for k, v in arrays.items()}

    nc = bacc.Bacc("TRN2", target_bir_lowering=False, num_devices=1)
    aps = {k: nc.dram_tensor(f"in_{k}", v.shape, mybir.dt.from_np(v.dtype), kind="ExternalInput").ap()
           for k, v in arrays.items()}
    aps["out"] = nc.dram_tensor("out_0", (B * T, D), F32, kind="ExternalOutput").ap()
    build(nc, aps)
    r = run_bass_kernel_spmd(nc, [{f"in_{k}": v for k, v in arrays.items()}], core_ids=[0])
    return r.results[0]["out_0"].reshape(B, T, D)
```
